# Optimizing a Trainium2 kernel written in Bass

```python
import numpy as np
import jax
import jax.numpy as jnp

def _softmax(x, axis=-1):
    return jax.nn.softmax(x, axis=axis)

def _gelu(x):
    return jax.nn.gelu(x, approximate=True)

def _silu(x):
    return jax.nn.silu(x)

def _sigmoid(x):
    return jax.nn.sigmoid(x)

def _layernorm(x, axis=-1, eps=1e-05):
    m = jnp.mean(x, axis=axis, keepdims=True)
    v = jnp.var(x, axis=axis, keepdims=True)
    return (x - m) / jnp.sqrt(v + eps)

def _scatter_add(tgt, idx, src, axis=0):
    return tgt.at[idx].add(src)

def _segment_sum(src, seg, n):
    return jax.ops.segment_sum(src, seg, n)
kernel_name = 'mk_xattn_seq_d4_seqx_r4_80d237'

def setup_inputs(seed: int=0):
    np.random.seed(seed)
    _w = jnp.asarray

    def _rec_inputs():
        import jax
        import jax.numpy as jnp
        _rk = jax.random.key(seed)
        x = 7.22e-05 + 1 * jax.random.normal(jax.random.fold_in(_rk, 1), (4, 512, 512), jnp.float32)
        _lenS = 512 - jax.random.randint(jax.random.fold_in(_rk, 7), (4,), 0, max(1, 512 // 4) + 1, jnp.int32)
        _lenS2 = 512 - jax.random.randint(jax.random.fold_in(_rk, 8), (4,), 0, max(1, 512 // 4) + 1, jnp.int32)
        _ctx_2048P = jax.random.normal(jax.random.fold_in(_rk, 11), (4, 16, 512), jnp.float32)
        _ctx_2048c = jax.random.dirichlet(jax.random.fold_in(_rk, 511), 0.3 * jnp.ones((16,), jnp.float32), (4, 512))
        _ctx_2048t = jnp.einsum('bsk,bkd->bsd', _ctx_2048c, _ctx_2048P)
        _ctx_2048t = _ctx_2048t * jax.lax.rsqrt(jnp.mean(jnp.square(_ctx_2048t)) + 1e-12) * 0.953939
        ctx_2048 = 4.13588e-05 + 0.999923 * (_ctx_2048t + 0.3 * jax.random.normal(jax.random.fold_in(_rk, 611), (4, 512, 512), jnp.float32))
        _validS = jnp.arange(512)[None, :] < _lenS[:, None]
        _validS2 = jnp.arange(512)[None, :] < _lenS2[:, None]
        _causal = jnp.tril(jnp.ones((512, 512), dtype=bool))
        mask_Bx1xSxS2_ff0 = jnp.where(jnp.ones((4, 1, 512, 512), dtype=bool), 0.0, -1000000000.0).astype(jnp.float32)
        mask_1x1xSxS2_fc1 = jnp.where(jnp.broadcast_to(_validS2[0:1, None, None, :], (1, 1, 512, 512)), 1.0, 0.0).astype(jnp.float32)
        mask_Bx1xSxS2_ff1 = jnp.where(jnp.ones((4, 1, 512, 512), dtype=bool), 1.0, 0.0).astype(jnp.float32)
        return (x, ctx_2048, mask_Bx1xSxS2_ff0, mask_1x1xSxS2_fc1, mask_Bx1xSxS2_ff1)
    x, ctx_2048, mask_Bx1xSxS2_ff0, mask_1x1xSxS2_fc1, mask_Bx1xSxS2_ff1 = _rec_inputs()

    def _L0_xattn_setup():
        import jax, jax.numpy as jnp
        import numpy as np
        H = 512
        NH = 32
        KVH = 8
        HD = H // NH
        GROUPS = NH // KVH
        EPS = 1e-06
        B, L, S = (4, 256, 256)

        def _gqa_forward(hidden_state, encoder_hidden_state, encoder_attention_mask, Wq, bq, Wk, bk, Wv, bv, Wo, bo, gamma, beta):
            b, l, _ = hidden_state.shape
            s = encoder_hidden_state.shape[1]
            q = hidden_state @ Wq + bq
            k = encoder_hidden_state @ Wk + bk
            v = encoder_hidden_state @ Wv + bv
            q = q.reshape(b, l, KVH, GROUPS, HD).transpose(0, 2, 3, 1, 4)
            k = k.reshape(b, s, KVH, HD).transpose(0, 2, 1, 3)
            v = v.reshape(b, s, KVH, HD).transpose(0, 2, 1, 3)
            scale = 1.0 / jnp.sqrt(jnp.asarray(HD, q.dtype))
            scores = jnp.einsum('bkgld,bksd->bkgls', q, k) * scale
            scores = scores + encoder_attention_mask[:, :, None, :, :]
            attn = jax.nn.softmax(scores, axis=-1)
            out = jnp.einsum('bkgls,bksd->bkgld', attn, v)
            out = out.transpose(0, 3, 1, 2, 4).reshape(b, l, H)
            out = out @ Wo + bo
            x = out + hidden_state
            mu = jnp.mean(x, axis=-1, keepdims=True)
            var = jnp.var(x, axis=-1, keepdims=True)
            return (x - mu) * jax.lax.rsqrt(var + EPS) * gamma + beta
        key = jax.random.key(seed)
        ks = jax.random.split(key, 12)
        sd = 0.02
        return {'hidden_state': jax.random.normal(ks[0], (B, L, H), jnp.float32), 'encoder_hidden_state': jax.random.normal(ks[1], (B, S, H), jnp.float32), 'encoder_attention_mask': jnp.zeros((B, 1, L, S), jnp.float32), 'Wq': jax.random.normal(ks[2], (H, H), jnp.float32) * sd, 'bq': jnp.zeros((H,), jnp.float32), 'Wk': jax.random.normal(ks[3], (H, KVH * HD), jnp.float32) * sd, 'bk': jnp.zeros((KVH * HD,), jnp.float32), 'Wv': jax.random.normal(ks[4], (H, KVH * HD), jnp.float32) * sd, 'bv': jnp.zeros((KVH * HD,), jnp.float32), 'Wo': jax.random.normal(ks[5], (H, H), jnp.float32) * sd, 'bo': jnp.zeros((H,), jnp.float32), 'gamma': jnp.ones((H,), jnp.float32), 'beta': jnp.zeros((H,), jnp.float32)}
    _L0_xattn_all = _L0_xattn_setup()
    _L0_xattn_in = {k: v for k, v in _L0_xattn_all.items() if k in ('Wq', 'bq', 'Wk', 'bk', 'Wv', 'bv', 'Wo', 'bo', 'gamma', 'beta')}
    del _L0_xattn_all

    def _L1_xattn_setup():
        import jax, jax.numpy as jnp
        import numpy as np
        H = 512
        NH = 16
        HD = H // NH
        EPS = 1e-05

        def gelu(x):
            return 0.5 * x * (1.0 + jnp.tanh(0.7978845608028654 * x * (1.0 + 0.044715 * x * x)))

        def layernorm(x, scale, bias):
            m = jnp.mean(x, axis=-1, keepdims=True)
            v = jnp.mean(jnp.square(x - m), axis=-1, keepdims=True)
            return (x - m) * jax.lax.rsqrt(v + EPS) * scale + bias

        def split_heads(x):
            b, s, _ = x.shape
            return x.reshape(b, s, NH, HD).transpose(0, 2, 1, 3)

        def merge_heads(x):
            b, nh, s, hd = x.shape
            return x.transpose(0, 2, 1, 3).reshape(b, s, nh * hd)

        def attention(q, k, v, mask):
            scores = jnp.einsum('bhqd,bhkd->bhqk', q, k) / jnp.sqrt(jnp.float32(HD))
            scores = scores * mask - 10000.0 * (1.0 - mask)
            probs = jax.nn.softmax(scores, axis=-1)
            return jnp.einsum('bhqk,bhkd->bhqd', probs, v)
        key = jax.random.key(seed)
        ks = jax.random.split(key, 16)
        b, s, t = (2, 256, 256)
        w = lambda k, i, o: jax.random.normal(k, (i, o), jnp.float32) * 0.02
        inp = {'hidden_states': jax.random.normal(ks[0], (b, s, H), jnp.float32), 'encoder_states': jax.random.normal(ks[1], (b, t, H), jnp.float32), 'ltor_mask': jnp.tril(jnp.ones((1, 1, s, s), jnp.float32)), 'cross_mask': jnp.ones((b, 1, s, t), jnp.float32), 'ln1_s': jnp.ones((H,), jnp.float32), 'ln1_b': jnp.zeros((H,), jnp.float32), 'w_qkv': w(ks[2], H, 3 * H), 'b_qkv': jnp.zeros((3 * H,), jnp.float32), 'w_ao': w(ks[3], H, H), 'b_ao': jnp.zeros((H,), jnp.float32), 'ln2_s': jnp.ones((H,), jnp.float32), 'ln2_b': jnp.zeros((H,), jnp.float32), 'w_q': w(ks[4], H, H), 'b_q': jnp.zeros((H,), jnp.float32), 'w_kv': w(ks[5], H, 2 * H), 'b_kv': jnp.zeros((2 * H,), jnp.float32), 'w_co': w(ks[6], H, H), 'b_co': jnp.zeros((H,), jnp.float32), 'ln3_s': jnp.ones((H,), jnp.float32), 'ln3_b': jnp.zeros((H,), jnp.float32), 'w1': w(ks[7], H, 4 * H), 'b1': jnp.zeros((4 * H,), jnp.float32), 'w2': w(ks[8], 4 * H, H), 'b2': jnp.zeros((H,), jnp.float32)}
        return inp
    _L1_xattn_all = _L1_xattn_setup()
    _L1_xattn_in = {k: v for k, v in _L1_xattn_all.items() if k in ('ln1_s', 'ln1_b', 'w_qkv', 'b_qkv', 'w_ao', 'b_ao', 'ln2_s', 'ln2_b', 'w_q', 'b_q', 'w_kv', 'b_kv', 'w_co', 'b_co', 'ln3_s', 'ln3_b', 'w1', 'b1', 'w2', 'b2')}
    del _L1_xattn_all

    def _L2_xattn_setup():
        import jax, jax.numpy as jnp
        import numpy as np
        E, H, L, B = (512, 32, 256, 4)
        S = E // H
        DM, DD = (32, 64)

        def _ln(x, w, b, eps=1e-05):
            m = x.mean(-1, keepdims=True)
            v = ((x - m) ** 2).mean(-1, keepdims=True)
            return (x - m) / jnp.sqrt(v + eps) * w + b

        def _block(x, state, ln1_w, ln1_b, ln2_w, ln2_b, maa_x, maa_w1, maa_w2, maa_stack, time_decay, td_w1, td_w2, u, Wr, Wk, Wv, Wg, Wo, gn_w, gn_b, ffn_maa_k, ffn_maa_r, Wfk, Wfr, Wfv):
            b, l, e = x.shape
            h = u.shape[0]
            s_ = e // h
            xa = _ln(x, ln1_w, ln1_b)
            sx = jnp.concatenate([state[:, 1:2] - xa[:, :1], xa[:, :-1] - xa[:, 1:]], axis=1)
            xxx = jnp.tanh((xa + sx * maa_x) @ maa_w1).reshape(b, l, 5, DM)
            xxx = jnp.einsum('blfd,fde->blfe', xxx, maa_w2)
            xm = xa[:, :, None] + sx[:, :, None] * (maa_stack + xxx)
            xk, xw, xv, xr, xg = (xm[:, :, j] for j in range(5))
            w = jnp.exp(-jnp.exp(time_decay + jnp.tanh(xw @ td_w1) @ td_w2)).reshape(b, l, h, s_)
            r = (xr @ Wr.T).reshape(b, l, h, s_)
            k = (xk @ Wk.T).reshape(b, l, h, s_)
            v = (xv @ Wv.T).reshape(b, l, h, s_)
            g = jax.nn.silu(xg @ Wg.T)
            s0 = state[:, 2:2 + s_].reshape(b, h, s_, s_)

            def step(s, rkvw):
                r_t, k_t, v_t, w_t = rkvw
                a = k_t[..., :, None] * v_t[..., None, :]
                out = jnp.einsum('bhi,bhij->bhj', r_t, u * a + s)
                s = a + w_t[..., :, None] * s
                return (s, out)
            rkvw = tuple((jnp.moveaxis(t, 1, 0) for t in (r, k, v, w)))
            _, out = jax.lax.scan(step, s0, rkvw)
            out = jnp.moveaxis(out, 0, 1).reshape(b, l, e)
            og = out.reshape(b, l, h, s_)
            m = og.mean(-1, keepdims=True)
            va = ((og - m) ** 2).mean(-1, keepdims=True)
            og = ((og - m) / jnp.sqrt(va + 1e-05)).reshape(b, l, e) * gn_w + gn_b
            x1 = x + og * g @ Wo.T
            xc = _ln(x1, ln2_w, ln2_b)
            sx2 = jnp.concatenate([state[:, 0:1] - xc[:, :1], xc[:, :-1] - xc[:, 1:]], axis=1)
            xk2 = xc + sx2 * ffn_maa_k
            xr2 = xc + sx2 * ffn_maa_r
            rr = jax.nn.sigmoid(xr2 @ Wfr.T)
            kk = jnp.square(jax.nn.relu(xk2 @ Wfk.T))
            return x1 + rr * (kk @ Wfv.T)
        key = jax.random.key(seed)
        ks = jax.random.split(key, 24)
        sc = 0.02
        d = {'x': jax.random.normal(ks[0], (B, L, E), jnp.float32), 'state': jax.random.normal(ks[1], (B, 2 + S, E), jnp.float32) * 0.1, 'ln1_w': jnp.ones((E,), jnp.float32), 'ln1_b': jnp.zeros((E,), jnp.float32), 'ln2_w': jnp.ones((E,), jnp.float32), 'ln2_b': jnp.zeros((E,), jnp.float32), 'maa_x': jax.random.normal(ks[2], (E,), jnp.float32) * 0.1, 'maa_w1': jax.random.normal(ks[3], (E, 5 * DM), jnp.float32) * sc, 'maa_w2': jax.random.normal(ks[4], (5, DM, E), jnp.float32) * sc, 'maa_stack': jax.random.normal(ks[5], (1, 5, E), jnp.float32) * 0.1, 'time_decay': jax.random.normal(ks[6], (E,), jnp.float32) * 0.5, 'td_w1': jax.random.normal(ks[7], (E, DD), jnp.float32) * sc, 'td_w2': jax.random.normal(ks[8], (DD, E), jnp.float32) * sc, 'u': jax.random.normal(ks[9], (H, S, 1), jnp.float32) * 0.1, 'Wr': jax.random.normal(ks[10], (E, E), jnp.float32) * sc, 'Wk': jax.random.normal(ks[11], (E, E), jnp.float32) * sc, 'Wv': jax.random.normal(ks[12], (E, E), jnp.float32) * sc, 'Wg': jax.random.normal(ks[13], (E, E), jnp.float32) * sc, 'Wo': jax.random.normal(ks[14], (E, E), jnp.float32) * sc, 'gn_w': jnp.ones((E,), jnp.float32), 'gn_b': jnp.zeros((E,), jnp.float32), 'ffn_maa_k': jax.random.normal(ks[15], (E,), jnp.float32) * 0.1, 'ffn_maa_r': jax.random.normal(ks[16], (E,), jnp.float32) * 0.1, 'Wfk': jax.random.normal(ks[17], (E, E), jnp.float32) * sc, 'Wfr': jax.random.normal(ks[18], (E, E), jnp.float32) * sc, 'Wfv': jax.random.normal(ks[19], (E, E), jnp.float32) * sc}
        return d
    _L2_xattn_all = _L2_xattn_setup()
    _L2_xattn_in = {k: v for k, v in _L2_xattn_all.items() if k in ('ln1_w', 'ln1_b', 'ln2_w', 'ln2_b', 'maa_x', 'maa_w1', 'maa_w2', 'maa_stack', 'time_decay', 'td_w1', 'td_w2', 'u', 'Wr', 'Wk', 'Wv', 'Wg', 'Wo', 'gn_w', 'gn_b', 'ffn_maa_k', 'ffn_maa_r', 'Wfk', 'Wfr', 'Wfv')}
    del _L2_xattn_all

    def _L3_xattn_setup():
        import jax, jax.numpy as jnp
        import numpy as np
        B, L, E, H = (4, 128, 512, 32)
        S = E // H
        EXTRA_MAA, EXTRA_DECAY = (32, 64)
        EPS = 1e-05

        def _ln(x, w, b):
            m = jnp.mean(x, axis=-1, keepdims=True)
            v = jnp.mean((x - m) ** 2, axis=-1, keepdims=True)
            return (x - m) * jax.lax.rsqrt(v + EPS) * w + b

        def _token_shift(xn, prev_row):
            first = (prev_row - xn[:, 0])[:, None]
            rest = xn[:, :-1] - xn[:, 1:]
            return jnp.concatenate([first, rest], axis=1)
        key = jax.random.key(seed)
        ks = jax.random.split(key, 24)
        rn = lambda k, shp, s=1.0: jax.random.normal(k, shp, dtype=jnp.float32) * s
        return dict(x=rn(ks[0], (B, L, E)), state=rn(ks[1], (B, 2 + S, E), 0.1), ln1_w=jnp.ones((E,), jnp.float32), ln1_b=jnp.zeros((E,), jnp.float32), ln2_w=jnp.ones((E,), jnp.float32), ln2_b=jnp.zeros((E,), jnp.float32), maa_x=rn(ks[2], (E,), 0.02), maa_w1=rn(ks[3], (E, 5 * EXTRA_MAA), 0.02), maa_w2=rn(ks[4], (5, EXTRA_MAA, E), 0.02), maa_stack=rn(ks[5], (5, E), 0.02), time_decay=rn(ks[6], (E,), 0.5), decay_w1=rn(ks[7], (E, EXTRA_DECAY), 0.02), decay_w2=rn(ks[8], (EXTRA_DECAY, E), 0.02), faaaa=rn(ks[9], (H, S), 0.1), Wr=rn(ks[10], (E, E), 0.02), Wk=rn(ks[11], (E, E), 0.02), Wv=rn(ks[12], (E, E), 0.02), Wg=rn(ks[13], (E, E), 0.02), Wo=rn(ks[14], (E, E), 0.02), gn_w=jnp.ones((E,), jnp.float32), gn_b=jnp.zeros((E,), jnp.float32), ffn_maa_k=rn(ks[15], (E,), 0.02), ffn_maa_r=rn(ks[16], (E,), 0.02), ffn_Wk=rn(ks[17], (E, E), 0.02), ffn_Wr=rn(ks[18], (E, E), 0.02), ffn_Wv=rn(ks[19], (E, E), 0.02), i=0)
    _L3_xattn_all = _L3_xattn_setup()
    _L3_xattn_in = {k: v for k, v in _L3_xattn_all.items() if k in ('ln1_w', 'ln1_b', 'ln2_w', 'ln2_b', 'maa_x', 'maa_w1', 'maa_w2', 'maa_stack', 'time_decay', 'decay_w1', 'decay_w2', 'faaaa', 'Wr', 'Wk', 'Wv', 'Wg', 'Wo', 'gn_w', 'gn_b', 'ffn_maa_k', 'ffn_maa_r', 'ffn_Wk', 'ffn_Wr', 'ffn_Wv')}
    del _L3_xattn_all
    return {'x': x, 'ctx_2048': ctx_2048, 'mask_Bx1xSxS2_ff0': mask_Bx1xSxS2_ff0, 'mask_1x1xSxS2_fc1': mask_1x1xSxS2_fc1, 'mask_Bx1xSxS2_ff1': mask_Bx1xSxS2_ff1, 'L0_xattn_Wq': _L0_xattn_in['Wq'], 'L0_xattn_bq': _L0_xattn_in['bq'], 'L0_xattn_Wk': _L0_xattn_in['Wk'], 'L0_xattn_bk': _L0_xattn_in['bk'], 'L0_xattn_Wv': _L0_xattn_in['Wv'], 'L0_xattn_bv': _L0_xattn_in['bv'], 'L0_xattn_Wo': _L0_xattn_in['Wo'], 'L0_xattn_bo': _L0_xattn_in['bo'], 'L0_xattn_gamma': _L0_xattn_in['gamma'], 'L0_xattn_beta': _L0_xattn_in['beta'], 'L1_xattn_ln1_s': _L1_xattn_in['ln1_s'], 'L1_xattn_ln1_b': _L1_xattn_in['ln1_b'], 'L1_xattn_w_qkv': _L1_xattn_in['w_qkv'], 'L1_xattn_b_qkv': _L1_xattn_in['b_qkv'], 'L1_xattn_w_ao': _L1_xattn_in['w_ao'], 'L1_xattn_b_ao': _L1_xattn_in['b_ao'], 'L1_xattn_ln2_s': _L1_xattn_in['ln2_s'], 'L1_xattn_ln2_b': _L1_xattn_in['ln2_b'], 'L1_xattn_w_q': _L1_xattn_in['w_q'], 'L1_xattn_b_q': _L1_xattn_in['b_q'], 'L1_xattn_w_kv': _L1_xattn_in['w_kv'], 'L1_xattn_b_kv': _L1_xattn_in['b_kv'], 'L1_xattn_w_co': _L1_xattn_in['w_co'], 'L1_xattn_b_co': _L1_xattn_in['b_co'], 'L1_xattn_ln3_s': _L1_xattn_in['ln3_s'], 'L1_xattn_ln3_b': _L1_xattn_in['ln3_b'], 'L1_xattn_w1': _L1_xattn_in['w1'], 'L1_xattn_b1': _L1_xattn_in['b1'], 'L1_xattn_w2': _L1_xattn_in['w2'], 'L1_xattn_b2': _L1_xattn_in['b2'], 'L2_xattn_ln1_w': _L2_xattn_in['ln1_w'], 'L2_xattn_ln1_b': _L2_xattn_in['ln1_b'], 'L2_xattn_ln2_w': _L2_xattn_in['ln2_w'], 'L2_xattn_ln2_b': _L2_xattn_in['ln2_b'], 'L2_xattn_maa_x': _L2_xattn_in['maa_x'], 'L2_xattn_maa_w1': _L2_xattn_in['maa_w1'], 'L2_xattn_maa_w2': _L2_xattn_in['maa_w2'], 'L2_xattn_maa_stack': _L2_xattn_in['maa_stack'], 'L2_xattn_time_decay': _L2_xattn_in['time_decay'], 'L2_xattn_td_w1': _L2_xattn_in['td_w1'], 'L2_xattn_td_w2': _L2_xattn_in['td_w2'], 'L2_xattn_u': _L2_xattn_in['u'], 'L2_xattn_Wr': _L2_xattn_in['Wr'], 'L2_xattn_Wk': _L2_xattn_in['Wk'], 'L2_xattn_Wv': _L2_xattn_in['Wv'], 'L2_xattn_Wg': _L2_xattn_in['Wg'], 'L2_xattn_Wo': _L2_xattn_in['Wo'], 'L2_xattn_gn_w': _L2_xattn_in['gn_w'], 'L2_xattn_gn_b': _L2_xattn_in['gn_b'], 'L2_xattn_ffn_maa_k': _L2_xattn_in['ffn_maa_k'], 'L2_xattn_ffn_maa_r': _L2_xattn_in['ffn_maa_r'], 'L2_xattn_Wfk': _L2_xattn_in['Wfk'], 'L2_xattn_Wfr': _L2_xattn_in['Wfr'], 'L2_xattn_Wfv': _L2_xattn_in['Wfv'], 'L3_xattn_ln1_w': _L3_xattn_in['ln1_w'], 'L3_xattn_ln1_b': _L3_xattn_in['ln1_b'], 'L3_xattn_ln2_w': _L3_xattn_in['ln2_w'], 'L3_xattn_ln2_b': _L3_xattn_in['ln2_b'], 'L3_xattn_maa_x': _L3_xattn_in['maa_x'], 'L3_xattn_maa_w1': _L3_xattn_in['maa_w1'], 'L3_xattn_maa_w2': _L3_xattn_in['maa_w2'], 'L3_xattn_maa_stack': _L3_xattn_in['maa_stack'], 'L3_xattn_time_decay': _L3_xattn_in['time_decay'], 'L3_xattn_decay_w1': _L3_xattn_in['decay_w1'], 'L3_xattn_decay_w2': _L3_xattn_in['decay_w2'], 'L3_xattn_faaaa': _L3_xattn_in['faaaa'], 'L3_xattn_Wr': _L3_xattn_in['Wr'], 'L3_xattn_Wk': _L3_xattn_in['Wk'], 'L3_xattn_Wv': _L3_xattn_in['Wv'], 'L3_xattn_Wg': _L3_xattn_in['Wg'], 'L3_xattn_Wo': _L3_xattn_in['Wo'], 'L3_xattn_gn_w': _L3_xattn_in['gn_w'], 'L3_xattn_gn_b': _L3_xattn_in['gn_b'], 'L3_xattn_ffn_maa_k': _L3_xattn_in['ffn_maa_k'], 'L3_xattn_ffn_maa_r': _L3_xattn_in['ffn_maa_r'], 'L3_xattn_ffn_Wk': _L3_xattn_in['ffn_Wk'], 'L3_xattn_ffn_Wr': _L3_xattn_in['ffn_Wr'], 'L3_xattn_ffn_Wv': _L3_xattn_in['ffn_Wv']}

def reference(x, ctx_2048, mask_Bx1xSxS2_ff0, mask_1x1xSxS2_fc1, mask_Bx1xSxS2_ff1, L0_xattn_Wq, L0_xattn_bq, L0_xattn_Wk, L0_xattn_bk, L0_xattn_Wv, L0_xattn_bv, L0_xattn_Wo, L0_xattn_bo, L0_xattn_gamma, L0_xattn_beta, L1_xattn_ln1_s, L1_xattn_ln1_b, L1_xattn_w_qkv, L1_xattn_b_qkv, L1_xattn_w_ao, L1_xattn_b_ao, L1_xattn_ln2_s, L1_xattn_ln2_b, L1_xattn_w_q, L1_xattn_b_q, L1_xattn_w_kv, L1_xattn_b_kv, L1_xattn_w_co, L1_xattn_b_co, L1_xattn_ln3_s, L1_xattn_ln3_b, L1_xattn_w1, L1_xattn_b1, L1_xattn_w2, L1_xattn_b2, L2_xattn_ln1_w, L2_xattn_ln1_b, L2_xattn_ln2_w, L2_xattn_ln2_b, L2_xattn_maa_x, L2_xattn_maa_w1, L2_xattn_maa_w2, L2_xattn_maa_stack, L2_xattn_time_decay, L2_xattn_td_w1, L2_xattn_td_w2, L2_xattn_u, L2_xattn_Wr, L2_xattn_Wk, L2_xattn_Wv, L2_xattn_Wg, L2_xattn_Wo, L2_xattn_gn_w, L2_xattn_gn_b, L2_xattn_ffn_maa_k, L2_xattn_ffn_maa_r, L2_xattn_Wfk, L2_xattn_Wfr, L2_xattn_Wfv, L3_xattn_ln1_w, L3_xattn_ln1_b, L3_xattn_ln2_w, L3_xattn_ln2_b, L3_xattn_maa_x, L3_xattn_maa_w1, L3_xattn_maa_w2, L3_xattn_maa_stack, L3_xattn_time_decay, L3_xattn_decay_w1, L3_xattn_decay_w2, L3_xattn_faaaa, L3_xattn_Wr, L3_xattn_Wk, L3_xattn_Wv, L3_xattn_Wg, L3_xattn_Wo, L3_xattn_gn_w, L3_xattn_gn_b, L3_xattn_ffn_maa_k, L3_xattn_ffn_maa_r, L3_xattn_ffn_Wk, L3_xattn_ffn_Wr, L3_xattn_ffn_Wv):
    import jax
    import jax.numpy as jnp

    def _L0_xattn_ref(hidden_state, encoder_hidden_state, encoder_attention_mask, Wq, bq, Wk, bk, Wv, bv, Wo, bo, gamma, beta):
        import jax, jax.numpy as jnp
        import numpy as np
        H = 512
        NH = 32
        KVH = 8
        HD = H // NH
        GROUPS = NH // KVH
        EPS = 1e-06
        B, L, S = (4, 256, 256)

        def _gqa_forward(hidden_state, encoder_hidden_state, encoder_attention_mask, Wq, bq, Wk, bk, Wv, bv, Wo, bo, gamma, beta):
            b, l, _ = hidden_state.shape
            s = encoder_hidden_state.shape[1]
            q = hidden_state @ Wq + bq
            k = encoder_hidden_state @ Wk + bk
            v = encoder_hidden_state @ Wv + bv
            q = q.reshape(b, l, KVH, GROUPS, HD).transpose(0, 2, 3, 1, 4)
            k = k.reshape(b, s, KVH, HD).transpose(0, 2, 1, 3)
            v = v.reshape(b, s, KVH, HD).transpose(0, 2, 1, 3)
            scale = 1.0 / jnp.sqrt(jnp.asarray(HD, q.dtype))
            scores = jnp.einsum('bkgld,bksd->bkgls', q, k) * scale
            scores = scores + encoder_attention_mask[:, :, None, :, :]
            attn = jax.nn.softmax(scores, axis=-1)
            out = jnp.einsum('bkgls,bksd->bkgld', attn, v)
            out = out.transpose(0, 3, 1, 2, 4).reshape(b, l, H)
            out = out @ Wo + bo
            x = out + hidden_state
            mu = jnp.mean(x, axis=-1, keepdims=True)
            var = jnp.var(x, axis=-1, keepdims=True)
            return (x - mu) * jax.lax.rsqrt(var + EPS) * gamma + beta
        return _gqa_forward(hidden_state, encoder_hidden_state, encoder_attention_mask, Wq, bq, Wk, bk, Wv, bv, Wo, bo, gamma, beta)

    def _L1_xattn_ref(hidden_states, encoder_states, ltor_mask, cross_mask, ln1_s, ln1_b, w_qkv, b_qkv, w_ao, b_ao, ln2_s, ln2_b, w_q, b_q, w_kv, b_kv, w_co, b_co, ln3_s, ln3_b, w1, b1, w2, b2):
        import jax, jax.numpy as jnp
        import numpy as np
        H = 512
        NH = 16
        HD = H // NH
        EPS = 1e-05

        def gelu(x):
            return 0.5 * x * (1.0 + jnp.tanh(0.7978845608028654 * x * (1.0 + 0.044715 * x * x)))

        def layernorm(x, scale, bias):
            m = jnp.mean(x, axis=-1, keepdims=True)
            v = jnp.mean(jnp.square(x - m), axis=-1, keepdims=True)
            return (x - m) * jax.lax.rsqrt(v + EPS) * scale + bias

        def split_heads(x):
            b, s, _ = x.shape
            return x.reshape(b, s, NH, HD).transpose(0, 2, 1, 3)

        def merge_heads(x):
            b, nh, s, hd = x.shape
            return x.transpose(0, 2, 1, 3).reshape(b, s, nh * hd)

        def attention(q, k, v, mask):
            scores = jnp.einsum('bhqd,bhkd->bhqk', q, k) / jnp.sqrt(jnp.float32(HD))
            scores = scores * mask - 10000.0 * (1.0 - mask)
            probs = jax.nn.softmax(scores, axis=-1)
            return jnp.einsum('bhqk,bhkd->bhqd', probs, v)
        ln_out = layernorm(hidden_states, ln1_s, ln1_b)
        qkv = ln_out @ w_qkv + b_qkv
        q, k, v = jnp.split(qkv, 3, axis=-1)
        ctx = merge_heads(attention(split_heads(q), split_heads(k), split_heads(v), ltor_mask))
        attn_out = ctx @ w_ao + b_ao
        x = hidden_states + attn_out
        ln_out = layernorm(x, ln2_s, ln2_b)
        q = ln_out @ w_q + b_q
        kv = encoder_states @ w_kv + b_kv
        k, v = jnp.split(kv, 2, axis=-1)
        ctx = merge_heads(attention(split_heads(q), split_heads(k), split_heads(v), cross_mask))
        cross_out = ctx @ w_co + b_co
        x = x + cross_out
        ln_out = layernorm(x, ln3_s, ln3_b)
        mlp_out = gelu(ln_out @ w1 + b1) @ w2 + b2
        return x + mlp_out

    def _L2_xattn_ref(x, state, ln1_w, ln1_b, ln2_w, ln2_b, maa_x, maa_w1, maa_w2, maa_stack, time_decay, td_w1, td_w2, u, Wr, Wk, Wv, Wg, Wo, gn_w, gn_b, ffn_maa_k, ffn_maa_r, Wfk, Wfr, Wfv):
        import jax, jax.numpy as jnp
        import numpy as np
        E, H, L, B = (512, 32, 256, 4)
        S = E // H
        DM, DD = (32, 64)

        def _ln(x, w, b, eps=1e-05):
            m = x.mean(-1, keepdims=True)
            v = ((x - m) ** 2).mean(-1, keepdims=True)
            return (x - m) / jnp.sqrt(v + eps) * w + b

        def _block(x, state, ln1_w, ln1_b, ln2_w, ln2_b, maa_x, maa_w1, maa_w2, maa_stack, time_decay, td_w1, td_w2, u, Wr, Wk, Wv, Wg, Wo, gn_w, gn_b, ffn_maa_k, ffn_maa_r, Wfk, Wfr, Wfv):
            b, l, e = x.shape
            h = u.shape[0]
            s_ = e // h
            xa = _ln(x, ln1_w, ln1_b)
            sx = jnp.concatenate([state[:, 1:2] - xa[:, :1], xa[:, :-1] - xa[:, 1:]], axis=1)
            xxx = jnp.tanh((xa + sx * maa_x) @ maa_w1).reshape(b, l, 5, DM)
            xxx = jnp.einsum('blfd,fde->blfe', xxx, maa_w2)
            xm = xa[:, :, None] + sx[:, :, None] * (maa_stack + xxx)
            xk, xw, xv, xr, xg = (xm[:, :, j] for j in range(5))
            w = jnp.exp(-jnp.exp(time_decay + jnp.tanh(xw @ td_w1) @ td_w2)).reshape(b, l, h, s_)
            r = (xr @ Wr.T).reshape(b, l, h, s_)
            k = (xk @ Wk.T).reshape(b, l, h, s_)
            v = (xv @ Wv.T).reshape(b, l, h, s_)
            g = jax.nn.silu(xg @ Wg.T)
            s0 = state[:, 2:2 + s_].reshape(b, h, s_, s_)

            def step(s, rkvw):
                r_t, k_t, v_t, w_t = rkvw
                a = k_t[..., :, None] * v_t[..., None, :]
                out = jnp.einsum('bhi,bhij->bhj', r_t, u * a + s)
                s = a + w_t[..., :, None] * s
                return (s, out)
            rkvw = tuple((jnp.moveaxis(t, 1, 0) for t in (r, k, v, w)))
            _, out = jax.lax.scan(step, s0, rkvw)
            out = jnp.moveaxis(out, 0, 1).reshape(b, l, e)
            og = out.reshape(b, l, h, s_)
            m = og.mean(-1, keepdims=True)
            va = ((og - m) ** 2).mean(-1, keepdims=True)
            og = ((og - m) / jnp.sqrt(va + 1e-05)).reshape(b, l, e) * gn_w + gn_b
            x1 = x + og * g @ Wo.T
            xc = _ln(x1, ln2_w, ln2_b)
            sx2 = jnp.concatenate([state[:, 0:1] - xc[:, :1], xc[:, :-1] - xc[:, 1:]], axis=1)
            xk2 = xc + sx2 * ffn_maa_k
            xr2 = xc + sx2 * ffn_maa_r
            rr = jax.nn.sigmoid(xr2 @ Wfr.T)
            kk = jnp.square(jax.nn.relu(xk2 @ Wfk.T))
            return x1 + rr * (kk @ Wfv.T)
        return _block(x, state, ln1_w, ln1_b, ln2_w, ln2_b, maa_x, maa_w1, maa_w2, maa_stack, time_decay, td_w1, td_w2, u, Wr, Wk, Wv, Wg, Wo, gn_w, gn_b, ffn_maa_k, ffn_maa_r, Wfk, Wfr, Wfv)

    def _L3_xattn_ref(x, state, ln1_w, ln1_b, ln2_w, ln2_b, maa_x, maa_w1, maa_w2, maa_stack, time_decay, decay_w1, decay_w2, faaaa, Wr, Wk, Wv, Wg, Wo, gn_w, gn_b, ffn_maa_k, ffn_maa_r, ffn_Wk, ffn_Wr, ffn_Wv, i):
        import jax, jax.numpy as jnp
        import numpy as np
        B, L, E, H = (4, 128, 512, 32)
        S = E // H
        EXTRA_MAA, EXTRA_DECAY = (32, 64)
        EPS = 1e-05

        def _ln(x, w, b):
            m = jnp.mean(x, axis=-1, keepdims=True)
            v = jnp.mean((x - m) ** 2, axis=-1, keepdims=True)
            return (x - m) * jax.lax.rsqrt(v + EPS) * w + b

        def _token_shift(xn, prev_row):
            first = (prev_row - xn[:, 0])[:, None]
            rest = xn[:, :-1] - xn[:, 1:]
            return jnp.concatenate([first, rest], axis=1)
        b, l = (x.shape[0], x.shape[1])
        i0 = (2 + S) * i + 0
        i1 = (2 + S) * i + 1
        xn = _ln(x, ln1_w, ln1_b)
        sx = _token_shift(xn, state[:, i1])
        xxx = jnp.tanh((xn + sx * maa_x) @ maa_w1).reshape(b, l, 5, 1, EXTRA_MAA)
        xxx = jnp.matmul(xxx, maa_w2).reshape(b, l, 5, E)
        x5 = xn[:, :, None] + sx[:, :, None] * (maa_stack + xxx)
        w = jnp.exp(-jnp.exp(time_decay + jnp.tanh(x5[:, :, 1] @ decay_w1) @ decay_w2))
        w = w.reshape(b, l, H, S)
        r = (x5[:, :, 3] @ Wr.T).reshape(b, l, H, S)
        k = (x5[:, :, 0] @ Wk.T).reshape(b, l, H, S)
        v = (x5[:, :, 2] @ Wv.T).reshape(b, l, H, S)
        g = jax.nn.silu(x5[:, :, 4] @ Wg.T)
        s0 = state[:, (2 + S) * i + 2:(2 + S) * (i + 1)].reshape(b, H, S, S)
        u = faaaa[None, :, :, None]

        def step(s, rkvw):
            r_t, k_t, v_t, w_t = rkvw
            a = k_t[:, :, :, None] * v_t[:, :, None, :]
            out = jnp.einsum('bhk,bhkd->bhd', r_t, u * a + s)
            return (a + w_t[:, :, :, None] * s, out)
        xs = tuple((jnp.moveaxis(t, 1, 0) for t in (r, k, v, w)))
        _, outs = jax.lax.scan(step, s0, xs)
        att = jnp.moveaxis(outs, 0, 1).reshape(b, l, E)
        a4 = att.reshape(b, l, H, S)
        m = jnp.mean(a4, axis=-1, keepdims=True)
        var = jnp.mean((a4 - m) ** 2, axis=-1, keepdims=True)
        att = ((a4 - m) * jax.lax.rsqrt(var + EPS)).reshape(b, l, E) * gn_w + gn_b
        x = x + att * g @ Wo.T
        xn2 = _ln(x, ln2_w, ln2_b)
        sx2 = _token_shift(xn2, state[:, i0])
        xk = xn2 + sx2 * ffn_maa_k
        xr = xn2 + sx2 * ffn_maa_r
        rr = jax.nn.sigmoid(xr @ ffn_Wr.T)
        kk = jnp.square(jax.nn.relu(xk @ ffn_Wk.T))
        x = x + rr * (kk @ ffn_Wv.T)
        return x
    x = _L0_xattn_ref(x, ctx_2048, mask_Bx1xSxS2_ff0, L0_xattn_Wq, L0_xattn_bq, L0_xattn_Wk, L0_xattn_bk, L0_xattn_Wv, L0_xattn_bv, L0_xattn_Wo, L0_xattn_bo, L0_xattn_gamma, L0_xattn_beta)
    x = _L1_xattn_ref(x, ctx_2048, mask_1x1xSxS2_fc1, mask_Bx1xSxS2_ff1, L1_xattn_ln1_s, L1_xattn_ln1_b, L1_xattn_w_qkv, L1_xattn_b_qkv, L1_xattn_w_ao, L1_xattn_b_ao, L1_xattn_ln2_s, L1_xattn_ln2_b, L1_xattn_w_q, L1_xattn_b_q, L1_xattn_w_kv, L1_xattn_b_kv, L1_xattn_w_co, L1_xattn_b_co, L1_xattn_ln3_s, L1_xattn_ln3_b, L1_xattn_w1, L1_xattn_b1, L1_xattn_w2, L1_xattn_b2)
    x = _L2_xattn_ref(x, ctx_2048, L2_xattn_ln1_w, L2_xattn_ln1_b, L2_xattn_ln2_w, L2_xattn_ln2_b, L2_xattn_maa_x, L2_xattn_maa_w1, L2_xattn_maa_w2, L2_xattn_maa_stack, L2_xattn_time_decay, L2_xattn_td_w1, L2_xattn_td_w2, L2_xattn_u, L2_xattn_Wr, L2_xattn_Wk, L2_xattn_Wv, L2_xattn_Wg, L2_xattn_Wo, L2_xattn_gn_w, L2_xattn_gn_b, L2_xattn_ffn_maa_k, L2_xattn_ffn_maa_r, L2_xattn_Wfk, L2_xattn_Wfr, L2_xattn_Wfv)
    x = _L3_xattn_ref(x, ctx_2048, L3_xattn_ln1_w, L3_xattn_ln1_b, L3_xattn_ln2_w, L3_xattn_ln2_b, L3_xattn_maa_x, L3_xattn_maa_w1, L3_xattn_maa_w2, L3_xattn_maa_stack, L3_xattn_time_decay, L3_xattn_decay_w1, L3_xattn_decay_w2, L3_xattn_faaaa, L3_xattn_Wr, L3_xattn_Wk, L3_xattn_Wv, L3_xattn_Wg, L3_xattn_Wo, L3_xattn_gn_w, L3_xattn_gn_b, L3_xattn_ffn_maa_k, L3_xattn_ffn_maa_r, L3_xattn_ffn_Wk, L3_xattn_ffn_Wr, L3_xattn_ffn_Wv, 0)
    return x

_drawn_inputs = setup_inputs


def setup_inputs(seed=0):
    import zlib

    import numpy as np

    out = dict(_drawn_inputs(seed))
    spreads = {'L0_xattn_bq': (0.0, 0.8),
     'L0_xattn_bk': (0.0, 2.0),
     'L0_xattn_bv': (0.0, 0.1),
     'L0_xattn_bo': (0.0, 0.1),
     'L0_xattn_gamma': (1.0, 0.2),
     'L0_xattn_beta': (0.0, 0.1),
     'L1_xattn_ln1_s': (1.0, 0.6),
     'L1_xattn_ln1_b': (0.0, 0.369),
     'L1_xattn_b_qkv': (0.0, 0.1),
     'L1_xattn_b_ao': (0.0, 0.1),
     'L1_xattn_ln2_s': (1.0, 0.6),
     'L1_xattn_ln2_b': (0.0, 0.8),
     'L1_xattn_b_q': (0.0, 2.0),
     'L1_xattn_b_kv': (0.0, 0.1),
     'L1_xattn_b_co': (0.0, 0.1),
     'L1_xattn_ln3_s': (1.0, 0.2),
     'L1_xattn_ln3_b': (0.0, 0.325),
     'L1_xattn_b1': (0.0, 0.1),
     'L1_xattn_b2': (0.0, 0.1),
     'L2_xattn_ln1_w': (1.0, 0.2),
     'L2_xattn_ln1_b': (0.0, 0.296),
     'L2_xattn_ln2_w': (1.0, 0.6),
     'L2_xattn_ln2_b': (0.0, 0.8),
     'L2_xattn_gn_w': (1.0, 0.6),
     'L2_xattn_gn_b': (0.0, 0.713),
     'L3_xattn_ln1_w': (1.0, 0.2),
     'L3_xattn_ln1_b': (0.0, 0.303),
     'L3_xattn_ln2_w': (1.0, 0.6),
     'L3_xattn_ln2_b': (0.0, 0.8),
     'L3_xattn_gn_w': (1.0, 0.6),
     'L3_xattn_gn_b': (0.0, 0.8)}
    factors = {'L0_xattn_Wq': 7.216,
     'L0_xattn_Wk': 7.021,
     'L1_xattn_w_q': 6.962,
     'L2_xattn_maa_x': 8.0,
     'L2_xattn_maa_w1': 3.123,
     'L2_xattn_maa_w2': 3.155,
     'L2_xattn_td_w1': 8.0,
     'L2_xattn_td_w2': 8.0,
     'L2_xattn_u': 3.128,
     'L2_xattn_ffn_maa_k': 5.761,
     'L2_xattn_ffn_maa_r': 8.0,
     'L2_xattn_Wfr': 4.096,
     'L3_xattn_maa_x': 8.0,
     'L3_xattn_maa_w1': 3.254,
     'L3_xattn_maa_w2': 3.276,
     'L3_xattn_maa_stack': 7.367,
     'L3_xattn_decay_w1': 8.0,
     'L3_xattn_decay_w2': 8.0,
     'L3_xattn_faaaa': 3.229,
     'L3_xattn_ffn_maa_k': 8.0,
     'L3_xattn_ffn_maa_r': 8.0,
     'L3_xattn_ffn_Wr': 4.345}
    for name, (base, spread) in spreads.items():
        noise = np.random.default_rng([zlib.crc32(name.encode()), seed]).standard_normal(out[name].shape)
        drawn = base * np.exp(spread * noise) if base else spread * noise
        out[name] = jnp.asarray(drawn.astype(out[name].dtype))
    for name, factor in factors.items():
        out[name] = (out[name] * factor).astype(out[name].dtype)
    return out
```

```python
from contextlib import ExitStack

import concourse.bass as bass
from concourse import mybir

F32 = mybir.dt.float32
F32R = mybir.dt.float32r
ALU = mybir.AluOpType
ACT = mybir.ActivationFunctionType
AX = mybir.AxisListType

P = 128
B, L, H = 4, 512, 512
C = H // P
FFN = 4
WSLOTS = 3
RING = 3
RING0 = 4
OBANK = 7
LAG = 2
PSLOTS = LAG + 1

VECTORS = ['bq0', 'bk0', 'ln1_s', 'ln1_b', 'bq1', 'bk1', 'ln2_s', 'ln2_b', 'bq2', 'bk2', 'ln3_s', 'ln3_b',
           'b1_0', 'b1_1', 'b1_2', 'b1_3']
RWKV_VECTORS = ['ln1_w', 'ln1_b', 'ln2_w', 'ln2_b', 'maa_x', 'maa_k', 'maa_w', 'maa_v', 'maa_r', 'maa_g',
                'decay', 'u', 'gn_w', 'gn_b', 'ffn_k', 'ffn_r']
for _layer in (2, 3):
    VECTORS += [f'{n}_{_layer}' for n in RWKV_VECTORS]
COL = {n: C * k for k, n in enumerate(VECTORS)}
ROWS = {0: ['bv', 'bo', 'gamma', 'beta'], 1: ['bv', 'b_ao', 'bv2', 'b_co', 'b2']}
NROWS = 4

BLOCKS = ['kv0', 'q0', 'o0', 'v1', 'q1', 'k1', 'o1', 'v2', 'q2', 'k2', 'o2',
          'up_0', 'up_1', 'down_0', 'up_2', 'down_1', 'up_3', 'down_2', 'down_3']
for _layer in (2, 3):
    BLOCKS += [f'{n}_{_layer}' for n in ('small', 'maa2', 'k', 'r', 'v', 'g', 'o', 'fk', 'fr', 'fv')]
SMALL_MAA, SMALL_TD1, SMALL_TD2 = 0, C * 160, C * 224

HEADS = 8
HS = 16


class Signal:

    def __init__(self, sem, known):
        self.sem, self.count, self.known, self.marks = sem, 0, known, {}

    def reach(self, *label):
        self.count += 1
        assert label not in self.marks, label
        self.marks[label] = self.count
        return self.sem, 1

    def when(self, *label):
        return self.sem, (self.known[label] if self.known is not None else 1)


class Ring:

    def __init__(self, known):
        self.labels, self.known = [], known

    def take(self, *label):
        self.labels.append(label)
        n = len(self.labels) - 1
        return RING0 + n % RING, self.labels[n - RING] if n >= RING else None

    def bank(self, *label):
        return RING0 + (self.known[label] if self.known is not None else 0) % RING


SIGNALS = ['tile_ready', 'scores_ready', 'context_ready', 'mlp_ready', 'vb_ready', 'reduced',
           'act_emptied', 'dve_emptied', 'exp_done', 'act_done', 'scores_taken', 'dve_done', 'inverse_done',
           'pool_done', 'normalised']
LOADS = ['x_in', 'xT_in', 'ctx_in', 'rows_in', 'mask0_in', 'mask1_in', 'mask2_in', 's0_in', 'stack0', 'stack1', 'out_done']


def build(nc, a, known, samples=B):
    base = -(-nc.sbuf_base // 32) * 32
    top = nc.sbuf_usable_end

    def place(name, shape, offset, dt=F32):
        n = 1
        for s in shape[1:]:
            n *= s
        assert base + offset + 4 * n <= top, (name, offset + 4 * n)
        return nc.alloc_sbuf_tensor_at(name, shape, dt, offset=base + offset), offset + -(-4 * n // 32) * 32

    at = 0
    x, at = place('x', [P, C, H], at)
    ctxT, at = place('ctxT', [P, C, L], at)
    wring, at = place('wring', [P, WSLOTS, C * H], at)
    maskA, at = place('maskA', [P, C, L], at)
    maskB, at = place('maskB', [P, C, L], at)
    neg, at = place('neg', [P, C, L], at)
    khi0, _ = place('khi0', [P, L], at - 4 * C * L, F32R)
    klo0, _ = place('klo0', [P, L], at - 4 * (C - 1) * L, F32R)
    cols, at = place('cols', [P, C * len(VECTORS)], at)
    scaled, at = place('scaled', [P, 3 * C], at)
    ident, at = place('ident', [P, P], at)
    ones_block, at = place('ones_block', [P, P], at)
    permute, at = place('permute', [P, P], at)
    permute_back, at = place('permute_back', [P, P], at)
    gather, at = place('gather', [P, 4, 32], at)
    stats, at = place('stats', [P, C, 6], at)
    moments, at = place('moments', [P, C, 2], at)
    rstd, at = place('rstd', [P, C], at)
    varep, at = place('varep', [P, C], at)
    minus_half, at = place('minus_half', [P, 32], at)
    top_common = at
    rows, at = place('rows', [P, NROWS, H], at)
    srcT, at = place('srcT', [P, C, L], at)
    v1, at = place('v1', [P, C, H], at)
    v0, _ = place('v0', [P, C, 8, 32], at - 8192)
    oT, at = place('oT', [P, C, L], at)
    probs, at = place('probs', [P, PSLOTS, C, L], at)
    xn, _ = place('xn', [P, C, H], at - 4 * PSLOTS * C * L)
    pT, at = place('pT', [P, 4, C, L], at)
    hidden, _ = place('hidden', [P, 2, C, L], at - 4 * 4 * C * L)
    qstack, at = place('qstack', [96, 2, 4, L], at, F32R)
    kstack, at = place('kstack', [96, 2, 4, L], at, F32R)
    split, at = place('split', [P, 2, L], at)
    hi, at = place('hi', [P, 4, L], at, F32R)
    lo, at = place('lo', [P, 4, L], at, F32R)
    row_max, at = place('row_max', [P, PSLOTS, C], at)
    row_sum, at = place('row_sum', [P, PSLOTS, C], at)
    row_inv, at = place('row_inv', [P, PSLOTS, C], at)
    at = top_common
    xa, at = place('xa', [P, C, L + 1], at)
    sx, at = place('sx', [P, C, L], at)
    mix, at = place('mix', [P, 4, C, L], at)
    xn2, _ = place('xn2', [P, C, H], at - 16 * C * L)
    centred, _ = place('centred', [P, C, H], at - 16 * C * L)
    squared, _ = place('squared', [P, C, H], at - 12 * C * L)
    gated, _ = place('gated', [P, C, L], at - 8 * C * L)
    decay, at = place('decay', [P, C, L], at)
    z, at = place('z', [P, 2, L], at)
    tdh, at = place('tdh', [64, L], at)
    kT, at = place('kT', [P, 2, L], at)
    rT, at = place('rT', [P, 2, L], at)
    vT, at = place('vT', [P, 2, L], at)
    vhi, at = place('vhi', [P, 2, L], at, F32R)
    vlo, at = place('vlo', [P, 2, L], at, F32R)
    ruk, at = place('ruk', [P, 2, L], at)
    bonus, at = place('bonus', [P, 2, L], at)
    kvp, at = place('kvp', [P, 3, L], at)
    state, at = place('state', [P, 3, L + 1], at)
    prod, at = place('prod', [P, 3, L], at)
    recT, at = place('recT', [P, C, L], at)
    gT, at = place('gT', [P, C, L], at)
    pick, at = place('pick', [P, HS * P], at, F32R)
    s0, at = place('s0', [P, C, HS], at)
    gsum, at = place('gsum', [P, C, 32], at)
    gsq, at = place('gsq', [P, C, 32], at)
    ginv, at = place('ginv', [P, C, 32], at)

    with ExitStack() as stack:
        ps = stack.enter_context(nc.psum_tensor('ps', [P, 8, 512], F32))
        sems = {n: stack.enter_context(nc.semaphore(n)) for n in SIGNALS + LOADS + [f'w{i}' for i in range(WSLOTS)]}
        setup_in = stack.enter_context(nc.semaphore('setup_in'))
        sig = {n: Signal(sems[n], (known or {}).get(n)) for n in SIGNALS}
        ring = Ring((known or {}).get('ring'))
        S = sig
        tile_ready, act_emptied, dve_emptied = S['tile_ready'], S['act_emptied'], S['dve_emptied']
        act_done, dve_done, pool_done = S['act_done'], S['dve_done'], S['pool_done']

        def col(name, c):
            return cols[:, COL[name] + c:COL[name] + c + 1]

        with nc.Block() as block:
            @block.sync
            def _(sp):
                sp.dma_start(cols[:, :], a['cols']).then_inc(setup_in, 16)
                sp.dma_start(ident[:, :], a['ident']).then_inc(setup_in, 16)
                sp.dma_start(ones_block[:, :], a['ones_block']).then_inc(setup_in, 16)
                sp.dma_start(permute[:, :], a['permute']).then_inc(setup_in, 16)
                sp.dma_start(permute_back[:, :], a['permute_back']).then_inc(setup_in, 16)
                sp.dma_start(gather[:, :, :], a['gather']).then_inc(setup_in, 16)
                sp.wait_ge(setup_in, 16 * 6)

        with nc.Block() as block:
            @block.gpsimd
            def _(pool):
                pool.memset(minus_half[:, :], -0.5)

            @block.vector
            def _(dve):
                for k, (n, s) in enumerate((('bq0', 0.25), ('bq1', 32.0 ** -0.5), ('bq2', 32.0 ** -0.5))):
                    dve.tensor_scalar(scaled[:, k * C:(k + 1) * C], cols[:, COL[n]:COL[n] + C], s, None, ALU.mult)

        def evac_wait(pe, label):
            if label in (act_emptied.known or {}):
                pe.wait_ge(*act_emptied.when(*label))
            else:
                pe.wait_ge(*dve_emptied.when(*label))

        def take(pe, *label):
            bank, before = ring.take(*label)
            if before is not None:
                evac_wait(pe, before)
            return ps[:, bank, :]

        uses = {b: n for n, b in enumerate(BLOCKS)}

        def weights(name):
            return wring[:, uses[name] % WSLOTS, :]

        def w_wait(pe, name):
            n = uses[name]
            pe.wait_ge(sems[f'w{n % WSLOTS}'], 16 * (n // WSLOTS + 1))

        loaded = [0]

        def load_weights(sp, upto, freed):
            while loaded[0] <= uses[upto]:
                n = loaded[0]
                if n >= WSLOTS:
                    sp.wait_ge(*freed(BLOCKS[n - WSLOTS]))
                sp.dma_start(wring[:, n % WSLOTS, :], a['blocks'][n]).then_inc(sems[f'w{n % WSLOTS}'], 16)
                loaded[0] += 1

        LAST = {'kv0': ('k', 0), 'q0': ('q', 0, 3), 'o0': ('out', 0, 3),
                'v1': ('v', 1, 3), 'q1': ('q', 1, 3), 'k1': ('k', 1, 3), 'o1': ('out', 1, 3),
                'v2': ('v', 2, 3), 'q2': ('q', 2, 3), 'k2': ('k', 2, 3), 'o2': ('out', 2, 3)}
        for i in range(FFN):
            LAST[f'up_{i}'] = ('up', i, 3)
        for l in (2, 3):
            LAST |= {f'small_{l}': ('decay', l, 3), f'maa2_{l}': ('mix', l, 'g', 3), f'k_{l}': ('kp', l, 3),
                     f'r_{l}': ('rp', l, 3), f'v_{l}': ('vp', l, 3), f'g_{l}': ('gp', l, 3), f'o_{l}': ('wo', l, 3),
                     f'fk_{l}': ('fk', l, 3), f'fr_{l}': ('fr', l, 3), f'fv_{l}': ('fv', l, 3)}

        def freed(name):
            if name.startswith('down'):
                return S['mlp_ready'].when(name)
            return tile_ready.when(*LAST[name])

        def to_T(pe, tile, w, src, oc, rows_=P, width=H, base_=0, fin=None):
            for fc in range(C):
                m = nc.tensor.matmul(tile[0:rows_, :], w[:, base_ + fc * width + oc * P:base_ + fc * width + oc * P + rows_],
                                     src[:, fc, :], start=(fc == 0), stop=(fc == C - 1))
            m.then_inc(*fin)

        def to_N(pe, tile, w, src, tc, n=H, base_=0, fin=None):
            for fc in range(C):
                m = nc.tensor.matmul(tile[:, 0:n], src[:, fc, tc * P:(tc + 1) * P],
                                     w[:, fc * H + base_:fc * H + base_ + n], start=(fc == 0), stop=(fc == C - 1))
            m.then_inc(*fin)

        def dve_norm(dve, tag, ready, out, version):
            for tc in range(C):
                if ready is not None:
                    ready(dve, tc)
                nc.vector.bn_stats(stats[:, tc, :], x[:, tc, :]).then_inc(*dve_done.reach('stats', tag, tc))
            for tc in range(C):
                dve.wait_ge(*dve_done.when('stats', tag, tc))
                nc.vector.bn_aggr(moments[:, tc, :], stats[:, tc, :]).then_inc(*dve_done.reach('moments', tag, tc))
            dve.wait_ge(*pool_done.when('rstd', tag))
            for tc in range(C):
                nc.vector.tensor_scalar(out[:, tc, :], x[:, tc, :], moments[:, tc, 0:1], rstd[:, tc:tc + 1],
                                        ALU.subtract, ALU.mult).then_inc(*dve_done.reach('xn', tag, tc))

        def pool_norm(pool, tag, eps):
            pool.wait_ge(*dve_done.when('moments', tag, C - 1))
            nc.gpsimd.tensor_scalar(varep[:, :], moments[:, :, 1], 1.0, eps, ALU.mult, ALU.add)\
                .then_inc(*pool_done.reach('varep', tag))
            pool.wait_ge(*pool_done.when('varep', tag))
            nc.gpsimd.tensor_tensor(rstd[:, :], varep[:, :], minus_half[:, 0:C], ALU.pow)\
                .then_inc(*pool_done.reach('rstd', tag))

        def pe_turn(pe, tag, src, what, wait, matrix=None):
            for c in range(C):
                tile = take(pe, what, tag, c)
                for t in range(C):
                    wait(pe, c, t)
                    m = nc.tensor.transpose(tile[:, t * P:(t + 1) * P], src[:, t, c * P:(c + 1) * P],
                                            (ident if matrix is None else matrix)[:, :])
                m.then_inc(*tile_ready.reach(what, tag, c))

        def pe_norm_turn(pe, tag, src):
            def wait(pe, c, t):
                if c == 0:
                    pe.wait_ge(*dve_done.when('xn', tag, t))
            pe_turn(pe, tag, src, 'lnT', wait)

        def act_norm(act, tag, out, wcol, bcol, shift=0):
            for c in range(C):
                act.wait_ge(*tile_ready.when('lnT', tag, c))
                nc.scalar.activation(out[:, c, shift:shift + L], ps[:, ring.bank('lnT', tag, c), :], ACT.Identity,
                                     bias=col(bcol, c), scale=col(wcol, c)).then_inc(*act_emptied.reach('lnT', tag, c))

        class Attention:
            def __init__(self, tag, hd, groups, vcols, vblk, voff, qblk, kblk, koff, src, oblk, bq, bk, scale, mask, rowbv, rowbo):
                self.tag, self.hd, self.groups, self.vcols = tag, hd, groups, vcols
                self.vblk, self.voff, self.qblk, self.kblk, self.koff = vblk, voff, qblk, kblk, koff
                self.src, self.oblk, self.bq, self.bk, self.scale, self.mask = src, oblk, bq, bk, scale, mask
                self.kt = 3 * hd
                self.rowbv, self.rowbo = rowbv, rowbo
                self.shared = groups == 8
                self.heads = 4 * groups
                self.owner = 'adad' if self.shared else 'aaaa'

            def qi(self, g):
                return g if self.shared else g % 2

            def ki(self, g):
                return 2 + g % 2

            def parts(self, kind, g):
                if kind == 'k' and self.shared:
                    return khi0[:, :], klo0[:, :]
                idx = self.qi(g) if kind == 'q' else self.ki(g)
                return hi[:, idx, :], lo[:, idx, :]

        cross_src = ctxT
        A0 = Attention(0, 16, 8, 128, 'kv0', 128, 'q0', 'kv0', 0, cross_src, 'o0', 0, 'bk0', 0.25, maskA, 0, 1)
        A1 = Attention(1, 32, 4, 512, 'v1', 0, 'q1', 'k1', 0, srcT, 'o1', 1, 'bk1', 32.0 ** -0.5, maskB, 0, 1)
        A2 = Attention(2, 32, 4, 512, 'v2', 0, 'q2', 'k2', 0, cross_src, 'o2', 2, 'bk2', 32.0 ** -0.5, maskA, 2, 3)

        def pe_q(pe, A, g):
            to_T(pe, take(pe, 'q', A.tag, g), weights(A.qblk), srcT, g, fin=tile_ready.reach('q', A.tag, g))

        def pe_k(pe, A, g):
            label = ('k', A.tag) if A.shared else ('k', A.tag, g)
            to_T(pe, take(pe, *label), weights(A.kblk), A.src, 0 if A.shared else g, base_=A.koff,
                 fin=tile_ready.reach(*label))

        def pe_attention(pe, A):
            t = A.tag
            w_wait(pe, A.vblk)
            if A.src is ctxT and t == 0:
                pe.wait_ge(sems['ctx_in'], 16)
            if t == 1:
                pe.wait_ge(*act_emptied.when('lnT', 'ln1', C - 1))
            for tc in range(C):
                to_N(pe, take(pe, 'v', t, tc), weights(A.vblk), A.src, tc, n=A.vcols, base_=A.voff,
                     fin=tile_ready.reach('v', t, tc))
            if A.shared:
                pe_k(pe, A, 0)
            w_wait(pe, A.qblk)
            if t == 0:
                pe.wait_ge(sems['xT_in'], 16)
            if t == 2:
                pe.wait_ge(*act_emptied.when('lnT', 'ln2', C - 1))
            for g in range(4 if A.shared else 1):
                pe_q(pe, A, g)
            if not A.shared:
                w_wait(pe, A.kblk)
                pe_k(pe, A, 0)
            for n in range(A.heads + LAG):
                g, i = divmod(n, 4)
                if n < A.heads:
                    if i == 0:
                        pe.wait_ge(sems[f'stack{g % 2}'], stack_total(A, g))
                    for qc in range(C):
                        if n >= 1:
                            pe.wait_ge(*S['scores_taken'].when(t, n - 1, qc))
                        m = nc.tensor.matmul(ps[:, qc, :], qstack[0:A.kt, g % 2, i, qc * P:(qc + 1) * P],
                                             kstack[0:A.kt, g % 2, 0 if A.shared else i, :], start=True, stop=True)
                        m.then_inc(*S['scores_ready'].reach(t, n, qc))
                    if not A.shared and g + 1 < A.groups:
                        if i == 0:
                            pe_q(pe, A, g + 1)
                        if i == 1:
                            pe_k(pe, A, g + 1)
                m = n - LAG
                if m >= 0:
                    mg, mi = divmod(m, 4)
                    for kc in range(C):
                        tile = take(pe, 'pT', t, m, kc)
                        for qc in range(C):
                            if kc == 0:
                                pe.wait_ge(*S['normalised'].when(t, m, qc))
                            ins = nc.tensor.transpose(tile[:, qc * P:(qc + 1) * P],
                                                      probs[:, m % PSLOTS, qc, kc * P:(kc + 1) * P], ident[:, :])
                        ins.then_inc(*tile_ready.reach('pT', t, m, kc))
                    if mi == 3:
                        first, final = (mg % 2 == 0, mg % 2 == 1) if A.shared else (True, True)
                        if first and mg > 0:
                            pe.wait_ge(*act_done.when('context', t, (mg // 2 if A.shared else mg) - 1))
                        if mg == 0:
                            for tc in range(C):
                                pe.wait_ge(*dve_emptied.when('v', t, tc))
                        for h in range(4):
                            for kc in range(C):
                                evac_wait(pe, ('pT', t, 4 * mg + h, kc))
                        for kc in range(C):
                            for h in range(4):
                                lhs = v0[:, kc, mg, :] if A.shared else v1[:, kc, (4 * mg + h) * 32:(4 * mg + h + 1) * 32]
                                ins = nc.tensor.matmul(ps[32 * h:32 * h + 32, OBANK, :], lhs, pT[:, h, kc, :],
                                                       start=(kc == 0 and first), stop=(kc == C - 1 and final))
                        ins.then_inc(*S['context_ready'].reach(t, mg))
            w_wait(pe, A.oblk)
            for c in range(C):
                pe.wait_ge(*act_done.when('context', t, c))
            for tc in range(C):
                to_N(pe, take(pe, 'out', t, tc), weights(A.oblk), oT, tc, fin=tile_ready.reach('out', t, tc))

        nstack = {0: 6, 1: 24}
        stack_counts = {}

        def stack_total(A, g):
            return stack_counts[(A.tag, g)]

        totals = [0, 0]
        for A in (A0, A1, A2):
            for g in range(A.groups):
                totals[g % 2] += 16 * (6 if A.shared else 24)
                stack_counts[(A.tag, g)] = totals[g % 2]

        def sp_stack(sp, A, g):
            t, s = A.tag, sems[f'stack{g % 2}']

            def copy(out, in_):
                return sp.dma_start(out.bitcast(F32), in_.bitcast(F32))

            if g >= 2:
                sp.wait_ge(*S['scores_ready'].when(t, 4 * (g - 2) + 3, C - 1))
            elif t > 0:
                sp.wait_ge(*S['scores_ready'].when(t - 1, (31 if t == 1 else 15), C - 1))
            if A.shared:
                if g == 0:
                    for j in range(4):
                        sp.wait_ge(*pool_done.when('qlo', t, j))
                    sp.wait_ge(*pool_done.when('klo', t, 0))
            else:
                sp.wait_ge(*pool_done.when('qlo', t, g))
                sp.wait_ge(*pool_done.when('klo', t, g))
            for part, (q, k) in enumerate(((hi, hi), (lo, hi), (hi, lo))):
                r = part * A.hd
                if A.shared:
                    copy(qstack[r:r + 16, g % 2, :, :], q[16 * g:16 * g + 16, 0:4, :]).then_inc(s, 16)
                    copy(kstack[r:r + 16, g % 2, 0, :], (khi0 if k is hi else klo0)[16 * g:16 * g + 16, :]).then_inc(s, 16)
                else:
                    for i in range(4):
                        copy(qstack[r:r + 32, g % 2, i, :], q[32 * i:32 * i + 32, A.qi(g), :]).then_inc(s, 16)
                        copy(kstack[r:r + 32, g % 2, i, :], k[32 * i:32 * i + 32, A.ki(g), :]).then_inc(s, 16)

        def act_split(act, A, kind, g):
            t = A.tag
            label = ('k', t) if kind == 'k' and A.shared else (kind, t, g)
            act.wait_ge(*tile_ready.when(*label))
            prev = last_split.get(kind)
            if prev is not None:
                act.wait_ge(*pool_done.when(*prev))
            last_split[kind] = (f'{kind}lo', t, g)
            s = 0 if kind == 'q' else 1
            bias = scaled[:, t * C + g:t * C + g + 1] if kind == 'q' else col(A.bk, g)
            nc.scalar.activation(split[:, s, :], ps[:, ring.bank(*label), :], ACT.Identity, bias=bias,
                                 scale=A.scale if kind == 'q' else 1.0).then_inc(*act_emptied.reach(*label))
            if not A.shared and g >= 2:
                act.wait_ge(sems[f'stack{g % 2}'], stack_total(A, g - 2))
            act.wait_ge(*act_emptied.when(*label))
            nc.scalar.activation(A.parts(kind, g)[0], split[:, s, :], ACT.Copy).then_inc(*act_done.reach(f'{kind}hi', t, g))

        last_split = {}

        def pool_split(pool, A, kind, g):
            t, s = A.tag, 0 if kind == 'q' else 1
            high, low = A.parts(kind, g)
            pool.wait_ge(*act_done.when(f'{kind}hi', t, g))
            nc.gpsimd.tensor_tensor(low, split[:, s, :], high.bitcast(F32), ALU.subtract)\
                .then_inc(*pool_done.reach(f'{kind}lo', t, g))

        def act_attention(act, A):
            t = A.tag
            if t == 1:
                act.wait_ge(sems['stack0'], stack_total(A0, 6))
                act.wait_ge(sems['stack1'], stack_total(A0, 7))
            if t == 2:
                act.wait_ge(sems['stack0'], stack_total(A1, 2))
                act.wait_ge(sems['stack1'], stack_total(A1, 3))
            if A.shared:
                act_split(act, A, 'k', 0)
            for g in range(4 if A.shared else 1):
                act_split(act, A, 'q', g)
            if not A.shared:
                act_split(act, A, 'k', 0)

            def empty(m, kc):
                if A.owner[kc] != 'a':
                    return
                act.wait_ge(*tile_ready.when('pT', t, m, kc))
                if m >= 4:
                    act.wait_ge(*S['context_ready'].when(t, m // 4 - 1))
                nc.scalar.activation(pT[:, m % 4, kc, :], ps[:, ring.bank('pT', t, m, kc), :], ACT.Copy)\
                    .then_inc(*act_emptied.reach('pT', t, m, kc))

            def exp(n, qc):
                act.wait_ge(*S['scores_taken'].when(t, n, qc) if A.shared else dve_done.when('sm', t, n, qc))
                p = probs[:, n % PSLOTS, qc, :]
                nc.scalar.activation(p, p, ACT.Exp, bias=row_max[:, n % PSLOTS, qc:qc + 1], scale=-1.0,
                                     accum_out=row_sum[:, n % PSLOTS, qc:qc + 1]).then_inc(*S['exp_done'].reach(t, n, qc))

            for n in range(A.heads + LAG):
                g, i = divmod(n, 4)
                m = n - LAG
                if n < A.heads and not A.shared and g + 1 < A.groups:
                    if i == 0:
                        act_split(act, A, 'q', g + 1)
                    if i == 1:
                        act_split(act, A, 'k', g + 1)
                for step in ('e0', 'e1', 'x0', 'e2', 'x1', 'e3', 'x2', 'x3'):
                    if step[0] == 'e' and m >= 0:
                        empty(m, int(step[1]))
                    if step[0] == 'x' and n < A.heads:
                        exp(n, int(step[1]))
                if m >= 0 and m % 4 == 3 and (not A.shared or (m // 4) % 2 == 1):
                    c = m // 8 if A.shared else m // 4
                    act.wait_ge(*S['context_ready'].when(t, m // 4))
                    nc.scalar.activation(oT[:, c, :], ps[:, OBANK, :], ACT.Copy).then_inc(*act_done.reach('context', t, c))

        def dve_attention(dve, A):
            t = A.tag
            if t == 0:
                dve.wait_ge(sems['rows_in'], 16)
            if t == 1:
                dve.wait_ge(sems['rows_in'], 32)
            for tc in range(C):
                dve.wait_ge(*tile_ready.when('v', t, tc))
                tile = ps[:, ring.bank('v', t, tc), :]
                if A.shared:
                    if tc == 0:
                        dve.wait_ge(*pool_done.when('v0', 'clear'))
                    for par in range(2):
                        o = v0[:, tc, :, :].rearrange('p (g two) d -> p two g d', two=2)[:, par, :, 16 * par:16 * par + 16]
                        i0 = tile[:, 0:128].rearrange('p (g two d) -> p two g d', two=2, d=16)[:, par, :, :]
                        i1 = rows[:, A.rowbv, 0:128].rearrange('p (g two d) -> p two g d', two=2, d=16)[:, par, :, :]
                        ins = nc.vector.tensor_tensor(o, i0, i1, ALU.add)
                    ins.then_inc(*dve_emptied.reach('v', t, tc))
                else:
                    nc.vector.tensor_tensor(v1[:, tc, :], tile, rows[:, A.rowbv, :], ALU.add)\
                        .then_inc(*dve_emptied.reach('v', t, tc))
            dve.wait_ge(sems['mask%d_in' % t], 16)
            if t > 0:
                dve.wait_ge(*pool_done.when('neg', t))

            def inverse(n):
                for qc in range(C):
                    dve.wait_ge(*S['exp_done'].when(t, n, qc))
                nc.vector.reciprocal(row_inv[:, n % PSLOTS, :], row_sum[:, n % PSLOTS, :])\
                    .then_inc(*S['inverse_done'].reach(t, n))

            def slot_free(n):
                if n >= PSLOTS:
                    dve.wait_ge(*tile_ready.when('pT', t, n - PSLOTS, C - 1))

            def add_max(n, qc):
                s = n % PSLOTS
                if A.shared:
                    dve.wait_ge(*S['scores_ready'].when(t, n, qc))
                    src, other, fin = ps[:, qc, :], A.mask[:, qc, :], S['scores_taken'].reach(t, n, qc)
                else:
                    dve.wait_ge(*S['scores_taken'].when(t, n, qc))
                    src, other, fin = probs[:, s, qc, :], neg[:, qc, :], dve_done.reach('sm', t, n, qc)
                nc.vector.tensor_tensor_reduce(out=probs[:, s, qc, :], in0=src, in1=other, scale=-1.0, scalar=3.0e38,
                                               op0=ALU.add, op1=ALU.min,
                                               accum_out=row_max[:, s, qc:qc + 1]).then_inc(*fin)

            def times_mask(n, qc):
                dve.wait_ge(*S['scores_ready'].when(t, n, qc))
                nc.vector.tensor_tensor(probs[:, n % PSLOTS, qc, :], ps[:, qc, :], A.mask[:, qc, :], ALU.mult)\
                    .then_inc(*S['scores_taken'].reach(t, n, qc))

            for n in range(A.heads + LAG):
                m = n - LAG
                if n < A.heads:
                    slot_free(n)
                if A.shared:
                    for qc in range(C):
                        if n < A.heads:
                            add_max(n, qc)
                        if qc == 1 and 0 < n <= A.heads:
                            inverse(n - 1)
                        if m >= 0 and A.owner[qc] == 'd':
                            dve.wait_ge(*tile_ready.when('pT', t, m, qc))
                            if m >= 4:
                                dve.wait_ge(*S['context_ready'].when(t, m // 4 - 1))
                            nc.vector.tensor_copy(pT[:, m % 4, qc, :], ps[:, ring.bank('pT', t, m, qc), :])\
                                .then_inc(*dve_emptied.reach('pT', t, m, qc))
                else:
                    for step in ('m0', 'm1', 'a0', 'i', 'm2', 'a1', 'm3', 'a2', 'a3'):
                        if step == 'i' and 0 < n <= A.heads:
                            inverse(n - 1)
                        if step[0] == 'm' and n < A.heads:
                            times_mask(n, int(step[1]))
                        if step[0] == 'a' and n < A.heads:
                            add_max(n, int(step[1]))
            dve.wait_ge(*pool_done.when('biased', t, C - 1))
            for tc in range(C):
                dve.wait_ge(*tile_ready.when('out', t, tc))
                nc.vector.tensor_tensor(x[:, tc, :], ps[:, ring.bank('out', t, tc), :], x[:, tc, :], ALU.add)\
                    .then_inc(*dve_emptied.reach('out', t, tc))

        def pool_bias(pool, t, row, before):
            for tc in range(C):
                before(pool, tc)
                nc.gpsimd.tensor_tensor(x[:, tc, :], x[:, tc, :], rows[:, row, :], ALU.add)\
                    .then_inc(*pool_done.reach('biased', t, tc))

        def pool_attention(pool, A):
            t = A.tag
            if A.shared:
                pool_split(pool, A, 'k', 0)
            for g in range(4 if A.shared else 1):
                pool_split(pool, A, 'q', g)
            if not A.shared:
                pool_split(pool, A, 'k', 0)
            for n in range(1, A.heads + 1):
                g, i = divmod(n - 1, 4)
                if not A.shared and g + 1 < A.groups:
                    if i == 0:
                        pool_split(pool, A, 'q', g + 1)
                    if i == 1:
                        pool_split(pool, A, 'k', g + 1)
                pool.wait_ge(*S['inverse_done'].when(t, n - 1))
                for qc in range(C):
                    p = probs[:, (n - 1) % PSLOTS, qc, :]
                    nc.gpsimd.tensor_scalar(p, p, row_inv[:, (n - 1) % PSLOTS, qc:qc + 1], 1.0, ALU.mult, ALU.mult)\
                        .then_inc(*S['normalised'].reach(t, n - 1, qc))

        def pool_neg(pool, A):
            pool.wait_ge(sems['mask%d_in' % A.tag], 16)
            if A.tag == 2:
                pool.wait_ge(*dve_done.when('sm', 1, 15, C - 1))
            ins = None
            for qc in range(C):
                ins = nc.gpsimd.tensor_scalar(neg[:, qc, :], A.mask[:, qc, :], -1.0, 10000.0, ALU.add, ALU.mult)
            ins.then_inc(*pool_done.reach('neg', A.tag))

        MIXES = ('w', 'k', 'v', 'r', 'g')
        MIX_ROW = {'k': 0, 'w': 1, 'v': 2, 'r': 3, 'g': 4}
        MIX_AT = {'w': 3, 'k': 0, 'v': 1, 'r': 2, 'g': 3}

        def pe_rwkv(pe, l):
            pe_norm_turn(pe, f'a{l}', xn2)
            w_wait(pe, f'small_{l}')
            small = weights(f'small_{l}')
            for c in range(C):
                pe.wait_ge(*dve_done.when('xin', l, c))
            for part, (n0, rows_) in enumerate(((0, 128), (128, 32))):
                tile = take(pe, 'z', l, part)
                for fc in range(C):
                    m = nc.tensor.matmul(tile[0:rows_, :], small[:, SMALL_MAA + fc * 160 + n0:SMALL_MAA + fc * 160 + n0 + rows_],
                                         mix[:, 0, fc, :], start=(fc == 0), stop=(fc == C - 1))
                m.then_inc(*tile_ready.reach('z', l, part))
            w_wait(pe, f'maa2_{l}')
            maa2 = weights(f'maa2_{l}')
            for part in range(2):
                pe.wait_ge(*act_emptied.when('z', l, part))
            for name in MIXES:
                f = MIX_ROW[name]
                r, part = (32 * f, 0) if f < 4 else (0, 1)
                for c in range(C):
                    tile = take(pe, 'mix', l, name, c)
                    nc.tensor.matmul(tile, maa2[r:r + 32, part * H + c * P:part * H + (c + 1) * P], z[r:r + 32, part, :],
                                     start=True, stop=True).then_inc(*tile_ready.reach('mix', l, name, c))
                if name == 'w':
                    for c in range(C):
                        pe.wait_ge(*pool_done.when('mix', l, 'w', c))
                    tile = take(pe, 'td', l)
                    for fc in range(C):
                        m = nc.tensor.matmul(tile[0:64, :], small[:, SMALL_TD1 + fc * 64:SMALL_TD1 + (fc + 1) * 64],
                                             mix[:, MIX_AT['w'], fc, :], start=(fc == 0), stop=(fc == C - 1))
                    m.then_inc(*tile_ready.reach('td', l))
                    pe.wait_ge(*act_emptied.when('td', l))
                    for c in range(C):
                        tile = take(pe, 'decay', l, c)
                        nc.tensor.matmul(tile, small[0:64, SMALL_TD2 + c * P:SMALL_TD2 + (c + 1) * P], tdh[:, :],
                                         start=True, stop=True).then_inc(*tile_ready.reach('decay', l, c))

            def project(hg, names=('k', 'v', 'r')):
                for name in names:
                    if hg == 0:
                        w_wait(pe, f'{name}_{l}')
                        for c in range(C):
                            pe.wait_ge(*pool_done.when('mix', l, name, c))
                    to_T(pe, take(pe, f'{name}p', l, hg), weights(f'{name}_{l}'), mix[:, MIX_AT[name]], hg,
                         fin=tile_ready.reach(f'{name}p', l, hg))

            def bonus_sum(hg):
                pe.wait_ge(*dve_done.when('ruk', l, hg))
                tile = take(pe, 'bonus', l, hg)
                nc.tensor.matmul(tile, ones_block[:, :], ruk[:, hg % 2, :], start=True, stop=True)\
                    .then_inc(*tile_ready.reach('bonus', l, hg))

            def gate(c):
                if c == 0:
                    w_wait(pe, f'g_{l}')
                    for cc in range(C):
                        pe.wait_ge(*pool_done.when('mix', l, 'g', cc))
                to_T(pe, take(pe, 'gp', l, c), weights(f'g_{l}'), mix[:, MIX_AT['g']], c, fin=tile_ready.reach('gp', l, c))

            def reduce(t):
                hg, j = divmod(t, HS)
                jj, m = j % 4, j // 4
                if j == 0 and hg > 0:
                    pe.wait_ge(*act_done.when('rec', l, hg - 1))
                pe.wait_ge(*pool_done.when('prod', l, t))
                nc.tensor.matmul(ps[32 * jj:32 * jj + 32, OBANK, :], gather[:, m, :], prod[:, t % 3, :],
                                 start=(m == 0), stop=False, skip_group_check=True).then_inc(*S['reduced'].reach(l, t))
                if j == HS - 1:
                    pe.wait_ge(*dve_emptied.when('bonus', l, hg))
                    nc.tensor.matmul(ps[:, OBANK, :], permute[:, :], bonus[:, hg % 2, :], start=False, stop=True,
                                     skip_group_check=True).then_inc(*S['context_ready'].reach('rec', l, hg))

            project(0)
            bonus_sum(0)
            lag = 3
            for t in range(C * HS + lag):
                hg, j = divmod(t, HS)
                if t < C * HS:
                    if j == 0:
                        pe.wait_ge(*dve_done.when('vlo', l, hg))
                    if t >= 4:
                        pe.wait_ge(*S['scores_taken'].when('kv', l, t - 4))
                    nc.tensor.matmul(ps[:, t % 4, :], pick[:, j * P:(j + 1) * P], vhi[:, hg % 2, :], start=True, stop=False)
                    nc.tensor.matmul(ps[:, t % 4, :], pick[:, j * P:(j + 1) * P], vlo[:, hg % 2, :], start=False, stop=True)\
                        .then_inc(*S['vb_ready'].reach(l, t))
                    if j in (3, 6, 9) and hg + 1 < C:
                        project(hg + 1, {3: 'k', 6: 'v', 9: 'r'}[j])
                    if j == 14 and hg + 1 < C:
                        bonus_sum(hg + 1)
                    if hg == C - 1 and j % 4 == 1:
                        gate(j // 4)
                if t >= lag:
                    reduce(t - lag)
            def wait(pe, c, t):
                if c == 0:
                    pe.wait_ge(*act_done.when('rec', l, t))
            pe_turn(pe, l, recT, 'recN', wait, permute_back)

            def wait(pe, c, t):
                if c == 0:
                    pe.wait_ge(*dve_done.when('gn', l, t))
            pe_turn(pe, l, centred, 'gnT', wait)
            w_wait(pe, f'o_{l}')
            for c in range(C):
                pe.wait_ge(*dve_done.when('gated', l, c))
            for tc in range(C):
                to_N(pe, take(pe, 'wo', l, tc), weights(f'o_{l}'), gated, tc, fin=tile_ready.reach('wo', l, tc))
            pe_norm_turn(pe, f'f{l}', xn2)
            w_wait(pe, f'fk_{l}')
            for c in range(C):
                pe.wait_ge(*dve_done.when('xk2', l, c))
            for c in range(C):
                to_T(pe, take(pe, 'fk', l, c), weights(f'fk_{l}'), mix[:, 1], c, fin=tile_ready.reach('fk', l, c))
            w_wait(pe, f'fr_{l}')
            for c in range(C):
                pe.wait_ge(*dve_done.when('xr2', l, c))
            for tc in range(C):
                to_N(pe, take(pe, 'fr', l, tc), weights(f'fr_{l}'), mix[:, 2], tc, fin=tile_ready.reach('fr', l, tc))
            w_wait(pe, f'fv_{l}')
            for c in range(C):
                pe.wait_ge(*act_done.when('kk', l, c))
            for tc in range(C):
                to_N(pe, take(pe, 'fv', l, tc), weights(f'fv_{l}'), mix[:, 3], tc, fin=tile_ready.reach('fv', l, tc))

        def dve_rwkv(dve, l):
            dve_norm(dve, f'a{l}', None, xn2, l)

            def shift_mix(tag, mixes):
                for c in range(C):
                    dve.wait_ge(*act_emptied.when('lnT', tag, c))
                    if c == 0:
                        dve.wait_ge(*pool_done.when('prev', tag))
                    nc.vector.tensor_tensor(sx[:, c, :], xa[:, c, 0:L], xa[:, c, 1:L + 1], ALU.subtract)\
                        .then_inc(*dve_done.reach('sx', tag, c))
                for at_, name, out_label in mixes:
                    for c in range(C):
                        dve.wait_ge(*dve_done.when('sx', tag, c))
                        nc.vector.scalar_tensor_tensor(mix[:, at_, c, :], sx[:, c, :], col(f'{name}_{l}', c),
                                                       xa[:, c, 1:L + 1], ALU.mult, ALU.add)\
                            .then_inc(*dve_done.reach(out_label, l, c))

            shift_mix(f'a{l}', ((0, 'maa_x', 'xin'),))

            def mixed(name):
                for c in range(C):
                    dve.wait_ge(*tile_ready.when('mix', l, name, c))
                    if name == 'k':
                        dve.wait_ge(*tile_ready.when('z', l, 1))
                    if name == 'g':
                        dve.wait_ge(*tile_ready.when('td', l))
                    nc.vector.scalar_tensor_tensor(mix[:, MIX_AT[name], c, :], ps[:, ring.bank('mix', l, name, c), :],
                                                   col(f'maa_{name}_{l}', c), sx[:, c, :], ALU.add, ALU.mult)\
                        .then_inc(*dve_emptied.reach('mix', l, name, c))

            for name in MIXES:
                mixed(name)

            def heads_in(hg):
                s = hg % 2
                dve.wait_ge(*act_emptied.when('vp', l, hg))
                if hg >= 2:
                    dve.wait_ge(*S['vb_ready'].when(l, HS * (hg - 1) - 1))
                nc.vector.tensor_copy(vhi[:, s, :], vT[:, s, :]).then_inc(*dve_done.reach('vhi', l, hg))
                dve.wait_ge(*act_emptied.when('rp', l, hg))
                dve.wait_ge(*act_emptied.when('kp', l, hg))
                if hg >= 2:
                    dve.wait_ge(*tile_ready.when('bonus', l, hg - 2))
                nc.vector.scalar_tensor_tensor(ruk[:, s, :], rT[:, s, :], col(f'u_{l}', hg), kT[:, s, :], ALU.mult, ALU.mult)\
                    .then_inc(*dve_done.reach('ruk', l, hg))
                dve.wait_ge(*dve_done.when('vhi', l, hg))
                nc.vector.tensor_tensor(vlo[:, s, :], vT[:, s, :], vhi[:, s, :].bitcast(F32), ALU.subtract)\
                    .then_inc(*dve_done.reach('vlo', l, hg))

            def bonus_out(hg):
                s = hg % 2
                dve.wait_ge(*tile_ready.when('bonus', l, hg))
                if hg >= 2:
                    dve.wait_ge(*S['context_ready'].when('rec', l, hg - 2))
                nc.vector.tensor_tensor(bonus[:, s, :], ps[:, ring.bank('bonus', l, hg), :], vT[:, s, :], ALU.mult)\
                    .then_inc(*dve_emptied.reach('bonus', l, hg))

            heads_in(0)
            dve.wait_ge(*act_done.when('w', l, C - 1))
            dve.wait_ge(sems['s0_in'], 16)
            n = C * HS
            for t in range(n + 1):
                hg, j = divmod(t, HS)
                if t < n:
                    dve.wait_ge(*S['vb_ready'].when(l, t))
                    if t >= 3:
                        dve.wait_ge(*dve_done.when('scan', l, t - 3))
                    nc.vector.tensor_tensor(kvp[:, t % 3, :], kT[:, hg % 2, :], ps[:, t % 4, :], ALU.mult)\
                        .then_inc(*S['scores_taken'].reach('kv', l, t))
                if t >= 1:
                    u = t - 1
                    ug, uj = divmod(u, HS)
                    dve.wait_ge(*S['scores_taken'].when('kv', l, u))
                    if u >= 3:
                        dve.wait_ge(*pool_done.when('prod', l, u - 3))
                    nc.vector.tensor_tensor_scan(state[:, u % 3, 1:L + 1], decay[:, ug, :], kvp[:, u % 3, :],
                                                 s0[:, ug, uj:uj + 1], ALU.mult, ALU.add)\
                        .then_inc(*dve_done.reach('scan', l, u))
                if t < n and j == 1:
                    bonus_out(hg)
                if t < n and j == 12 and hg + 1 < C:
                    heads_in(hg + 1)
            def heads(ap):
                return ap.rearrange('p (h j) -> p h j', j=HS)

            def wide(ap):
                return ap.unsqueeze(2).to_broadcast([P, 32, HS])

            for tc in range(C):
                dve.wait_ge(*tile_ready.when('recN', l, tc))
                tile = ps[:, ring.bank('recN', l, tc), :]
                nc.vector.tensor_reduce(gsum[:, tc, :], heads(tile), AX.X, ALU.add).then_inc(*dve_done.reach('gsum', l, tc))
                dve.wait_ge(*dve_done.when('gsum', l, tc))
                nc.vector.scalar_tensor_tensor(heads(centred[:, tc, :]), wide(gsum[:, tc, :]), -1.0 / HS, heads(tile),
                                               ALU.mult, ALU.add)\
                    .then_inc(*dve_emptied.reach('recN', l, tc))
            for tc in range(C):
                dve.wait_ge(*act_done.when('gsq', l, tc))
                nc.vector.tensor_reduce(gsq[:, tc, :], heads(squared[:, tc, :]), AX.X, ALU.add)\
                    .then_inc(*dve_done.reach('gsq', l, tc))
            for tc in range(C):
                dve.wait_ge(*pool_done.when('ginv', l, tc))
                nc.vector.tensor_tensor(heads(centred[:, tc, :]), heads(centred[:, tc, :]), wide(ginv[:, tc, :]), ALU.mult)\
                    .then_inc(*dve_done.reach('gn', l, tc))
            for c in range(C):
                dve.wait_ge(*act_emptied.when('gnT', l, c))
                dve.wait_ge(*act_emptied.when('gp', l, c))
                nc.vector.tensor_tensor(gated[:, c, :], squared[:, c, :], gT[:, c, :], ALU.mult)\
                    .then_inc(*dve_done.reach('gated', l, c))
            for tc in range(C):
                dve.wait_ge(*tile_ready.when('wo', l, tc))
                nc.vector.tensor_tensor(x[:, tc, :], ps[:, ring.bank('wo', l, tc), :], x[:, tc, :], ALU.add)\
                    .then_inc(*dve_emptied.reach('wo', l, tc))
            dve_norm(dve, f'f{l}', lambda e, tc: e.wait_ge(*dve_emptied.when('wo', l, tc)), xn2, l)
            shift_mix(f'f{l}', ((1, 'ffn_k', 'xk2'), (2, 'ffn_r', 'xr2')))
            for tc in range(C):
                dve.wait_ge(*act_emptied.when('fr', l, tc))
                dve.wait_ge(*tile_ready.when('fv', l, tc))
                nc.vector.tensor_tensor(recT[:, tc, :], ps[:, ring.bank('fv', l, tc), :], gT[:, tc, :], ALU.mult)\
                    .then_inc(*dve_emptied.reach('fv', l, tc))
            for tc in range(C):
                dve.wait_ge(*dve_emptied.when('fv', l, tc))
                nc.vector.tensor_tensor(x[:, tc, :], x[:, tc, :], recT[:, tc, :], ALU.add)\
                    .then_inc(*dve_done.reach('x', l, tc))

        def act_rwkv(act, l):
            act_norm(act, f'a{l}', xa, f'ln1_w_{l}', f'ln1_b_{l}', shift=1)
            for part, rows_ in enumerate((128, 32)):
                act.wait_ge(*tile_ready.when('z', l, part))
                nc.scalar.activation(z[0:rows_, part, :], ps[0:rows_, ring.bank('z', l, part), :], ACT.Tanh)\
                    .then_inc(*act_emptied.reach('z', l, part))
            act.wait_ge(*tile_ready.when('td', l))
            nc.scalar.activation(tdh[:, :], ps[0:64, ring.bank('td', l), :], ACT.Tanh).then_inc(*act_emptied.reach('td', l))
            for c in range(C):
                act.wait_ge(*tile_ready.when('decay', l, c))
                nc.scalar.activation(decay[:, c, :], ps[:, ring.bank('decay', l, c), :], ACT.Exp, bias=col(f'decay_{l}', c))\
                    .then_inc(*act_emptied.reach('decay', l, c))
            for c in range(C):
                act.wait_ge(*act_emptied.when('decay', l, c))
                nc.scalar.activation(decay[:, c, :], decay[:, c, :], ACT.Exp, scale=-1.0).then_inc(*act_done.reach('w', l, c))

            def heads_in(hg, names=('k', 'v', 'r')):
                s = hg % 2
                for name in names:
                    out = {'k': kT, 'v': vT, 'r': rT}[name]
                    act.wait_ge(*tile_ready.when(f'{name}p', l, hg))
                    if hg >= 2:
                        act.wait_ge(*pool_done.when('prod', l, HS * (hg - 1) - 1))
                        act.wait_ge(*dve_emptied.when('bonus', l, hg - 2))
                    nc.scalar.activation(out[:, s, :], ps[:, ring.bank(f'{name}p', l, hg), :], ACT.Copy)\
                        .then_inc(*act_emptied.reach(f'{name}p', l, hg))

            heads_in(0)
            act.wait_ge(sems['s0_in'], 16)
            for t in range(C * HS):
                hg, j = divmod(t, HS)
                if t >= 3:
                    act.wait_ge(*pool_done.when('prod', l, t - 3))
                nc.scalar.activation(state[:, t % 3, 0:1], s0[:, hg, j:j + 1], ACT.Copy).then_inc(*act_done.reach('s0', l, t))
                if j in (3, 6, 9) and hg + 1 < C:
                    heads_in(hg + 1, {3: 'k', 6: 'v', 9: 'r'}[j])
                if j == 4 and hg > 0:
                    act.wait_ge(*S['context_ready'].when('rec', l, hg - 1))
                    nc.scalar.activation(recT[:, hg - 1, :], ps[:, OBANK, :], ACT.Copy).then_inc(*act_done.reach('rec', l, hg - 1))
                if hg == C - 1 and j % 4 == 2:
                    c = j // 4
                    act.wait_ge(*tile_ready.when('gp', l, c))
                    nc.scalar.activation(gT[:, c, :], ps[:, ring.bank('gp', l, c), :], ACT.Silu)\
                        .then_inc(*act_emptied.reach('gp', l, c))
            act.wait_ge(*S['context_ready'].when('rec', l, C - 1))
            nc.scalar.activation(recT[:, C - 1, :], ps[:, OBANK, :], ACT.Copy).then_inc(*act_done.reach('rec', l, C - 1))
            for tc in range(C):
                act.wait_ge(*dve_emptied.when('recN', l, tc))
                nc.scalar.activation(squared[:, tc, :], centred[:, tc, :], ACT.Square).then_inc(*act_done.reach('gsq', l, tc))
            for c in range(C):
                act.wait_ge(*tile_ready.when('gnT', l, c))
                if c == 0:
                    act.wait_ge(*dve_done.when('gsq', l, C - 1))
                nc.scalar.activation(squared[:, c, :], ps[:, ring.bank('gnT', l, c), :], ACT.Identity,
                                     bias=col(f'gn_b_{l}', c), scale=col(f'gn_w_{l}', c))\
                    .then_inc(*act_emptied.reach('gnT', l, c))
            act_norm(act, f'f{l}', xa, f'ln2_w_{l}', f'ln2_b_{l}', shift=1)
            for c in range(C):
                act.wait_ge(*tile_ready.when('fk', l, c))
                nc.scalar.activation(mix[:, 3, c, :], ps[:, ring.bank('fk', l, c), :], ACT.Relu)\
                    .then_inc(*act_emptied.reach('fk', l, c))
                act.wait_ge(*act_emptied.when('fk', l, c))
                nc.scalar.activation(mix[:, 3, c, :], mix[:, 3, c, :], ACT.Square).then_inc(*act_done.reach('kk', l, c))
            for tc in range(C):
                act.wait_ge(*tile_ready.when('fr', l, tc))
                nc.scalar.activation(gT[:, tc, :], ps[:, ring.bank('fr', l, tc), :], ACT.Sigmoid)\
                    .then_inc(*act_emptied.reach('fr', l, tc))

        def pool_rwkv(pool, l):
            def previous(tag, token, before):
                before(pool)
                nc.gpsimd.tensor_copy(xa[:, :, 0:1], ctxT[:, :, token:token + 1]).then_inc(*pool_done.reach('prev', tag))

            previous(f'a{l}', 1, lambda e: e.wait_ge(*dve_done.when('moments', f'a{l}', C - 1)))
            pool_norm(pool, f'a{l}', 1e-5)
            for name in MIXES:
                for c in range(C):
                    pool.wait_ge(*dve_emptied.when('mix', l, name, c))
                    m = mix[:, MIX_AT[name], c, :]
                    nc.gpsimd.tensor_tensor(m, m, xa[:, c, 1:L + 1], ALU.add).then_inc(*pool_done.reach('mix', l, name, c))
            for t in range(C * HS):
                hg, j = divmod(t, HS)
                pool.wait_ge(*dve_done.when('scan', l, t))
                pool.wait_ge(*act_done.when('s0', l, t))
                if t >= 3:
                    pool.wait_ge(*S['reduced'].when(l, t - 3))
                nc.gpsimd.tensor_tensor(prod[:, t % 3, :], state[:, t % 3, 0:L], rT[:, hg % 2, :], ALU.mult)\
                    .then_inc(*pool_done.reach('prod', l, t))
            for tc in range(C):
                pool.wait_ge(*dve_done.when('gsq', l, tc))
                nc.gpsimd.tensor_scalar(gsq[:, tc, :], gsq[:, tc, :], 1.0 / HS, 1e-5, ALU.mult, ALU.add)\
                    .then_inc(*pool_done.reach('gvar', l, tc))
                pool.wait_ge(*pool_done.when('gvar', l, tc))
                nc.gpsimd.tensor_tensor(ginv[:, tc, :], gsq[:, tc, :], minus_half[:, 0:32], ALU.pow)\
                    .then_inc(*pool_done.reach('ginv', l, tc))
            previous(f'f{l}', 0, lambda e: e.wait_ge(*dve_done.when('moments', f'f{l}', C - 1)))
            pool_norm(pool, f'f{l}', 1e-5)

        with nc.Fori(0, samples) as b:
            with nc.Block() as block:
                @block.gpsimd
                def _(pool):
                    for s in sems.values():
                        nc.gpsimd.sem_clear(s)

            with nc.Block() as block:
                @block.tensor
                def _(pe):
                    pe_attention(pe, A0)
                    pe_norm_turn(pe, 'ln1', xn)
                    pe_attention(pe, A1)
                    pe_norm_turn(pe, 'ln2', xn)
                    pe_attention(pe, A2)
                    pe_norm_turn(pe, 'ln3', xn)
                    for c in range(C):
                        pe.wait_ge(*act_emptied.when('lnT', 'ln3', c))

                    def up(i):
                        w_wait(pe, f'up_{i}')
                        for c in range(C):
                            to_T(pe, take(pe, 'up', i, c), weights(f'up_{i}'), srcT, c, fin=tile_ready.reach('up', i, c))

                    def down(i):
                        w_wait(pe, f'down_{i}')
                        for c in range(C):
                            pe.wait_ge(*act_emptied.when('up', i, c))
                        for tc in range(C):
                            for fc in range(C):
                                m = nc.tensor.matmul(ps[:, tc, :], hidden[:, i % 2, fc, tc * P:(tc + 1) * P],
                                                     weights(f'down_{i}')[:, fc * H:(fc + 1) * H],
                                                     start=(i == 0 and fc == 0), stop=(i == FFN - 1 and fc == C - 1))
                        m.then_inc(*S['mlp_ready'].reach(f'down_{i}'))

                    up(0)
                    for i in range(1, FFN):
                        up(i)
                        down(i - 1)
                    down(FFN - 1)
                    for l in (2, 3):
                        pe_rwkv(pe, l)

                @block.scalar
                def _(act):
                    act_attention(act, A0)
                    act_norm(act, 'ln1', srcT, 'ln1_s', 'ln1_b')
                    act_attention(act, A1)
                    act_norm(act, 'ln2', srcT, 'ln2_s', 'ln2_b')
                    act_attention(act, A2)
                    act_norm(act, 'ln3', srcT, 'ln3_s', 'ln3_b')
                    for i in range(FFN):
                        for c in range(C):
                            act.wait_ge(*tile_ready.when('up', i, c))
                            if i >= 2:
                                act.wait_ge(*S['mlp_ready'].when(f'down_{i - 2}'))
                            nc.scalar.activation(hidden[:, i % 2, c, :], ps[:, ring.bank('up', i, c), :],
                                                 ACT.Gelu_apprx_tanh, bias=col(f'b1_{i}', c))\
                                .then_inc(*act_emptied.reach('up', i, c))
                    for l in (2, 3):
                        act_rwkv(act, l)

                @block.vector
                def _(dve):
                    dve_attention(dve, A0)
                    dve_norm(dve, 'ln0', lambda e, tc: e.wait_ge(*dve_emptied.when('out', 0, tc)), xn, 0)
                    for tc in range(C):
                        dve.wait_ge(*dve_done.when('xn', 'ln0', tc))
                        nc.vector.tensor_tensor(xn[:, tc, :], xn[:, tc, :], rows[:, 2, :], ALU.mult)\
                            .then_inc(*dve_done.reach('gamma', tc))
                    for tc in range(C):
                        dve.wait_ge(*dve_done.when('gamma', tc))
                        nc.vector.tensor_tensor(x[:, tc, :], xn[:, tc, :], rows[:, 3, :], ALU.add)\
                            .then_inc(*dve_done.reach('x', 0, tc))
                    dve_norm(dve, 'ln1', lambda e, tc: e.wait_ge(*dve_done.when('x', 0, tc)), xn, 1)
                    dve_attention(dve, A1)
                    dve_norm(dve, 'ln2', lambda e, tc: e.wait_ge(*dve_emptied.when('out', 1, tc)), xn, 2)
                    dve_attention(dve, A2)
                    dve_norm(dve, 'ln3', lambda e, tc: e.wait_ge(*dve_emptied.when('out', 2, tc)), xn, 3)
                    dve.wait_ge(*S['mlp_ready'].when(f'down_{FFN - 1}'))
                    dve.wait_ge(*pool_done.when('biased', 'mlp', C - 1))
                    for tc in range(C):
                        nc.vector.tensor_tensor(x[:, tc, :], ps[:, tc, :], x[:, tc, :], ALU.add)\
                            .then_inc(*dve_done.reach('x', 1, tc))
                    for tc in range(C):
                        dve.wait_ge(*dve_done.when('x', 1, tc))
                    nc.vector.tensor_copy(pick[:, :].rearrange('p (j h i) -> p j h i', j=HS, h=HEADS),
                                          ident[:, :].rearrange('p (h j) -> p j h', h=HEADS).unsqueeze(3)
                                          .to_broadcast([P, HS, HEADS, HS])).then_inc(*dve_done.reach('pick'))
                    dve.wait_ge(*dve_done.when('pick'))
                    dve_rwkv(dve, 2)
                    for tc in range(C):
                        dve.wait_ge(*dve_done.when('x', 2, tc))
                    dve_rwkv(dve, 3)

                @block.gpsimd
                def _(pool):
                    nc.gpsimd.memset(v0[:, :, :, :], 0.0).then_inc(*pool_done.reach('v0', 'clear'))
                    pool.wait_ge(sems['x_in'], 16)
                    pool.wait_ge(sems['rows_in'], 16)
                    pool_bias(pool, 0, A0.rowbo, lambda e, tc: None)
                    pool_attention(pool, A0)
                    pool_norm(pool, 'ln0', 1e-6)
                    pool_neg(pool, A1)
                    pool_norm(pool, 'ln1', 1e-5)
                    pool.wait_ge(sems['rows_in'], 32)
                    pool_bias(pool, 1, A1.rowbo, lambda e, tc: e.wait_ge(*dve_done.when('xn', 'ln1', tc)))
                    pool_attention(pool, A1)
                    pool_norm(pool, 'ln2', 1e-5)
                    pool_neg(pool, A2)
                    pool_bias(pool, 2, A2.rowbo, lambda e, tc: e.wait_ge(*dve_done.when('xn', 'ln2', tc)))
                    pool_attention(pool, A2)
                    pool_norm(pool, 'ln3', 1e-5)
                    pool.wait_ge(sems['rows_in'], 48)
                    pool_bias(pool, 'mlp', 0, lambda e, tc: e.wait_ge(*dve_done.when('xn', 'ln3', tc)))
                    for l in (2, 3):
                        pool_rwkv(pool, l)

                @block.sync
                def _(sp):
                    def load(dst, src, name):
                        sp.dma_start(dst, src).then_inc(sems[name], 16)

                    load(ctxT[:, :, :], a['ctxT'][b].rearrange('(c p) t -> p c t', p=P), 'ctx_in')
                    load_weights(sp, 'kv0', freed)
                    load(srcT[:, :, :], a['xT'][b].rearrange('(c p) t -> p c t', p=P), 'xT_in')
                    load_weights(sp, 'q0', freed)
                    load(rows[:, 0:4, :], a['rows0'].unsqueeze(0).to_broadcast([P, 4, H]), 'rows_in')
                    load(maskA[:, :, :], a['mask0'][b].rearrange('(c p) t -> p c t', p=P), 'mask0_in')
                    load(x[:, :, :], a['x'][b].rearrange('(c p) t -> p c t', p=P), 'x_in')
                    load(maskB[:, :, :], a['mask1'].rearrange('(c p) t -> p c t', p=P), 'mask1_in')
                    load_weights(sp, 'o0', freed)
                    for g in range(A0.groups):
                        sp_stack(sp, A0, g)
                        if g == 0:
                            load_weights(sp, 'q1', freed)
                    sp.wait_ge(*dve_done.when('x', 0, C - 1))
                    load(rows[:, :, :], a['rows1'][0:NROWS].unsqueeze(0).to_broadcast([P, NROWS, H]), 'rows_in')
                    load(maskA[:, :, :], a['mask2'][b].rearrange('(c p) t -> p c t', p=P), 'mask2_in')
                    load_weights(sp, 'k1', freed)
                    for A in (A1, A2):
                        if A is A2:
                            load(rows[:, 0, :], a['rows1'][NROWS:].to_broadcast([P, H]), 'rows_in')
                        for g in range(A.groups):
                            sp_stack(sp, A, g)
                            if g == 0:
                                load_weights(sp, f'o{A.tag}', freed)
                        if A.tag == 1:
                            load_weights(sp, 'k2', freed)
                    load_weights(sp, 'down_3', freed)
                    sp.wait_ge(*dve_done.when('x', 1, C - 1))
                    load(s0[:, :, :], a['ctx'][b, 2:2 + HS, :].rearrange('(c r) (q j) -> (r q) c j', c=C, j=HS), 's0_in')
                    for l in (2, 3):
                        load_weights(sp, f'fv_{l}', freed)
                    fin = dve_done.when('x', 3, C - 1)
                    sp.wait_ge(*fin)
                    sp.dma_start(a['out'][b].rearrange('(c p) t -> p c t', p=P), x[:, :, :]).then_inc(sems['out_done'], 16)
                    sp.wait_ge(sems['out_done'], 16)

    out = {n: s.marks for n, s in sig.items()}
    out['ring'] = {label: n for n, label in enumerate(ring.labels)}
    return out


def _block(w):
    import numpy as np
    n = w.shape[1]
    out = np.zeros((P, C * H), np.float32)
    out[:, :C * n] = w.reshape(C, P, n).transpose(1, 0, 2).reshape(P, C * n)
    return out


def _arrays(v):
    import numpy as np
    x, ctx = v['x'], v['ctx_2048']
    d = {'x': x, 'xT': x.transpose(0, 2, 1), 'ctx': ctx, 'ctxT': ctx.transpose(0, 2, 1),
         'mask0': v['mask_Bx1xSxS2_ff0'].reshape(B, L, L), 'mask1': v['mask_1x1xSxS2_fc1'].reshape(L, L),
         'mask2': v['mask_Bx1xSxS2_ff1'].reshape(B, L, L)}
    g = lambda n: v['L0_xattn_' + n]
    blk = {'kv0': _block(np.concatenate([g('Wk'), g('Wv'), np.zeros((H, 256), np.float32)], 1)),
           'q0': _block(g('Wq').reshape(H, 8, 4, 16).transpose(0, 2, 1, 3).reshape(H, H)),
           'o0': _block(g('Wo').reshape(4, 2, 4, 16, H).transpose(0, 2, 1, 3, 4).reshape(H, H))}
    vec = {'bq0': g('bq').reshape(8, 4, 16).transpose(1, 0, 2).reshape(H), 'bk0': np.pad(g('bk'), (0, 384))}
    r0 = [np.pad(g('bv'), (0, 384)), g('bo'), g('gamma'), g('beta')]
    g = lambda n: v['L1_xattn_' + n]
    q, k, w = np.split(g('w_qkv'), 3, 1)
    k2, w2 = np.split(g('w_kv'), 2, 1)
    blk |= {'q1': _block(q), 'k1': _block(k), 'v1': _block(w), 'o1': _block(g('w_ao')), 'q2': _block(g('w_q')),
            'k2': _block(k2), 'v2': _block(w2), 'o2': _block(g('w_co'))}
    b, b2 = g('b_qkv'), g('b_kv')
    vec |= {'ln1_s': g('ln1_s'), 'ln1_b': g('ln1_b'), 'bq1': b[:H], 'bk1': b[H:2 * H], 'ln2_s': g('ln2_s'),
            'ln2_b': g('ln2_b'), 'bq2': g('b_q'), 'bk2': b2[:H], 'ln3_s': g('ln3_s'), 'ln3_b': g('ln3_b')}
    r1 = [b[2 * H:], g('b_ao'), b2[H:], g('b_co'), g('b2')]
    for i in range(FFN):
        s = slice(i * H, (i + 1) * H)
        blk |= {f'up_{i}': _block(g('w1')[:, s]), f'down_{i}': _block(g('w2')[s])}
        vec[f'b1_{i}'] = g('b1')[s]
    for l in (2, 3):
        g = lambda n: v[f'L{l}_xattn_' + n]
        td, u = ('td', 'u') if l == 2 else ('decay', 'faaaa')
        wf = {c: g(f'Wf{c}') if l == 2 else g(f'ffn_W{c}') for c in 'krv'}
        small = _block(g('maa_w1'))
        small[:, SMALL_TD1:SMALL_TD2] = _block(g(f'{td}_w1'))[:, :SMALL_TD2 - SMALL_TD1]
        small[:64, SMALL_TD2:SMALL_TD2 + H] = g(f'{td}_w2')
        maa2 = np.zeros((P, C * H), np.float32)
        maa2[:, :H] = g('maa_w2')[:4].reshape(P, H)
        maa2[:32, H:2 * H] = g('maa_w2')[4]
        blk |= {f'small_{l}': small, f'maa2_{l}': maa2}
        for n, w in (('k', g('Wk')), ('r', g('Wr')), ('v', g('Wv')), ('g', g('Wg')), ('o', g('Wo')),
                     ('fk', wf['k']), ('fr', wf['r']), ('fv', wf['v'])):
            blk[f'{n}_{l}'] = _block(w.T)
        ms = g('maa_stack').reshape(5, H)
        vec |= {f'{n}_{l}': g(n) for n in ('ln1_w', 'ln1_b', 'ln2_w', 'ln2_b', 'maa_x', 'gn_w', 'gn_b')}
        vec |= {f'maa_{n}_{l}': ms[i] for i, n in enumerate('kwvrg')}
        vec |= {f'decay_{l}': g('time_decay'), f'u_{l}': g(u).reshape(H), f'ffn_k_{l}': g('ffn_maa_k'),
                f'ffn_r_{l}': g('ffn_maa_r')}
    d['blocks'] = np.stack([blk[n] for n in BLOCKS])
    d['cols'] = np.stack([vec[n] for n in VECTORS]).reshape(len(VECTORS), C, P).transpose(2, 0, 1).reshape(P, -1)
    d['rows0'], d['rows1'] = np.stack(r0), np.stack(r1)
    d['ident'] = np.eye(P, dtype=np.float32)
    d['ones_block'] = np.kron(np.eye(HEADS), np.ones((HS, HS))).astype(np.float32)
    perm, gather = np.zeros((P, P), np.float32), np.zeros((P, 4, 32), np.float32)
    for h in range(HEADS):
        for j in range(HS):
            m, jj = divmod(j, 4)
            perm[h * HS + j, 32 * jj + 4 * h + m] = 1
        for m in range(4):
            gather[h * HS:(h + 1) * HS, m, 4 * h + m] = 1
    d['permute'], d['permute_back'], d['gather'] = perm, perm.T, gather
    return {n: np.ascontiguousarray(w, dtype=np.float32) for n, w in d.items()}


def kernel(**inputs):
    import numpy as np
    import concourse.bacc as bacc
    from concourse.bass_utils import run_bass_kernel_spmd
    arrays = _arrays({n: np.asarray(w) for n, w in inputs.items()})
    known = None
    for _ in range(2):
        nc = bacc.Bacc("TRN2", target_bir_lowering=False, num_devices=1)
        a = {n: nc.dram_tensor(f"in_{n}_dram", w.shape, F32, kind="ExternalInput").ap() for n, w in arrays.items()}
        a['out'] = nc.dram_tensor("out_dram", (B, L, H), F32, kind="ExternalOutput").ap()
        known = build(nc, a, known)
    r = run_bass_kernel_spmd(nc, [{f"in_{n}_dram": w for n, w in arrays.items()}], core_ids=[0])
    return r.results[0]["out_dram"]
```

```python
from contextlib import ExitStack

import concourse.bass as bass
from concourse import mybir

F32 = mybir.dt.float32
F32R = mybir.dt.float32r
ALU = mybir.AluOpType
ACT = mybir.ActivationFunctionType
AX = mybir.AxisListType

P = 128
B, L, H = 4, 512, 512
C = H // P
FFN = 4
WSLOTS = 3
RING = 3
RING0 = 4
OBANK = 7
LAG = 2
PSLOTS = LAG + 1

VECTORS = ['bq0', 'bk0', 'ln1_s', 'ln1_b', 'bq1', 'bk1', 'ln2_s', 'ln2_b', 'bq2', 'bk2', 'ln3_s', 'ln3_b',
           'b1_0', 'b1_1', 'b1_2', 'b1_3']
RWKV_VECTORS = ['ln1_w', 'ln1_b', 'ln2_w', 'ln2_b', 'maa_x', 'maa_k', 'maa_w', 'maa_v', 'maa_r', 'maa_g',
                'decay', 'u', 'gn_w', 'gn_b', 'ffn_k', 'ffn_r']
for _layer in (2, 3):
    VECTORS += [f'{n}_{_layer}' for n in RWKV_VECTORS]
COL = {n: C * k for k, n in enumerate(VECTORS)}
ROWS = {0: ['bv', 'bo', 'gamma', 'beta'], 1: ['bv', 'b_ao', 'bv2', 'b_co', 'b2']}
NROWS = 4

BLOCKS = ['kv0', 'q0', 'o0', 'q1', 'k1', 'v1', 'o1', 'k2', 'v2', 'q2', 'o2',
          'up_0', 'up_1', 'down_0', 'up_2', 'down_1', 'up_3', 'down_2', 'down_3']
for _layer in (2, 3):
    BLOCKS += [f'{n}_{_layer}' for n in ('small', 'k', 'v', 'r', 'g', 'o', 'fk', 'fr', 'fv')]
SMALL_MAA, SMALL_TD1, SMALL_TD2 = 0, C * 160, C * 224

HEADS = 8
HS = 16


class Signal:

    def __init__(self, sem, known):
        self.sem, self.count, self.known, self.marks = sem, 0, known, {}

    def reach(self, *label):
        self.count += 1
        assert label not in self.marks, label
        self.marks[label] = self.count
        return self.sem, 1

    def when(self, *label):
        return self.sem, (self.known[label] if self.known is not None else 1)


class Ring:

    def __init__(self, known):
        self.labels, self.known = [], known

    def take(self, *label):
        self.labels.append(label)
        n = len(self.labels) - 1
        return RING0 + n % RING, self.labels[n - RING] if n >= RING else None

    def bank(self, *label):
        return RING0 + (self.known[label] if self.known is not None else 0) % RING


SIGNALS = ['tile_ready', 'scores_ready', 'context_ready', 'mlp_ready', 'vb_ready', 'reduced',
           'act_emptied', 'dve_emptied', 'exp_done', 'act_done', 'scores_taken', 'dve_done', 'inverse_done',
           'pool_done', 'normalised']
LOADS = ['x_in', 'xT_in', 'ctx_in', 'rows_in', 'mask0_in', 'mask1_in', 'mask2_in', 's0_in', 'mixers_in', 'stack0', 'stack1', 'x_stored']


def build(nc, a, known, samples=B):
    base = -(-nc.sbuf_base // 32) * 32
    top = nc.sbuf_usable_end

    def place(name, shape, offset, dt=F32):
        n = 1
        for s in shape[1:]:
            n *= s
        assert base + offset + 4 * n <= top, (name, offset + 4 * n)
        return nc.alloc_sbuf_tensor_at(name, shape, dt, offset=base + offset), offset + -(-4 * n // 32) * 32

    at = 0
    x, at = place('x', [P, C, H], at)
    ctxT, at = place('ctxT', [P, C, L], at)
    wring, at = place('wring', [P, WSLOTS, C * H], at)
    maskA, at = place('maskA', [P, C, L], at)
    maskB, at = place('maskB', [P, C, L], at)
    neg, at = place('neg', [P, C, L], at)
    khi0, _ = place('khi0', [P, L], at - 4 * C * L, F32R)
    klo0, _ = place('klo0', [P, L], at - 4 * (C - 1) * L, F32R)
    cols, at = place('cols', [P, C * len(VECTORS)], at)
    scaled, at = place('scaled', [P, 3 * C], at)
    ident, at = place('ident', [P, P], at)
    ones_block, at = place('ones_block', [P, P], at)
    permute, at = place('permute', [P, P], at)
    permute_back, at = place('permute_back', [P, P], at)
    gather, at = place('gather', [P, 4, 32], at)
    stats, at = place('stats', [P, C, 6], at)
    moments, at = place('moments', [P, C, 2], at)
    rstd, at = place('rstd', [P, C], at)
    varep, at = place('varep', [P, C], at)
    minus_half, at = place('minus_half', [P, 32], at)
    top_common = at
    rows, at = place('rows', [P, NROWS, H], at)
    srcT, at = place('srcT', [P, C, L], at)
    v1, at = place('v1', [P, C, H], at)
    v0, _ = place('v0', [P, C, 8, 32], at - 8192)
    oT, at = place('oT', [P, C, L], at)
    probs, at = place('probs', [P, PSLOTS, C, L], at)
    xn, _ = place('xn', [P, C, H], at - 4 * PSLOTS * C * L)
    pT, at = place('pT', [P, 4, C, L], at)
    hidden, _ = place('hidden', [P, C, L], at - 4 * (4 + PSLOTS - 1) * C * L)
    hidden_hi, _ = place('hidden_hi', [P, 2, C, L], at - 4 * 4 * C * L, F32R)
    hidden_lo, _ = place('hidden_lo', [P, 2, C, L], at - 4 * 2 * C * L, F32R)
    mlp_w, _ = place('mlp_w', [P, 2, 2, C * H], at, F32R)
    qstack, at = place('qstack', [96, 2, 4, L], at, F32R)
    kstack, at = place('kstack', [96, 2, 4, L], at, F32R)
    split, at = place('split', [P, 2, L], at)
    hi, at = place('hi', [P, 4, L], at, F32R)
    lo, at = place('lo', [P, 4, L], at, F32R)
    row_max, at = place('row_max', [P, PSLOTS, C], at)
    row_sum, at = place('row_sum', [P, PSLOTS, C], at)
    row_inv, at = place('row_inv', [P, PSLOTS, C], at)
    at = top_common
    xa, at = place('xa', [P, C, L + 1], at)
    sx, at = place('sx', [P, C, L], at)
    mix, at = place('mix', [P, 4, C, L], at)
    xn2, _ = place('xn2', [P, C, H], at - 16 * C * L)
    centred, _ = place('centred', [P, C, H], at - 16 * C * L)
    squared, _ = place('squared', [P, C, H], at - 12 * C * L)
    ffn_w, _ = place('ffn_w', [P, 2, 2, C * H], at, F32R)
    act_hi, _ = place('act_hi', [P, 3, C, L], at + 4 * 4 * C * H, F32R)
    act_lo, _ = place('act_lo', [P, 4, C, L], at - 16 * C * L, F32R)
    decay, at = place('decay', [P, C, L], at)
    z, at = place('z', [P, 2, L], at)
    tdh, at = place('tdh', [64, L], at)
    kT, at = place('kT', [P, 2, L], at)
    rT, at = place('rT', [P, 2, L], at)
    vT, at = place('vT', [P, 2, L], at)
    vhi, at = place('vhi', [P, 2, L], at, F32R)
    vlo, at = place('vlo', [P, 2, L], at, F32R)
    ruk, at = place('ruk', [P, 2, L], at)
    bonus, at = place('bonus', [P, 2, L], at)
    kvp, at = place('kvp', [P, 3, L], at)
    state, at = place('state', [P, 3, L + 1], at)
    prod, at = place('prod', [P, 3, L], at)
    recT, at = place('recT', [P, C, L], at)
    gT, at = place('gT', [P, C, L], at)
    pick, at = place('pick', [P, HS * P], at, F32R)
    mixers, at = place('mixers', [P, 2 * H], at)
    s0, at = place('s0', [P, C, HS], at)
    gsum, at = place('gsum', [P, C, 32], at)
    gsq, at = place('gsq', [P, C, 32], at)
    ginv, at = place('ginv', [P, C, 32], at)

    with ExitStack() as stack:
        ps = stack.enter_context(nc.psum_tensor('ps', [P, 8, 512], F32))
        sems = {n: stack.enter_context(nc.semaphore(n)) for n in SIGNALS + LOADS + [f'w{i}' for i in range(WSLOTS)]}
        setup_in = stack.enter_context(nc.semaphore('setup_in'))
        sig = {n: Signal(sems[n], (known or {}).get(n)) for n in SIGNALS}
        ring = Ring((known or {}).get('ring'))
        S = sig
        tile_ready, act_emptied, dve_emptied = S['tile_ready'], S['act_emptied'], S['dve_emptied']
        act_done, dve_done, pool_done = S['act_done'], S['dve_done'], S['pool_done']

        def col(name, c):
            return cols[:, COL[name] + c:COL[name] + c + 1]

        with nc.Block() as block:
            @block.sync
            def _(sp):
                sp.dma_start(cols[:, :], a['cols']).then_inc(setup_in, 16)
                sp.dma_start(ident[:, :], a['ident']).then_inc(setup_in, 16)
                sp.dma_start(ones_block[:, :], a['ones_block']).then_inc(setup_in, 16)
                sp.dma_start(permute[:, :], a['permute']).then_inc(setup_in, 16)
                sp.dma_start(permute_back[:, :], a['permute_back']).then_inc(setup_in, 16)
                sp.dma_start(gather[:, :, :], a['gather']).then_inc(setup_in, 16)
                sp.wait_ge(setup_in, 16 * 6)

        with nc.Block() as block:
            @block.gpsimd
            def _(pool):
                pool.memset(minus_half[:, :], -0.5).then_inc(sems['x_stored'], 16)

            @block.vector
            def _(dve):
                for k, (n, s) in enumerate((('bq0', 0.25), ('bq1', 32.0 ** -0.5), ('bq2', 32.0 ** -0.5))):
                    dve.tensor_scalar(scaled[:, k * C:(k + 1) * C], cols[:, COL[n]:COL[n] + C], s, None, ALU.mult)

        def evac_wait(pe, label):
            if label in (act_emptied.known or {}):
                pe.wait_ge(*act_emptied.when(*label))
            else:
                pe.wait_ge(*dve_emptied.when(*label))

        def take(pe, *label):
            bank, before = ring.take(*label)
            if before is not None:
                evac_wait(pe, before)
            return ps[:, bank, :]

        uses = {b: n for n, b in enumerate(BLOCKS)}

        def weights(name):
            return wring[:, uses[name] % WSLOTS, :]

        def w_wait(pe, name):
            n = uses[name]
            pe.wait_ge(sems[f'w{n % WSLOTS}'], 16 * (n // WSLOTS + 1))

        loaded = [WSLOTS]

        def load_weights(sp, upto, freed):
            while loaded[0] <= uses[upto]:
                n = loaded[0]
                sp.wait_ge(*freed(BLOCKS[n - WSLOTS]))
                sp.dma_start(wring[:, n % WSLOTS, :], a['blocks'][n]).then_inc(sems[f'w{n % WSLOTS}'], 16)
                loaded[0] += 1

        LAST = {'kv0': ('v', 0, 3), 'q0': ('q', 0, 3), 'o0': ('out', 0, 3),
                'v1': ('v', 1, 3), 'q1': ('q', 1, 3), 'k1': ('k', 1, 3), 'o1': ('out', 1, 3),
                'v2': ('v', 2, 3), 'q2': ('q', 2, 3), 'k2': ('k', 2, 3), 'o2': ('out', 2, 3)}
        for i in range(FFN):
            LAST[f'up_{i}'] = ('up', i, 3)
        for l in (2, 3):
            LAST |= {f'small_{l}': ('decay', l, 3), f'k_{l}': ('kp', l, 3),
                     f'r_{l}': ('rp', l, 3), f'v_{l}': ('vp', l, 3), f'g_{l}': ('gp', l, 3), f'o_{l}': ('wo', l, 3),
                     f'fk_{l}': ('fk', l, 3), f'fr_{l}': ('fr', l, 3), f'fv_{l}': ('fv', l, 3)}

        MLP_ORDER = [n for n in BLOCKS if n.startswith(('up', 'down'))]
        SPLIT = {n: (mlp_w, k) for k, n in enumerate(MLP_ORDER)}
        for l in (2, 3):
            SPLIT |= {f'{n}_{l}': (ffn_w, k) for k, n in enumerate(('o', 'fk', 'fr', 'fv'))}

        def used(name):
            if name.startswith('down'):
                return S['mlp_ready'].when(name)
            return tile_ready.when(*LAST[name])

        def freed(name):
            return pool_done.when('wlo', name) if name in SPLIT else used(name)

        def w_parts(name):
            buf, k = SPLIT[name]
            return buf[:, k % 2, 0, :], buf[:, k % 2, 1, :]

        def act_w(act, name, *first):
            buf, k = SPLIT[name]
            w_wait(act, name)
            if k >= 2:
                order = MLP_ORDER if buf is mlp_w else [f'{n}_{name[-1]}' for n in ('o', 'fk', 'fr', 'fv')]
                act.wait_ge(*used(order[k - 2]))
            for w in first:
                act.wait_ge(*w)
            nc.scalar.activation(w_parts(name)[0], weights(name), ACT.Copy).then_inc(*act_done.reach('whi', name))

        def pool_w(pool, name):
            pool.wait_ge(*act_done.when('whi', name))
            high, low = w_parts(name)
            nc.gpsimd.tensor_tensor(low, weights(name), high.bitcast(F32), ALU.subtract).then_inc(*pool_done.reach('wlo', name))

        def parts_wait(pe, name):
            pe.wait_ge(*act_done.when('whi', name))
            pe.wait_ge(*pool_done.when('wlo', name))

        def three(w, src):
            return ((w[0], src[0]), (w[1], src[0]), (w[0], src[1]))

        def to_T3(pe, tile, name, src, oc, fin, ready=None):
            for fc in range(C):
                if ready is not None:
                    ready(fc)
                for k, (w, x_) in enumerate(three(w_parts(name), src)):
                    m = nc.tensor.matmul(tile, w[:, fc * H + oc * P:fc * H + (oc + 1) * P], x_[:, fc, :],
                                         start=(fc == 0 and k == 0), stop=(fc == C - 1 and k == 2))
            m.then_inc(*fin)

        def to_N3(pe, tile, name, src, tc, fin=None, ready=None, begins=True, ends=True):
            for fc in range(C):
                if ready is not None:
                    ready(fc)
                for k, (w, x_) in enumerate(three(w_parts(name), src)):
                    m = nc.tensor.matmul(tile, x_[:, fc, tc * P:(tc + 1) * P], w[:, fc * H:(fc + 1) * H],
                                         start=(begins and fc == 0 and k == 0), stop=(ends and fc == C - 1 and k == 2))
            if fin is not None:
                m.then_inc(*fin)
            return m

        def to_T(pe, tile, w, src, oc, base_=0, fin=None, fcs=range(C), ready=None):
            for fc in fcs:
                if ready is not None:
                    ready(fc)
                m = nc.tensor.matmul(tile, w[:, base_ + fc * H + oc * P:base_ + fc * H + (oc + 1) * P],
                                     src[:, fc, :], start=(fc == 0), stop=(fc == C - 1))
            if C - 1 in fcs:
                m.then_inc(*fin)

        def to_N(pe, tile, w, src, tc, n=H, base_=0, fin=None, ready=None):
            for fc in range(C):
                if ready is not None:
                    ready(fc)
                m = nc.tensor.matmul(tile[:, 0:n], src[:, fc, tc * P:(tc + 1) * P],
                                     w[:, fc * H + base_:fc * H + base_ + n], start=(fc == 0), stop=(fc == C - 1))
            m.then_inc(*fin)

        def dve_stats(dve, tag, tc):
            nc.vector.bn_stats(stats[:, tc, :], x[:, tc, :]).then_inc(*dve_done.reach('stats', tag, tc))
            dve.wait_ge(*dve_done.when('stats', tag, tc))
            nc.vector.bn_aggr(moments[:, tc, :], stats[:, tc, :]).then_inc(*dve_done.reach('moments', tag, tc))

        def dve_normalise(dve, tag, tc, out):
            dve.wait_ge(*pool_done.when('rstd', tag, tc))
            nc.vector.tensor_scalar(out[:, tc, :], x[:, tc, :], moments[:, tc, 0:1], rstd[:, tc:tc + 1],
                                    ALU.subtract, ALU.mult).then_inc(*dve_done.reach('xn', tag, tc))

        def dve_norm(dve, tag, out, before, after=None):
            for tc in range(C + 1):
                if tc < C:
                    before(tc)
                    dve_stats(dve, tag, tc)
                if tc > 0:
                    dve_normalise(dve, tag, tc - 1, out)
                    if after is not None:
                        after(tc - 1)

        def pool_norm(pool, tag, eps):
            for tc in range(C):
                pool.wait_ge(*dve_done.when('moments', tag, tc))
                nc.gpsimd.tensor_scalar(varep[:, tc:tc + 1], moments[:, tc, 1:2], 1.0, eps, ALU.mult, ALU.add)\
                    .then_inc(*pool_done.reach('varep', tag, tc))
                pool.wait_ge(*pool_done.when('varep', tag, tc))
                nc.gpsimd.tensor_tensor(rstd[:, tc:tc + 1], varep[:, tc:tc + 1], minus_half[:, 0:1], ALU.pow)\
                    .then_inc(*pool_done.reach('rstd', tag, tc))

        def pe_turn(pe, tag, src, what, wait, matrix=None):
            for c in range(C):
                tile = take(pe, what, tag, c)
                for t in range(C):
                    wait(pe, c, t)
                    m = nc.tensor.transpose(tile[:, t * P:(t + 1) * P], src[:, t, c * P:(c + 1) * P],
                                            (ident if matrix is None else matrix)[:, :])
                m.then_inc(*tile_ready.reach(what, tag, c))

        def pe_norm_turn(pe, tag, src):
            def wait(pe, c, t):
                if c == 0:
                    pe.wait_ge(*dve_done.when('xn', tag, t))
            pe_turn(pe, tag, src, 'lnT', wait)

        def act_norm(act, tag, out, wcol, bcol, shift=0, parts=False):
            for c in range(C):
                act.wait_ge(*tile_ready.when('lnT', tag, c))
                nc.scalar.activation(out[:, c, shift:shift + L], ps[:, ring.bank('lnT', tag, c), :], ACT.Identity,
                                     bias=col(bcol, c), scale=col(wcol, c)).then_inc(*act_emptied.reach('lnT', tag, c))
                if parts:
                    act.wait_ge(*act_emptied.when('lnT', tag, c))
                    nc.scalar.activation(hi[:, c, :], out[:, c, :], ACT.Copy).then_inc(*act_done.reach('srcT_hi', c))

        class Attention:
            def __init__(self, tag, hd, groups, vcols, vblk, voff, qblk, kblk, koff, src, oblk, bq, bk, scale, mask, rowbv, rowbo):
                self.tag, self.hd, self.groups, self.vcols = tag, hd, groups, vcols
                self.vblk, self.voff, self.qblk, self.kblk, self.koff = vblk, voff, qblk, kblk, koff
                self.src, self.oblk, self.bq, self.bk, self.scale, self.mask = src, oblk, bq, bk, scale, mask
                self.kt = 3 * hd
                self.rowbv, self.rowbo = rowbv, rowbo
                self.shared = groups == 8
                self.heads = 4 * groups
                self.owner = 'adad' if self.shared else 'aaaa'

            def qi(self, g):
                return g if self.shared else g % 2

            def ki(self, g):
                return 2 + g % 2

            def parts(self, kind, g):
                if kind == 'k' and self.shared:
                    return khi0[:, :], klo0[:, :]
                idx = self.qi(g) if kind == 'q' else self.ki(g)
                return hi[:, idx, :], lo[:, idx, :]

        cross_src = ctxT
        A0 = Attention(0, 16, 8, 128, 'kv0', 128, 'q0', 'kv0', 0, cross_src, 'o0', 0, 'bk0', 0.25, maskA, 0, 1)
        A1 = Attention(1, 32, 4, 512, 'v1', 0, 'q1', 'k1', 0, srcT, 'o1', 1, 'bk1', 32.0 ** -0.5, maskB, 0, 1)
        A2 = Attention(2, 32, 4, 512, 'v2', 0, 'q2', 'k2', 0, cross_src, 'o2', 2, 'bk2', 32.0 ** -0.5, maskA, 2, 3)

        def pe_q(pe, A, g, fcs=range(C), tile=None, ready=None):
            tile = take(pe, 'q', A.tag, g) if tile is None else tile
            to_T(pe, tile, weights(A.qblk), srcT, g, fcs=fcs, ready=ready, fin=tile_ready.reach('q', A.tag, g) if C - 1 in fcs else None)
            return tile

        def pe_k(pe, A, g, fcs=range(C), tile=None, ready=None):
            label = ('k', A.tag) if A.shared else ('k', A.tag, g)
            tile = take(pe, *label) if tile is None else tile
            to_T(pe, tile, weights(A.kblk), A.src, 0 if A.shared else g, base_=A.koff, fcs=fcs, ready=ready,
                 fin=tile_ready.reach(*label) if C - 1 in fcs else None)
            return tile

        def pe_values(pe, A, tiles=range(C)):
            w_wait(pe, A.vblk)
            for tc in tiles:
                to_N(pe, take(pe, 'v', A.tag, tc), weights(A.vblk), A.src, tc, n=A.vcols, base_=A.voff,
                     fin=tile_ready.reach('v', A.tag, tc))

        def pe_queries(pe, A):
            w_wait(pe, A.qblk)
            if A.tag == 0:
                pe.wait_ge(sems['xT_in'], 16)
            for g in range(4 if A.shared else 2):
                pe_q(pe, A, g, ready=(lambda fc: pe.wait_ge(*act_emptied.when('lnT', f'ln{A.tag}', fc))) if A.tag > 0 and g == 0 else None)

        def pe_attention(pe, A):
            t = A.tag
            if t == 0:
                w_wait(pe, A.kblk)
                pe.wait_ge(sems['ctx_in'], 16)
                pe_k(pe, A, 0)
                pe_queries(pe, A)
                pe_values(pe, A)
            if t == 1:
                pe_queries(pe, A)
                w_wait(pe, A.kblk)
                pe_k(pe, A, 0)
                pe_k(pe, A, 1)
                pe_values(pe, A)
            if t == 2:
                pe_queries(pe, A)
                pe_values(pe, A, (2, 3))
            part = None
            for n in range(A.heads + LAG + 1):
                g, i = divmod(n, 4)
                m = n - LAG
                mg, mi = divmod(m, 4)
                vg = mg - 1
                first, final = (vg % 2 == 0, vg % 2 == 1) if A.shared else (True, True)
                if n < A.heads and i == 0:
                    pe.wait_ge(sems[f'stack{g % 2}'], stack_total(A, g))
                for kc in range(C):
                    if n < A.heads:
                        if n >= 1:
                            pe.wait_ge(*S['scores_taken'].when(t, n - 1, kc))
                        nc.tensor.matmul(ps[:, kc, :], qstack[0:A.kt, g % 2, i, kc * P:(kc + 1) * P],
                                         kstack[0:A.kt, g % 2, 0 if A.shared else i, :], start=True, stop=True)\
                            .then_inc(*S['scores_ready'].reach(t, n, kc))
                    if m >= 0 and mi == 0 and vg >= 0:
                        if kc == 0:
                            if first and vg > 0:
                                pe.wait_ge(*act_done.when('context', t, (vg // 2 if A.shared else vg) - 1))
                            if vg == 0:
                                for tc in range(C):
                                    pe.wait_ge(*dve_emptied.when('v', t, tc))
                        for h in range(4):
                            evac_wait(pe, ('pT', t, 4 * vg + h, kc))
                        for h in range(4):
                            lhs = v0[:, kc, vg, :] if A.shared else v1[:, kc, (4 * vg + h) * 32:(4 * vg + h + 1) * 32]
                            ins = nc.tensor.matmul(ps[32 * h:32 * h + 32, OBANK, :], lhs, pT[:, h, kc, :],
                                                   start=(kc == 0 and first), stop=(kc == C - 1 and final))
                        ins.then_inc(*S['context_ready'].reach(t, vg, kc))
                    if 0 <= m < A.heads:
                        tile = take(pe, 'pT', t, m, kc)
                        for qc in range(C):
                            if kc == 0:
                                pe.wait_ge(*S['normalised'].when(t, m, qc))
                            ins = nc.tensor.transpose(tile[:, qc * P:(qc + 1) * P],
                                                      probs[:, m % PSLOTS, qc, kc * P:(kc + 1) * P], ident[:, :])
                        ins.then_inc(*tile_ready.reach('pT', t, m, kc))
                    if not A.shared and g + 2 < A.groups and kc < 2 and i < 2:
                        part = (pe_q, pe_k)[i](pe, A, g + 2, fcs=(2 * kc, 2 * kc + 1), tile=None if kc == 0 else part)
            w_wait(pe, A.oblk)
            for tc in range(C):
                to_N(pe, take(pe, 'out', t, tc), weights(A.oblk), oT, tc, fin=tile_ready.reach('out', t, tc),
                     ready=(lambda fc: pe.wait_ge(*act_done.when('context', t, fc))) if tc == 0 else None)

        nstack = {0: 6, 1: 24}
        stack_counts = {}

        def stack_total(A, g):
            return stack_counts[(A.tag, g)]

        totals = [0, 0]
        for A in (A0, A1, A2):
            for g in range(A.groups):
                totals[g % 2] += 16 * (6 if A.shared else 24)
                stack_counts[(A.tag, g)] = totals[g % 2]

        def sp_stack(sp, A, g):
            t, s = A.tag, sems[f'stack{g % 2}']

            def copy(out, in_):
                return sp.dma_start(out.bitcast(F32), in_.bitcast(F32))

            if g >= 2:
                sp.wait_ge(*S['scores_ready'].when(t, 4 * (g - 2) + 3, C - 1))
            elif t > 0:
                sp.wait_ge(*S['scores_ready'].when(t - 1, (31 if t == 1 else 15), C - 1))
            if A.shared:
                if g == 0:
                    for j in range(4):
                        sp.wait_ge(*pool_done.when('qlo', t, j))
                    sp.wait_ge(*pool_done.when('klo', t, 0))
            else:
                sp.wait_ge(*pool_done.when('qlo', t, g))
                sp.wait_ge(*pool_done.when('klo', t, g))
            for part, (q, k) in enumerate(((hi, hi), (lo, hi), (hi, lo))):
                r = part * A.hd
                if A.shared:
                    copy(qstack[r:r + 16, g % 2, :, :], q[16 * g:16 * g + 16, 0:4, :]).then_inc(s, 16)
                    copy(kstack[r:r + 16, g % 2, 0, :], (khi0 if k is hi else klo0)[16 * g:16 * g + 16, :]).then_inc(s, 16)
                else:
                    for i in range(4):
                        copy(qstack[r:r + 32, g % 2, i, :], q[32 * i:32 * i + 32, A.qi(g), :]).then_inc(s, 16)
                        copy(kstack[r:r + 32, g % 2, i, :], k[32 * i:32 * i + 32, A.ki(g), :]).then_inc(s, 16)

        def act_split(act, A, kind, g):
            t = A.tag
            label = ('k', t) if kind == 'k' and A.shared else (kind, t, g)
            act.wait_ge(*tile_ready.when(*label))
            prev = last_split.get(kind)
            if prev is not None:
                act.wait_ge(*pool_done.when(*prev))
            last_split[kind] = (f'{kind}lo', t, g)
            s = 0 if kind == 'q' else 1
            bias = scaled[:, t * C + g:t * C + g + 1] if kind == 'q' else col(A.bk, g)
            nc.scalar.activation(split[:, s, :], ps[:, ring.bank(*label), :], ACT.Identity, bias=bias,
                                 scale=A.scale if kind == 'q' else 1.0).then_inc(*act_emptied.reach(*label))
            if not A.shared and g >= 2:
                act.wait_ge(sems[f'stack{g % 2}'], stack_total(A, g - 2))
            act.wait_ge(*act_emptied.when(*label))
            nc.scalar.activation(A.parts(kind, g)[0], split[:, s, :], ACT.Copy).then_inc(*act_done.reach(f'{kind}hi', t, g))

        last_split = {}

        def pool_split(pool, A, kind, g):
            t, s = A.tag, 0 if kind == 'q' else 1
            high, low = A.parts(kind, g)
            pool.wait_ge(*act_done.when(f'{kind}hi', t, g))
            nc.gpsimd.tensor_tensor(low, split[:, s, :], high.bitcast(F32), ALU.subtract)\
                .then_inc(*pool_done.reach(f'{kind}lo', t, g))

        def act_attention(act, A):
            t = A.tag
            if t == 1:
                act.wait_ge(sems['stack0'], stack_total(A0, 6))
                act.wait_ge(sems['stack1'], stack_total(A0, 7))
            if A.shared:
                act_split(act, A, 'k', 0)
            for g in range(4 if A.shared else 2):
                act_split(act, A, 'q', g)
            if t == 1:
                act_split(act, A, 'k', 0)
                act_split(act, A, 'k', 1)

            def empty(m, kc):
                if A.owner[kc] != 'a':
                    return
                act.wait_ge(*tile_ready.when('pT', t, m, kc))
                if m >= 4:
                    act.wait_ge(*S['context_ready'].when(t, m // 4 - 1, kc))
                nc.scalar.activation(pT[:, m % 4, kc, :], ps[:, ring.bank('pT', t, m, kc), :], ACT.Copy)\
                    .then_inc(*act_emptied.reach('pT', t, m, kc))

            def exp(n, qc):
                act.wait_ge(*S['scores_taken'].when(t, n, qc) if A.shared else dve_done.when('sm', t, n, qc))
                p = probs[:, n % PSLOTS, qc, :]
                nc.scalar.activation(p, p, ACT.Exp, bias=row_max[:, n % PSLOTS, qc:qc + 1], scale=-1.0,
                                     accum_out=row_sum[:, n % PSLOTS, qc:qc + 1]).then_inc(*S['exp_done'].reach(t, n, qc))

            for n in range(A.heads + LAG + 1):
                g, i = divmod(n, 4)
                m = n - LAG
                if m >= 5 and (m - 1) % 4 == 0 and (not A.shared or (m // 4) % 2 == 0):
                    vg = m // 4 - 1
                    c = vg // 2 if A.shared else vg
                    act.wait_ge(*S['context_ready'].when(t, vg, C - 1))
                    nc.scalar.activation(oT[:, c, :], ps[:, OBANK, :], ACT.Copy).then_inc(*act_done.reach('context', t, c))
                for step in ('e0', 'e1', 'x0', 's', 'e2', 'x1', 'e3', 'x2', 'x3'):
                    if step == 's' and not A.shared and g + 2 < A.groups and i < 2:
                        act_split(act, A, 'qk'[i], g + 2)
                    if step[0] == 'e' and 0 <= m < A.heads:
                        empty(m, int(step[1]))
                    if step[0] == 'x' and n < A.heads:
                        exp(n, int(step[1]))
            c = C - 1
            act.wait_ge(*S['context_ready'].when(t, A.groups - 1, C - 1))
            nc.scalar.activation(oT[:, c, :], ps[:, OBANK, :], ACT.Copy).then_inc(*act_done.reach('context', t, c))

        def dve_values(dve, A, tiles):
            t = A.tag
            if t < 2:
                dve.wait_ge(sems['rows_in'], 16 * (t + 1))
            for tc in tiles:
                dve.wait_ge(*tile_ready.when('v', t, tc))
                tile = ps[:, ring.bank('v', t, tc), :]
                if A.shared:
                    if tc == 0:
                        dve.wait_ge(*pool_done.when('v0', 'clear'))
                    for par in range(2):
                        o = v0[:, tc, :, :].rearrange('p (g two) d -> p two g d', two=2)[:, par, :, 16 * par:16 * par + 16]
                        i0 = tile[:, 0:128].rearrange('p (g two d) -> p two g d', two=2, d=16)[:, par, :, :]
                        i1 = rows[:, A.rowbv, 0:128].rearrange('p (g two d) -> p two g d', two=2, d=16)[:, par, :, :]
                        ins = nc.vector.tensor_tensor(o, i0, i1, ALU.add)
                    ins.then_inc(*dve_emptied.reach('v', t, tc))
                else:
                    nc.vector.tensor_tensor(v1[:, tc, :], tile, rows[:, A.rowbv, :], ALU.add)\
                        .then_inc(*dve_emptied.reach('v', t, tc))

        def dve_attention(dve, A):
            t = A.tag
            if t < 2:
                dve_values(dve, A, range(C))
            dve.wait_ge(sems['mask%d_in' % t], 16)
            if t > 0:
                dve.wait_ge(*pool_done.when('neg', t))

            def inverse(n):
                for qc in range(C):
                    dve.wait_ge(*S['exp_done'].when(t, n, qc))
                nc.vector.reciprocal(row_inv[:, n % PSLOTS, :], row_sum[:, n % PSLOTS, :])\
                    .then_inc(*S['inverse_done'].reach(t, n))

            def slot_free(n):
                if n >= PSLOTS:
                    dve.wait_ge(*tile_ready.when('pT', t, n - PSLOTS, C - 1))

            def add_max(n, qc):
                s = n % PSLOTS
                if A.shared:
                    dve.wait_ge(*S['scores_ready'].when(t, n, qc))
                    src, other, fin = ps[:, qc, :], A.mask[:, qc, :], S['scores_taken'].reach(t, n, qc)
                else:
                    dve.wait_ge(*S['scores_taken'].when(t, n, qc))
                    src, other, fin = probs[:, s, qc, :], neg[:, qc, :], dve_done.reach('sm', t, n, qc)
                nc.vector.tensor_tensor_reduce(out=probs[:, s, qc, :], in0=src, in1=other, scale=-1.0, scalar=3.0e38,
                                               op0=ALU.add, op1=ALU.min,
                                               accum_out=row_max[:, s, qc:qc + 1]).then_inc(*fin)

            def times_mask(n, qc):
                dve.wait_ge(*S['scores_ready'].when(t, n, qc))
                nc.vector.tensor_tensor(probs[:, n % PSLOTS, qc, :], ps[:, qc, :], A.mask[:, qc, :], ALU.mult)\
                    .then_inc(*S['scores_taken'].reach(t, n, qc))

            for n in range(A.heads + LAG):
                m = n - LAG
                if n < A.heads:
                    slot_free(n)
                if A.shared:
                    for qc in range(C):
                        if n < A.heads:
                            add_max(n, qc)
                        if qc == 1 and 0 < n <= A.heads:
                            inverse(n - 1)
                        if m >= 0 and A.owner[qc] == 'd':
                            dve.wait_ge(*tile_ready.when('pT', t, m, qc))
                            if m >= 4:
                                dve.wait_ge(*S['context_ready'].when(t, m // 4 - 1, qc))
                            nc.vector.tensor_copy(pT[:, m % 4, qc, :], ps[:, ring.bank('pT', t, m, qc), :])\
                                .then_inc(*dve_emptied.reach('pT', t, m, qc))
                else:
                    for step in ('m0', 'm1', 'a0', 'i', 'm2', 'a1', 'm3', 'a2', 'a3'):
                        if step == 'i' and 0 < n <= A.heads:
                            inverse(n - 1)
                        if step[0] == 'm' and n < A.heads:
                            times_mask(n, int(step[1]))
                        if step[0] == 'a' and n < A.heads:
                            add_max(n, int(step[1]))

        def residual(dve, t, tc):
            dve.wait_ge(*pool_done.when('biased', t, tc))
            dve.wait_ge(*tile_ready.when('out', t, tc))
            nc.vector.tensor_tensor(x[:, tc, :], ps[:, ring.bank('out', t, tc), :], x[:, tc, :], ALU.add)\
                .then_inc(*dve_emptied.reach('out', t, tc))
            dve.wait_ge(*dve_emptied.when('out', t, tc))

        def pool_bias(pool, t, row, before):
            for tc in range(C):
                before(pool, tc)
                nc.gpsimd.tensor_tensor(x[:, tc, :], x[:, tc, :], rows[:, row, :], ALU.add)\
                    .then_inc(*pool_done.reach('biased', t, tc))

        def pool_attention(pool, A):
            t = A.tag
            if A.shared:
                pool_split(pool, A, 'k', 0)
            for g in range(4 if A.shared else 2):
                pool_split(pool, A, 'q', g)
            if t == 1:
                pool_split(pool, A, 'k', 0)
                pool_split(pool, A, 'k', 1)
            for n in range(1, A.heads + 1):
                g, i = divmod(n - 1, 4)
                if not A.shared and g + 2 < A.groups:
                    if i == 1:
                        pool_split(pool, A, 'q', g + 2)
                    if i == 2:
                        pool_split(pool, A, 'k', g + 2)
                pool.wait_ge(*S['inverse_done'].when(t, n - 1))
                for qc in range(C):
                    p = probs[:, (n - 1) % PSLOTS, qc, :]
                    nc.gpsimd.tensor_scalar(p, p, row_inv[:, (n - 1) % PSLOTS, qc:qc + 1], 1.0, ALU.mult, ALU.mult)\
                        .then_inc(*S['normalised'].reach(t, n - 1, qc))

        def pool_neg(pool, A):
            pool.wait_ge(sems[f'mask{A.tag}_in'], 16)
            if A.tag == 2:
                pool.wait_ge(*dve_done.when('sm', 1, 15, C - 1))
            ins = None
            for qc in range(C):
                ins = nc.gpsimd.tensor_scalar(neg[:, qc, :], A.mask[:, qc, :], -1.0, 10000.0, ALU.add, ALU.mult)
            ins.then_inc(*pool_done.reach('neg', A.tag))

        MIX_ROW = {'k': 0, 'w': 1, 'v': 2, 'r': 3, 'g': 4}
        MIX_AT = {'w': 3, 'k': 0, 'v': 1, 'r': 2, 'g': 3}

        HI_AT = {'xk2': 0, 'xr2': 1, 'gated': 2, 'kk': 2}

        def mix_wait(eng, l, name, c):
            eng.wait_ge(*(dve_done if c == C - 1 and name != 'g' else pool_done).when('mix', l, name, c))

        def pe_rwkv(pe, l):
            pe_norm_turn(pe, f'a{l}', xn2)
            w_wait(pe, f'small_{l}')
            small = weights(f'small_{l}')
            for part, (n0, rows_) in enumerate(((0, 128), (128, 32))):
                tile = take(pe, 'z', l, part)
                for fc in range(C):
                    if part == 0:
                        pe.wait_ge(*dve_done.when('xin', l, fc))
                    m = nc.tensor.matmul(tile[0:rows_, :], small[:, SMALL_MAA + fc * 160 + n0:SMALL_MAA + fc * 160 + n0 + rows_],
                                         mix[:, 2, fc, :], start=(fc == 0), stop=(fc == C - 1))
                m.then_inc(*tile_ready.reach('z', l, part))
            pe.wait_ge(sems['mixers_in'], 16 * (l - 1))

            def mixing(name, c):
                f = MIX_ROW[name]
                r, part = (32 * f, 0) if f < 4 else (0, 1)
                if c == 0:
                    pe.wait_ge(*act_emptied.when('z', l, part))
                tile = take(pe, 'mix', l, name, c)
                nc.tensor.matmul(tile, mixers[r:r + 32, part * H + c * P:part * H + (c + 1) * P], z[r:r + 32, part, :],
                                 start=True, stop=True).then_inc(*tile_ready.reach('mix', l, name, c))

            def project(hg, name, fcs=range(C), tile=None):
                if hg == 0:
                    w_wait(pe, f'{name}_{l}')
                tile = take(pe, f'{name}p', l, hg) if tile is None else tile
                to_T(pe, tile, weights(f'{name}_{l}'), mix[:, MIX_AT[name]], hg, fcs=fcs,
                     fin=tile_ready.reach(f'{name}p', l, hg) if C - 1 in fcs else None,
                     ready=(lambda fc: mix_wait(pe, l, name, fc)) if hg == 0 else None)
                return tile

            for name in 'wk':
                for c in range(C):
                    mixing(name, c)
            tile = take(pe, 'td', l)
            for fc in range(C):
                mix_wait(pe, l, 'w', fc)
                m = nc.tensor.matmul(tile[0:64, :], small[:, SMALL_TD1 + fc * 64:SMALL_TD1 + (fc + 1) * 64],
                                     mix[:, MIX_AT['w'], fc, :], start=(fc == 0), stop=(fc == C - 1))
            m.then_inc(*tile_ready.reach('td', l))
            for c in range(C):
                mixing('v', c)
            pe.wait_ge(*act_emptied.when('td', l))
            for c in range(C):
                tile = take(pe, 'decay', l, c)
                nc.tensor.matmul(tile, small[0:64, SMALL_TD2 + c * P:SMALL_TD2 + (c + 1) * P], tdh[:, :],
                                 start=True, stop=True).then_inc(*tile_ready.reach('decay', l, c))
            project(0, 'k')
            for c in range(C):
                mixing('r', c)
            project(0, 'v')
            project(0, 'r')

            def bonus_sum(hg):
                pe.wait_ge(*dve_done.when('ruk', l, hg))
                tile = take(pe, 'bonus', l, hg)
                nc.tensor.matmul(tile, ones_block[:, :], ruk[:, hg % 2, :], start=True, stop=True)\
                    .then_inc(*tile_ready.reach('bonus', l, hg))

            def gate(c, fc, tile):
                if (c, fc) == (0, 0):
                    w_wait(pe, f'g_{l}')
                tile = take(pe, 'gp', l, c) if fc == 0 else tile
                to_T(pe, tile, weights(f'g_{l}'), mix[:, MIX_AT['g']], c, fcs=(fc,),
                     fin=tile_ready.reach('gp', l, c) if fc == C - 1 else None,
                     ready=(lambda fc: mix_wait(pe, l, 'g', fc)) if c == 0 else None)
                return tile

            def reduce(t):
                hg, j = divmod(t, HS)
                jj, m = j % 4, j // 4
                if j == 0 and hg > 0:
                    pe.wait_ge(*act_done.when('rec', l, hg - 1))
                pe.wait_ge(*pool_done.when('prod', l, t))
                nc.tensor.matmul(ps[32 * jj:32 * jj + 32, OBANK, :], gather[:, m, :], prod[:, t % 3, :],
                                 start=(m == 0), stop=False, skip_group_check=True).then_inc(*S['reduced'].reach(l, t))
                if j == HS - 1:
                    pe.wait_ge(*dve_emptied.when('bonus', l, hg))
                    nc.tensor.matmul(ps[:, OBANK, :], permute[:, :], bonus[:, hg % 2, :], start=False, stop=True,
                                     skip_group_check=True).then_inc(*S['context_ready'].reach('rec', l, hg))

            bonus_sum(0)
            part = None
            lag = 3
            for t in range(C * HS + lag):
                hg, j = divmod(t, HS)
                if t < C * HS:
                    if j == 0:
                        pe.wait_ge(*dve_done.when('vlo', l, hg))
                    if t >= 4:
                        pe.wait_ge(*S['scores_taken'].when('kv', l, t - 4))
                    nc.tensor.matmul(ps[:, t % 4, :], pick[:, j * P:(j + 1) * P], vhi[:, hg % 2, :], start=True, stop=False)
                    nc.tensor.matmul(ps[:, t % 4, :], pick[:, j * P:(j + 1) * P], vlo[:, hg % 2, :], start=False, stop=True)\
                        .then_inc(*S['vb_ready'].reach(l, t))
                    if hg + 1 < C and 1 <= j <= 12:
                        fc = (j - 1) % 4
                        part = project(hg + 1, 'kvr'[(j - 1) // 4], (fc,), None if fc == 0 else part)
                    if hg == 0 and 11 <= j <= 14:
                        mixing('g', j - 11)
                    if hg + 1 < C and j == 15:
                        bonus_sum(hg + 1)
                    if hg == C - 1:
                        part = gate(j // 4, j % 4, part)
                if t >= lag:
                    reduce(t - lag)
            def wait(pe, c, t):
                if c == 0:
                    pe.wait_ge(*act_done.when('rec', l, t))
            pe_turn(pe, l, recT, 'recN', wait, permute_back)

            def wait(pe, c, t):
                if c == 0:
                    pe.wait_ge(*dve_done.when('gn', l, t))
            pe_turn(pe, l, centred, 'gnT', wait)
            parts_wait(pe, f'o_{l}')
            for tc in range(C):
                to_N3(pe, take(pe, 'wo', l, tc), f'o_{l}', (act_hi[:, 2], act_lo[:, 2]), tc, tile_ready.reach('wo', l, tc),
                      ready=(lambda fc: pe.wait_ge(*dve_done.when('gated_lo', l, fc))) if tc == 0 else None)
            pe_norm_turn(pe, f'f{l}', xn2)
            parts_wait(pe, f'fk_{l}')
            for c in range(C):
                to_T3(pe, take(pe, 'fk', l, c), f'fk_{l}', (act_hi[:, 0], act_lo[:, 1]), c, tile_ready.reach('fk', l, c),
                      ready=(lambda fc: pe.wait_ge(*dve_done.when('xk2_lo', l, fc))) if c == 0 else None)
            parts_wait(pe, f'fr_{l}')
            for tc in range(C):
                to_N3(pe, take(pe, 'fr', l, tc), f'fr_{l}', (act_hi[:, 1], act_lo[:, 2]), tc, tile_ready.reach('fr', l, tc),
                      ready=(lambda fc: pe.wait_ge(*dve_done.when('xr2_lo', l, fc))) if tc == 0 else None)
            parts_wait(pe, f'fv_{l}')
            for tc in range(C):
                to_N3(pe, take(pe, 'fv', l, tc), f'fv_{l}', (act_hi[:, 2], act_lo[:, 3]), tc, tile_ready.reach('fv', l, tc),
                      ready=(lambda fc: pe.wait_ge(*dve_done.when('kk_lo', l, fc))) if tc == 0 else None)

        def dve_rwkv(dve, l):
            def shift_mix(tag, mixes, then=None):
                def shift(c):
                    dve.wait_ge(*act_emptied.when('lnT', tag, c))
                    if c == 0:
                        dve.wait_ge(*pool_done.when('prev', tag))
                    nc.vector.tensor_tensor(sx[:, c, :], xa[:, c, 0:L], xa[:, c, 1:L + 1], ALU.subtract)\
                        .then_inc(*dve_done.reach('sx', tag, c))

                for k, (at_, name, out_label) in enumerate(mixes):
                    for c in range(C + 1):
                        if c < C:
                            if k == 0:
                                shift(c)
                                dve.wait_ge(*dve_done.when('sx', tag, c))
                            nc.vector.scalar_tensor_tensor(mix[:, at_, c, :], sx[:, c, :], col(f'{name}_{l}', c),
                                                           xa[:, c, 1:L + 1], ALU.mult, ALU.add)\
                                .then_inc(*dve_done.reach(out_label, l, c))
                        if c > 0 and then is not None:
                            then(out_label, c - 1, at_)

            shift_mix(f'a{l}', ((2, 'maa_x', 'xin'),))

            def mixed(name, chunks=range(C)):
                for c in chunks:
                    dve.wait_ge(*tile_ready.when('mix', l, name, c))
                    if name == 'r':
                        dve.wait_ge(*tile_ready.when('z', l, 1))
                    if name == 'g':
                        dve.wait_ge(*tile_ready.when('td', l))
                    nc.vector.scalar_tensor_tensor(mix[:, MIX_AT[name], c, :], ps[:, ring.bank('mix', l, name, c), :],
                                                   col(f'maa_{name}_{l}', c), sx[:, c, :], ALU.add, ALU.mult)\
                        .then_inc(*dve_emptied.reach('mix', l, name, c))
                    if c == C - 1 and name != 'g':
                        dve.wait_ge(*dve_emptied.when('mix', l, name, c))
                        m = mix[:, MIX_AT[name], c, :]
                        nc.vector.tensor_tensor(m, m, xa[:, c, 1:L + 1], ALU.add).then_inc(*dve_done.reach('mix', l, name, c))

            for name in 'wkvr':
                mixed(name)

            def heads_in(hg):
                s = hg % 2
                dve.wait_ge(*act_emptied.when('vp', l, hg))
                if hg >= 2:
                    dve.wait_ge(*S['vb_ready'].when(l, HS * (hg - 1) - 1))
                nc.vector.tensor_copy(vhi[:, s, :], vT[:, s, :]).then_inc(*dve_done.reach('vhi', l, hg))
                dve.wait_ge(*dve_done.when('vhi', l, hg))
                nc.vector.tensor_tensor(vlo[:, s, :], vT[:, s, :], vhi[:, s, :].bitcast(F32), ALU.subtract)\
                    .then_inc(*dve_done.reach('vlo', l, hg))
                dve.wait_ge(*act_emptied.when('rp', l, hg))
                dve.wait_ge(*act_emptied.when('kp', l, hg))
                if hg >= 2:
                    dve.wait_ge(*tile_ready.when('bonus', l, hg - 2))
                nc.vector.scalar_tensor_tensor(ruk[:, s, :], rT[:, s, :], col(f'u_{l}', hg), kT[:, s, :], ALU.mult, ALU.mult)\
                    .then_inc(*dve_done.reach('ruk', l, hg))

            def bonus_out(hg):
                s = hg % 2
                dve.wait_ge(*tile_ready.when('bonus', l, hg))
                if hg >= 2:
                    dve.wait_ge(*S['context_ready'].when('rec', l, hg - 2))
                nc.vector.tensor_tensor(bonus[:, s, :], ps[:, ring.bank('bonus', l, hg), :], vT[:, s, :], ALU.mult)\
                    .then_inc(*dve_emptied.reach('bonus', l, hg))

            heads_in(0)
            dve.wait_ge(*act_done.when('w', l, C - 1))
            dve.wait_ge(sems['s0_in'], 16)
            n = C * HS
            for t in range(n + 1):
                hg, j = divmod(t, HS)
                if t < n:
                    dve.wait_ge(*S['vb_ready'].when(l, t))
                    if t >= 3:
                        dve.wait_ge(*dve_done.when('scan', l, t - 3))
                    nc.vector.tensor_tensor(kvp[:, t % 3, :], kT[:, hg % 2, :], ps[:, t % 4, :], ALU.mult)\
                        .then_inc(*S['scores_taken'].reach('kv', l, t))
                if t >= 1:
                    u = t - 1
                    ug, uj = divmod(u, HS)
                    dve.wait_ge(*S['scores_taken'].when('kv', l, u))
                    if u >= 3:
                        dve.wait_ge(*pool_done.when('prod', l, u - 3))
                    nc.vector.tensor_tensor_scan(state[:, u % 3, 1:L + 1], decay[:, ug, :], kvp[:, u % 3, :],
                                                 s0[:, ug, uj:uj + 1], ALU.mult, ALU.add)\
                        .then_inc(*dve_done.reach('scan', l, u))
                if t < n and j == 1:
                    bonus_out(hg)
                if t < n and hg == 0 and j >= 12:
                    mixed('g', (j - 12,))
                if t < n and j == 14 and hg + 1 < C:
                    heads_in(hg + 1)
            def heads(ap):
                return ap.rearrange('p (h j) -> p h j', j=HS)

            def wide(ap):
                return ap.unsqueeze(2).to_broadcast([P, 32, HS])

            for tc in range(C):
                dve.wait_ge(*tile_ready.when('recN', l, tc))
                tile = ps[:, ring.bank('recN', l, tc), :]
                nc.vector.tensor_reduce(gsum[:, tc, :], heads(tile), AX.X, ALU.add).then_inc(*dve_done.reach('gsum', l, tc))
                dve.wait_ge(*dve_done.when('gsum', l, tc))
                nc.vector.scalar_tensor_tensor(heads(centred[:, tc, :]), wide(gsum[:, tc, :]), -1.0 / HS, heads(tile),
                                               ALU.mult, ALU.add)\
                    .then_inc(*dve_emptied.reach('recN', l, tc))
            for tc in range(C):
                dve.wait_ge(*act_done.when('gsq', l, tc))
                nc.vector.tensor_reduce(gsq[:, tc, :], heads(squared[:, tc, :]), AX.X, ALU.add)\
                    .then_inc(*dve_done.reach('gsq', l, tc))
            def small_step(what, *before):
                for w in before:
                    dve.wait_ge(*w)
                return dve_done.reach(what, l)

            fin = small_step('gvar', *(dve_done.when('gsq', l, tc) for tc in range(C)))
            nc.vector.tensor_scalar(gsq[:, :, :], gsq[:, :, :], 1.0 / HS, 1e-5, ALU.mult, ALU.add).then_inc(*fin)
            fin = small_step('root_inverse', act_done.when('root', l))
            nc.vector.reciprocal(ginv[:, :, :], gsum[:, :, :]).then_inc(*fin)
            fin = small_step('root_other', dve_done.when('root_inverse', l))
            nc.vector.tensor_tensor(ginv[:, :, :], gsq[:, :, :], ginv[:, :, :], ALU.mult).then_inc(*fin)
            fin = small_step('root_twice', dve_done.when('root_other', l))
            nc.vector.tensor_tensor(ginv[:, :, :], ginv[:, :, :], gsum[:, :, :], ALU.add).then_inc(*fin)
            fin = small_step('ginv', dve_done.when('root_twice', l))
            nc.vector.reciprocal(ginv[:, :, :], ginv[:, :, :]).then_inc(*fin)
            dve.wait_ge(*dve_done.when('ginv', l))
            for tc in range(C):
                nc.vector.scalar_tensor_tensor(heads(centred[:, tc, :]), heads(centred[:, tc, :]), 2.0, wide(ginv[:, tc, :]),
                                               ALU.mult, ALU.mult).then_inc(*dve_done.reach('gn', l, tc))
            def low_part(name, c, place_):
                dve.wait_ge(*act_done.when(name + '_hi', l, c))
                nc.vector.tensor_tensor(act_lo[:, place_, c, :], mix[:, place_, c, :],
                                        act_hi[:, HI_AT[name], c, :].bitcast(F32), ALU.subtract)\
                    .then_inc(*dve_done.reach(name + '_lo', l, c))

            for c in range(C + 1):
                if c < C:
                    dve.wait_ge(*act_emptied.when('gnT', l, c))
                    dve.wait_ge(*act_emptied.when('gp', l, c))
                    nc.vector.tensor_tensor(mix[:, 2, c, :], squared[:, c, :], gT[:, c, :], ALU.mult)\
                        .then_inc(*dve_done.reach('gated', l, c))
                if c > 0:
                    low_part('gated', c - 1, 2)

            def add_wo(tc):
                dve.wait_ge(*tile_ready.when('wo', l, tc))
                nc.vector.tensor_tensor(x[:, tc, :], ps[:, ring.bank('wo', l, tc), :], x[:, tc, :], ALU.add)\
                    .then_inc(*dve_emptied.reach('wo', l, tc))
                dve.wait_ge(*dve_emptied.when('wo', l, tc))

            dve_norm(dve, f'f{l}', xn2, add_wo)
            shift_mix(f'f{l}', ((1, 'ffn_k', 'xk2'), (2, 'ffn_r', 'xr2')), low_part)
            for c in range(C):
                low_part('kk', c, 3)
            def add_ffn(tc):
                dve.wait_ge(*act_emptied.when('fr', l, tc))
                dve.wait_ge(*tile_ready.when('fv', l, tc))
                nc.vector.tensor_tensor(recT[:, tc, :], ps[:, ring.bank('fv', l, tc), :], gT[:, tc, :], ALU.mult)\
                    .then_inc(*dve_emptied.reach('fv', l, tc))
                dve.wait_ge(*dve_emptied.when('fv', l, tc))
                nc.vector.tensor_tensor(x[:, tc, :], x[:, tc, :], recT[:, tc, :], ALU.add)\
                    .then_inc(*dve_done.reach('x', l, tc))
                dve.wait_ge(*dve_done.when('x', l, tc))

            if l == 2:
                dve_norm(dve, 'a3', xn2, add_ffn)
            else:
                for tc in range(C):
                    add_ffn(tc)

        def act_rwkv(act, l):
            act_norm(act, f'a{l}', xa, f'ln1_w_{l}', f'ln1_b_{l}', shift=1)
            for part, rows_ in enumerate((128, 32)):
                act.wait_ge(*tile_ready.when('z', l, part))
                nc.scalar.activation(z[0:rows_, part, :], ps[0:rows_, ring.bank('z', l, part), :], ACT.Tanh)\
                    .then_inc(*act_emptied.reach('z', l, part))
            act.wait_ge(*tile_ready.when('td', l))
            nc.scalar.activation(tdh[:, :], ps[0:64, ring.bank('td', l), :], ACT.Tanh).then_inc(*act_emptied.reach('td', l))
            for c in range(C):
                act.wait_ge(*tile_ready.when('decay', l, c))
                nc.scalar.activation(decay[:, c, :], ps[:, ring.bank('decay', l, c), :], ACT.Exp, bias=col(f'decay_{l}', c))\
                    .then_inc(*act_emptied.reach('decay', l, c))
            def heads_in(hg, names=('k', 'v', 'r')):
                s = hg % 2
                for name in names:
                    out = {'k': kT, 'v': vT, 'r': rT}[name]
                    act.wait_ge(*tile_ready.when(f'{name}p', l, hg))
                    if hg >= 2:
                        act.wait_ge(*pool_done.when('prod', l, HS * (hg - 1) - 1))
                        act.wait_ge(*dve_emptied.when('bonus', l, hg - 2))
                    nc.scalar.activation(out[:, s, :], ps[:, ring.bank(f'{name}p', l, hg), :], ACT.Copy)\
                        .then_inc(*act_emptied.reach(f'{name}p', l, hg))

            heads_in(0, 'k')
            for c in range(C):
                act.wait_ge(*act_emptied.when('decay', l, c))
                nc.scalar.activation(decay[:, c, :], decay[:, c, :], ACT.Exp, scale=-1.0).then_inc(*act_done.reach('w', l, c))

            heads_in(0, 'vr')
            act.wait_ge(sems['s0_in'], 16)
            for t in range(C * HS):
                hg, j = divmod(t, HS)
                if t >= 3:
                    act.wait_ge(*pool_done.when('prod', l, t - 3))
                nc.scalar.activation(state[:, t % 3, 0:1], s0[:, hg, j:j + 1], ACT.Copy).then_inc(*act_done.reach('s0', l, t))
                if j in (5, 9, 13) and hg + 1 < C:
                    heads_in(hg + 1, 'kvr'[j // 4 - 1])
                if j == 4 and hg > 0:
                    act.wait_ge(*S['context_ready'].when('rec', l, hg - 1))
                    nc.scalar.activation(recT[:, hg - 1, :], ps[:, OBANK, :], ACT.Copy).then_inc(*act_done.reach('rec', l, hg - 1))
                if hg == C - 1 and j % 4 == 3:
                    c = j // 4
                    act.wait_ge(*tile_ready.when('gp', l, c))
                    nc.scalar.activation(gT[:, c, :], ps[:, ring.bank('gp', l, c), :], ACT.Silu)\
                        .then_inc(*act_emptied.reach('gp', l, c))
            act.wait_ge(*S['context_ready'].when('rec', l, C - 1))
            nc.scalar.activation(recT[:, C - 1, :], ps[:, OBANK, :], ACT.Copy).then_inc(*act_done.reach('rec', l, C - 1))

            def high_part(name, c, place_, ready):
                act.wait_ge(*ready)
                nc.scalar.activation(act_hi[:, HI_AT[name], c, :], mix[:, place_, c, :], ACT.Copy)\
                    .then_inc(*act_done.reach(name + '_hi', l, c))

            act_w(act, f'o_{l}')
            for tc in range(C):
                act.wait_ge(*dve_emptied.when('recN', l, tc))
                nc.scalar.activation(squared[:, tc, :], centred[:, tc, :], ACT.Square).then_inc(*act_done.reach('gsq', l, tc))
            act.wait_ge(*dve_done.when('gvar', l))
            nc.scalar.activation(gsum[:, :, :], gsq[:, :, :], ACT.Sqrt).then_inc(*act_done.reach('root', l))
            act_w(act, f'fk_{l}')
            for c in range(C):
                act.wait_ge(*tile_ready.when('gnT', l, c))
                if c == 0:
                    act.wait_ge(*dve_done.when('gsq', l, C - 1))
                nc.scalar.activation(squared[:, c, :], ps[:, ring.bank('gnT', l, c), :], ACT.Identity,
                                     bias=col(f'gn_b_{l}', c), scale=col(f'gn_w_{l}', c))\
                    .then_inc(*act_emptied.reach('gnT', l, c))
            for c in range(C):
                high_part('gated', c, 2, dve_done.when('gated', l, c))
            act_norm(act, f'f{l}', xa, f'ln2_w_{l}', f'ln2_b_{l}', shift=1)
            for c in range(C):
                high_part('xk2', c, 1, dve_done.when('xk2', l, c))
            act_w(act, f'fr_{l}')
            for c in range(C):
                high_part('xr2', c, 2, dve_done.when('xr2', l, c))
            for c in range(C):
                act.wait_ge(*tile_ready.when('fk', l, c))
                nc.scalar.activation(mix[:, 3, c, :], ps[:, ring.bank('fk', l, c), :], ACT.Relu)\
                    .then_inc(*act_emptied.reach('fk', l, c))
                act.wait_ge(*act_emptied.when('fk', l, c))
                nc.scalar.activation(mix[:, 3, c, :], mix[:, 3, c, :], ACT.Square).then_inc(*act_done.reach('kk', l, c))
                high_part('kk', c, 3, act_done.when('kk', l, c))
            act_w(act, f'fv_{l}')
            for tc in range(C):
                act.wait_ge(*tile_ready.when('fr', l, tc))
                nc.scalar.activation(gT[:, tc, :], ps[:, ring.bank('fr', l, tc), :], ACT.Sigmoid)\
                    .then_inc(*act_emptied.reach('fr', l, tc))

        def pool_rwkv(pool, l):
            def previous(tag, token):
                nc.gpsimd.tensor_copy(xa[:, :, 0:1], ctxT[:, :, token:token + 1]).then_inc(*pool_done.reach('prev', tag))

            pool_norm(pool, f'a{l}', 1e-5)
            previous(f'a{l}', 1)

            def add_xa(name, c):
                pool.wait_ge(*dve_emptied.when('mix', l, name, c))
                m = mix[:, MIX_AT[name], c, :]
                nc.gpsimd.tensor_tensor(m, m, xa[:, c, 1:L + 1], ALU.add).then_inc(*pool_done.reach('mix', l, name, c))

            for name in 'wkvr':
                for c in range(C - 1):
                    add_xa(name, c)
            for t in range(C * HS):
                hg, j = divmod(t, HS)
                pool.wait_ge(*dve_done.when('scan', l, t))
                pool.wait_ge(*act_done.when('s0', l, t))
                if t >= 3:
                    pool.wait_ge(*S['reduced'].when(l, t - 3))
                nc.gpsimd.tensor_tensor(prod[:, t % 3, :], state[:, t % 3, 0:L], rT[:, hg % 2, :], ALU.mult)\
                    .then_inc(*pool_done.reach('prod', l, t))
                if hg == 0 and j >= 12:
                    add_xa('g', j - 12)
            pool_w(pool, f'o_{l}')
            pool_w(pool, f'fk_{l}')
            pool_norm(pool, f'f{l}', 1e-5)
            previous(f'f{l}', 0)
            pool_w(pool, f'fr_{l}')
            pool_w(pool, f'fv_{l}')

        AHEAD = ['ctx_in', 'mask0_in', 'xT_in'] + [f'w{n}' for n in range(WSLOTS)]

        def ahead(sp, name, index, clear=True):
            if clear:
                sp.sem_clear(sems[name])
            if name[0] == 'w':
                n = int(name[1])
                sp.dma_start(wring[:, n, :], a['blocks'][n]).then_inc(sems[name], 16)
                return
            src, dst = {'ctx_in': ('ctxT', ctxT), 'mask0_in': ('mask0', maskA), 'xT_in': ('xT', srcT)}[name]
            sp.dma_start(dst[:, :, :], a[src][index].rearrange('(c p) t -> p c t', p=P)).then_inc(sems[name], 16)

        with nc.Block() as block:
            @block.sync
            def _(sp):
                for name in ('w0', 'ctx_in', 'xT_in', 'w1', 'mask0_in', 'w2'):
                    ahead(sp, name, 0, clear=False)
                sp.dma_start(maskB[:, :, :], a['mask1'].rearrange('(c p) t -> p c t', p=P)).then_inc(sems['mask1_in'], 16)

        with nc.Fori(0, samples) as b:
            with nc.Block() as block:
                @block.gpsimd
                def _(pool):
                    for n, s in sems.items():
                        if n not in AHEAD + ['mask1_in', 'x_stored']:
                            nc.gpsimd.sem_clear(s)

            with nc.Block() as block:
                @block.tensor
                def _(pe):
                    pe_attention(pe, A0)
                    pe_norm_turn(pe, 'ln1', xn)
                    pe_attention(pe, A1)
                    w_wait(pe, A2.kblk)
                    pe_k(pe, A2, 0)
                    pe_k(pe, A2, 1)
                    pe_values(pe, A2, (0, 1))
                    pe_norm_turn(pe, 'ln2', xn)
                    pe_attention(pe, A2)
                    pe_norm_turn(pe, 'ln3', xn)
                    def up(i):
                        parts_wait(pe, f'up_{i}')
                        for c in range(C):
                            to_T3(pe, take(pe, 'up', i, c), f'up_{i}', (hi, lo), c, tile_ready.reach('up', i, c),
                                  ready=(lambda fc: pe.wait_ge(*dve_done.when('srcT_lo', fc))) if (i, c) == (0, 0) else None)

                    def down(i):
                        parts_wait(pe, f'down_{i}')
                        src = hidden_hi[:, i % 2], hidden_lo[:, i % 2]
                        for tc in range(C):
                            m = to_N3(pe, ps[:, tc, :], f'down_{i}', src, tc, begins=(i == 0), ends=(i == FFN - 1),
                                      ready=(lambda fc: pe.wait_ge(*dve_done.when('hidden_lo', i, fc))) if tc == 0 else None)
                            if i == FFN - 1 and tc < C - 1:
                                m.then_inc(*S['mlp_ready'].reach('tile', tc))
                        m.then_inc(*S['mlp_ready'].reach(f'down_{i}'))

                    up(0)
                    for i in range(1, FFN):
                        up(i)
                        down(i - 1)
                    down(FFN - 1)
                    for l in (2, 3):
                        pe_rwkv(pe, l)

                @block.scalar
                def _(act):
                    act_attention(act, A0)
                    act_norm(act, 'ln1', srcT, 'ln1_s', 'ln1_b')
                    act_attention(act, A1)
                    act.wait_ge(sems['stack0'], stack_total(A1, 2))
                    act.wait_ge(sems['stack1'], stack_total(A1, 3))
                    act_split(act, A2, 'k', 0)
                    act_split(act, A2, 'k', 1)
                    act_norm(act, 'ln2', srcT, 'ln2_s', 'ln2_b')
                    act_attention(act, A2)
                    act_w(act, 'up_0', S['scores_ready'].when(2, 15, C - 1))
                    act_norm(act, 'ln3', srcT, 'ln3_s', 'ln3_b', parts=True)
                    act_w(act, 'up_1')
                    for k, name in enumerate(MLP_ORDER):
                        if name.startswith('up'):
                            i = int(name[-1])
                            for c in range(C):
                                act.wait_ge(*tile_ready.when('up', i, c))
                                if i >= 1:
                                    act.wait_ge(*dve_done.when('hidden_lo', i - 1, c))
                                nc.scalar.activation(hidden[:, c, :], ps[:, ring.bank('up', i, c), :],
                                                     ACT.Gelu_apprx_tanh, bias=col(f'b1_{i}', c))\
                                    .then_inc(*act_emptied.reach('up', i, c))
                                act.wait_ge(*act_emptied.when('up', i, c))
                                if i >= 2:
                                    act.wait_ge(*S['mlp_ready'].when(f'down_{i - 2}'))
                                nc.scalar.activation(hidden_hi[:, i % 2, c, :], hidden[:, c, :], ACT.Copy)\
                                    .then_inc(*act_done.reach('hidden_hi', i, c))
                        if k + 2 < len(MLP_ORDER):
                            act_w(act, MLP_ORDER[k + 2])
                    for l in (2, 3):
                        act_rwkv(act, l)

                @block.vector
                def _(dve):
                    dve_attention(dve, A0)
                    def affine(tc):
                        dve.wait_ge(*dve_done.when('xn', 'ln0', tc))
                        nc.vector.tensor_tensor(xn[:, tc, :], xn[:, tc, :], rows[:, 2, :], ALU.mult)\
                            .then_inc(*dve_done.reach('gamma', tc))
                        dve.wait_ge(*dve_done.when('gamma', tc))
                        nc.vector.tensor_tensor(x[:, tc, :], xn[:, tc, :], rows[:, 3, :], ALU.add)\
                            .then_inc(*dve_done.reach('x', 0, tc))
                        dve.wait_ge(*dve_done.when('x', 0, tc))
                        dve_stats(dve, 'ln1', tc)

                    dve_norm(dve, 'ln0', xn, lambda tc: residual(dve, 0, tc), affine)
                    for tc in range(C):
                        dve_normalise(dve, 'ln1', tc, xn)
                    dve_attention(dve, A1)

                    dve_norm(dve, 'ln2', xn, lambda tc: residual(dve, 1, tc))
                    dve_values(dve, A2, range(C))
                    dve_attention(dve, A2)
                    dve_norm(dve, 'ln3', xn, lambda tc: residual(dve, 2, tc))
                    for c in range(C):
                        dve.wait_ge(*act_done.when('srcT_hi', c))
                        nc.vector.tensor_tensor(lo[:, c, :], srcT[:, c, :], hi[:, c, :].bitcast(F32), ALU.subtract)\
                            .then_inc(*dve_done.reach('srcT_lo', c))
                    for i in range(FFN):
                        for c in range(C):
                            dve.wait_ge(*act_done.when('hidden_hi', i, c))
                            nc.vector.tensor_tensor(hidden_lo[:, i % 2, c, :], hidden[:, c, :],
                                                    hidden_hi[:, i % 2, c, :].bitcast(F32), ALU.subtract)\
                                .then_inc(*dve_done.reach('hidden_lo', i, c))

                    def add_mlp(tc):
                        dve.wait_ge(*(S['mlp_ready'].when('tile', tc) if tc < C - 1 else S['mlp_ready'].when(f'down_{FFN - 1}')))
                        dve.wait_ge(*pool_done.when('biased', 'mlp', tc))
                        nc.vector.tensor_tensor(x[:, tc, :], ps[:, tc, :], x[:, tc, :], ALU.add)\
                            .then_inc(*dve_done.reach('x', 1, tc))
                        dve.wait_ge(*dve_done.when('x', 1, tc))

                    dve_norm(dve, 'a2', xn2, add_mlp)
                    nc.vector.tensor_copy(pick[:, :].rearrange('p (j h i) -> p j h i', j=HS, h=HEADS),
                                          ident[:, :].rearrange('p (h j) -> p j h', h=HEADS).unsqueeze(3)
                                          .to_broadcast([P, HS, HEADS, HS])).then_inc(*dve_done.reach('pick'))
                    dve.wait_ge(*dve_done.when('pick'))
                    dve_rwkv(dve, 2)
                    dve_rwkv(dve, 3)

                @block.gpsimd
                def _(pool):
                    nc.gpsimd.memset(v0[:, :, :, :], 0.0).then_inc(*pool_done.reach('v0', 'clear'))
                    pool_attention(pool, A0)
                    pool.wait_ge(sems['x_in'], 16)
                    pool.wait_ge(sems['rows_in'], 16)
                    pool_bias(pool, 0, A0.rowbo, lambda e, tc: None)
                    pool_norm(pool, 'ln0', 1e-6)
                    pool_norm(pool, 'ln1', 1e-5)
                    pool_neg(pool, A1)
                    pool.wait_ge(sems['rows_in'], 32)
                    pool_bias(pool, 1, A1.rowbo, lambda e, tc: e.wait_ge(*dve_done.when('xn', 'ln1', tc)))
                    pool_attention(pool, A1)
                    pool_norm(pool, 'ln2', 1e-5)
                    pool_split(pool, A2, 'k', 0)
                    pool_split(pool, A2, 'k', 1)
                    pool_neg(pool, A2)
                    pool_bias(pool, 2, A2.rowbo, lambda e, tc: e.wait_ge(*dve_done.when('xn', 'ln2', tc)))
                    pool_attention(pool, A2)
                    pool_w(pool, 'up_0')
                    pool_norm(pool, 'ln3', 1e-5)
                    pool.wait_ge(sems['rows_in'], 48)
                    pool_w(pool, 'up_1')
                    pool_bias(pool, 'mlp', 0, lambda e, tc: e.wait_ge(*dve_done.when('xn', 'ln3', tc)))
                    for name in MLP_ORDER[2:]:
                        pool_w(pool, name)
                    for l in (2, 3):
                        pool_rwkv(pool, l)

                @block.sync
                def _(sp):
                    def load(dst, src, name):
                        sp.dma_start(dst, src).then_inc(sems[name], 16)

                    load(rows[:, 0:4, :], a['rows0'].unsqueeze(0).to_broadcast([P, 4, H]), 'rows_in')
                    sp.wait_ge(sems['x_stored'], 16)
                    sp.sem_clear(sems['x_stored'])
                    load(x[:, :, :], a['x'][b].rearrange('(c p) t -> p c t', p=P), 'x_in')
                    for g in range(A0.groups):
                        sp_stack(sp, A0, g)
                        if g == 1:
                            load_weights(sp, 'k1', freed)
                    sp.wait_ge(*dve_done.when('x', 0, C - 1))
                    load(rows[:, :, :], a['rows1'][0:NROWS].unsqueeze(0).to_broadcast([P, NROWS, H]), 'rows_in')
                    load(maskA[:, :, :], a['mask2'][b].rearrange('(c p) t -> p c t', p=P), 'mask2_in')
                    load_weights(sp, 'v1', freed)
                    sp_stack(sp, A1, 0)
                    sp_stack(sp, A1, 1)
                    sp_stack(sp, A1, 2)
                    load_weights(sp, 'o1', freed)
                    sp_stack(sp, A1, 3)
                    load_weights(sp, 'k2', freed)
                    load_weights(sp, 'v2', freed)
                    load(rows[:, 0, :], a['rows1'][NROWS:].to_broadcast([P, H]), 'rows_in')
                    load_weights(sp, 'q2', freed)
                    sp_stack(sp, A2, 0)
                    sp_stack(sp, A2, 1)
                    sp_stack(sp, A2, 2)
                    load_weights(sp, 'o2', freed)
                    sp_stack(sp, A2, 3)
                    load_weights(sp, 'down_3', freed)
                    sp.wait_ge(*dve_done.when('x', 1, C - 1))
                    load(s0[:, :, :], a['ctx'][b, 2:2 + HS, :].rearrange('(c r) (q j) -> (r q) c j', c=C, j=HS), 's0_in')
                    load(mixers[:, :], a['mixers'][0], 'mixers_in')
                    load_weights(sp, 'fv_2', freed)
                    sp.wait_ge(*tile_ready.when('mix', 2, 'g', C - 1))
                    load(mixers[:, :], a['mixers'][1], 'mixers_in')
                    load_weights(sp, 'fv_3', freed)
                    sp.wait_ge(*pool_done.when('prev', 'f3'))
                    ahead(sp, 'ctx_in', b + 1)
                    ahead(sp, 'mask0_in', b + 1)
                    sp.wait_ge(*dve_done.when('xr2', 3, C - 1))
                    ahead(sp, 'xT_in', b + 1)
                    for n in (1, 2, 0):
                        sp.wait_ge(*freed(BLOCKS[len(BLOCKS) - WSLOTS + (n - len(BLOCKS)) % WSLOTS]))
                        ahead(sp, f'w{n}', b + 1)
                    fin = dve_done.when('x', 3, C - 1)
                    sp.wait_ge(*fin)
                    sp.dma_start(a['out'][b].rearrange('(c p) t -> p c t', p=P), x[:, :, :]).then_inc(sems['x_stored'], 16)

        with nc.Block() as block:
            @block.sync
            def _(sp):
                for name in AHEAD + ['x_stored']:
                    sp.wait_ge(sems[name], 16)

    out = {n: s.marks for n, s in sig.items()}
    out['ring'] = {label: n for n, label in enumerate(ring.labels)}
    return out


def _block(w):
    import numpy as np
    n = w.shape[1]
    out = np.zeros((P, C * H), np.float32)
    out[:, :C * n] = w.reshape(C, P, n).transpose(1, 0, 2).reshape(P, C * n)
    return out


def _arrays(v):
    import numpy as np
    x, ctx = v['x'], v['ctx_2048']
    more = lambda w: np.concatenate([w, w[-1:]])
    d = {'x': x, 'xT': more(x.transpose(0, 2, 1)), 'ctx': ctx, 'ctxT': more(ctx.transpose(0, 2, 1)),
         'mask0': more(v['mask_Bx1xSxS2_ff0'].reshape(B, L, L)), 'mask1': v['mask_1x1xSxS2_fc1'].reshape(L, L),
         'mask2': v['mask_Bx1xSxS2_ff1'].reshape(B, L, L)}
    g = lambda n: v['L0_xattn_' + n]
    blk = {'kv0': _block(np.concatenate([g('Wk'), g('Wv'), np.zeros((H, 256), np.float32)], 1)),
           'q0': _block(g('Wq').reshape(H, 8, 4, 16).transpose(0, 2, 1, 3).reshape(H, H)),
           'o0': _block(g('Wo').reshape(4, 2, 4, 16, H).transpose(0, 2, 1, 3, 4).reshape(H, H))}
    vec = {'bq0': g('bq').reshape(8, 4, 16).transpose(1, 0, 2).reshape(H), 'bk0': np.pad(g('bk'), (0, 384))}
    r0 = [np.pad(g('bv'), (0, 384)), g('bo'), g('gamma'), g('beta')]
    g = lambda n: v['L1_xattn_' + n]
    q, k, w = np.split(g('w_qkv'), 3, 1)
    k2, w2 = np.split(g('w_kv'), 2, 1)
    blk |= {'q1': _block(q), 'k1': _block(k), 'v1': _block(w), 'o1': _block(g('w_ao')), 'q2': _block(g('w_q')),
            'k2': _block(k2), 'v2': _block(w2), 'o2': _block(g('w_co'))}
    b, b2 = g('b_qkv'), g('b_kv')
    vec |= {'ln1_s': g('ln1_s'), 'ln1_b': g('ln1_b'), 'bq1': b[:H], 'bk1': b[H:2 * H], 'ln2_s': g('ln2_s'),
            'ln2_b': g('ln2_b'), 'bq2': g('b_q'), 'bk2': b2[:H], 'ln3_s': g('ln3_s'), 'ln3_b': g('ln3_b')}
    r1 = [b[2 * H:], g('b_ao'), b2[H:], g('b_co'), g('b2')]
    for i in range(FFN):
        s = slice(i * H, (i + 1) * H)
        blk |= {f'up_{i}': _block(g('w1')[:, s]), f'down_{i}': _block(g('w2')[s])}
        vec[f'b1_{i}'] = g('b1')[s]
    mixers = np.zeros((2, P, 2 * H), np.float32)
    for l in (2, 3):
        g = lambda n: v[f'L{l}_xattn_' + n]
        td, u = ('td', 'u') if l == 2 else ('decay', 'faaaa')
        wf = {c: g(f'Wf{c}') if l == 2 else g(f'ffn_W{c}') for c in 'krv'}
        small = _block(g('maa_w1'))
        small[:, SMALL_TD1:SMALL_TD2] = _block(g(f'{td}_w1'))[:, :SMALL_TD2 - SMALL_TD1]
        small[:64, SMALL_TD2:SMALL_TD2 + H] = g(f'{td}_w2')
        blk[f'small_{l}'] = small
        mixers[l - 2, :, :H] = g('maa_w2')[:4].reshape(P, H)
        mixers[l - 2, :32, H:] = g('maa_w2')[4]
        for n, w in (('k', g('Wk')), ('r', g('Wr')), ('v', g('Wv')), ('g', g('Wg')), ('o', g('Wo')),
                     ('fk', wf['k']), ('fr', wf['r']), ('fv', wf['v'])):
            blk[f'{n}_{l}'] = _block(w.T)
        ms = g('maa_stack').reshape(5, H)
        vec |= {f'{n}_{l}': g(n) for n in ('ln1_w', 'ln1_b', 'ln2_w', 'ln2_b', 'maa_x', 'gn_w', 'gn_b')}
        vec |= {f'maa_{n}_{l}': ms[i] for i, n in enumerate('kwvrg')}
        vec |= {f'decay_{l}': g('time_decay'), f'u_{l}': g(u).reshape(H), f'ffn_k_{l}': g('ffn_maa_k'),
                f'ffn_r_{l}': g('ffn_maa_r')}
    d['mixers'] = mixers
    d['blocks'] = np.stack([blk[n] for n in BLOCKS])
    d['cols'] = np.stack([vec[n] for n in VECTORS]).reshape(len(VECTORS), C, P).transpose(2, 0, 1).reshape(P, -1)
    d['rows0'], d['rows1'] = np.stack(r0), np.stack(r1)
    d['ident'] = np.eye(P, dtype=np.float32)
    d['ones_block'] = np.kron(np.eye(HEADS), np.ones((HS, HS))).astype(np.float32)
    perm, gather = np.zeros((P, P), np.float32), np.zeros((P, 4, 32), np.float32)
    for h in range(HEADS):
        for j in range(HS):
            m, jj = divmod(j, 4)
            perm[h * HS + j, 32 * jj + 4 * h + m] = 1
        for m in range(4):
            gather[h * HS:(h + 1) * HS, m, 4 * h + m] = 1
    d['permute'], d['permute_back'], d['gather'] = perm, perm.T, gather
    return {n: np.ascontiguousarray(w, dtype=np.float32) for n, w in d.items()}


def kernel(**inputs):
    import numpy as np
    import concourse.bacc as bacc
    from concourse.bass_utils import run_bass_kernel_spmd
    arrays = _arrays({n: np.asarray(w) for n, w in inputs.items()})
    known = None
    for _ in range(2):
        nc = bacc.Bacc("TRN2", target_bir_lowering=False, num_devices=1)
        a = {n: nc.dram_tensor(f"in_{n}_dram", w.shape, F32, kind="ExternalInput").ap() for n, w in arrays.items()}
        a['out'] = nc.dram_tensor("out_dram", (B, L, H), F32, kind="ExternalOutput").ap()
        known = build(nc, a, known)
    r = run_bass_kernel_spmd(nc, [{f"in_{n}_dram": w for n, w in arrays.items()}], core_ids=[0])
    return r.results[0]["out_dram"]
```

```python
from contextlib import ExitStack

import concourse.bass as bass
from concourse import mybir

F32 = mybir.dt.float32
F32R = mybir.dt.float32r
ALU = mybir.AluOpType
ACT = mybir.ActivationFunctionType
AX = mybir.AxisListType

P = 128
B, L, H = 4, 512, 512
C = H // P
FFN = 4
WSLOTS = 3
RING = 3
RING0 = 4
OBANK = 7
LAG = 2
PSLOTS = LAG + 1
WKV_LAG = 5

VECTORS = ['bq0', 'bk0', 'ln1_s', 'ln1_b', 'bq1', 'bk1', 'ln2_s', 'ln2_b', 'bq2', 'bk2', 'ln3_s', 'ln3_b',
           'b1_0', 'b1_1', 'b1_2', 'b1_3']
RWKV_VECTORS = ['ln1_w', 'ln1_b', 'ln2_w', 'ln2_b', 'maa_x', 'maa_k', 'maa_w', 'maa_v', 'maa_r', 'maa_g',
                'decay', 'u', 'gn_w', 'gn_b', 'ffn_k', 'ffn_r']
for _layer in (2, 3):
    VECTORS += [f'{n}_{_layer}' for n in RWKV_VECTORS]
COL = {n: C * k for k, n in enumerate(VECTORS)}
ROWS = {0: ['bv', 'bo', 'gamma', 'beta'], 1: ['bv', 'b_ao', 'bv2', 'b_co', 'b2']}
NROWS = 4

BLOCKS = ['kv0', 'q0', 'o0', 'q1', 'k1', 'v1', 'o1', 'k2', 'v2', 'q2', 'o2',
          'up_0', 'up_1', 'down_0', 'up_2', 'down_1', 'up_3', 'down_2', 'down_3']
for _layer in (2, 3):
    BLOCKS += [f'{n}_{_layer}' for n in ('small', 'k', 'v', 'r', 'g', 'o', 'fk', 'fr', 'fv')]
SMALL_MAA, SMALL_TD1, SMALL_TD2 = 0, C * 160, C * 224

HEADS = 8
HS = 16
PRODS = 6


class Signal:

    def __init__(self, sem, known):
        self.sem, self.count, self.known, self.marks = sem, 0, known, {}

    def reach(self, *label):
        self.count += 1
        assert label not in self.marks, label
        self.marks[label] = self.count
        return self.sem, 1

    def when(self, *label):
        return self.sem, (self.known[label] if self.known is not None else 1)


class Ring:

    def __init__(self, known):
        self.labels, self.known = [], known

    def take(self, *label):
        self.labels.append(label)
        n = len(self.labels) - 1
        return RING0 + n % RING, self.labels[n - RING] if n >= RING else None

    def bank(self, *label):
        return RING0 + (self.known[label] if self.known is not None else 0) % RING


SIGNALS = ['tile_ready', 'scores_ready', 'context_ready', 'mlp_ready', 'vb_ready', 'reduced',
           'act_emptied', 'dve_emptied', 'exp_done', 'act_done', 'scores_taken', 'dve_done', 'inverse_done',
           'pool_done', 'normalised']
LOADS = ['x_in', 'xT_in', 'ctx_in', 'rows_in', 'mask0_in', 'mask1_in', 'mask2_in', 's0_in', 'fold_in', 'mixers_in', 'stack0', 'stack1', 'x_stored']


def build(nc, a, known, samples=B):
    base = -(-nc.sbuf_base // 32) * 32
    top = nc.sbuf_usable_end

    def place(name, shape, offset, dt=F32):
        n = 1
        for s in shape[1:]:
            n *= s
        assert base + offset + 4 * n <= top, (name, offset + 4 * n)
        return nc.alloc_sbuf_tensor_at(name, shape, dt, offset=base + offset), offset + -(-4 * n // 32) * 32

    at = 0
    x, at = place('x', [P, C, H], at)
    ctxT, at = place('ctxT', [P, C, L], at)
    wring, at = place('wring', [P, WSLOTS, C * H], at)
    maskA, at = place('maskA', [P, C, L], at)
    maskB, at = place('maskB', [P, C, L], at)
    neg, at = place('neg', [P, C, L], at)
    khi0, _ = place('khi0', [P, L], at - 4 * C * L, F32R)
    klo0, _ = place('klo0', [P, L], at - 4 * (C - 1) * L, F32R)
    cols, at = place('cols', [P, C * len(VECTORS)], at)
    scaled, at = place('scaled', [P, 3 * C], at)
    ident, at = place('ident', [P, P], at)
    head_sum, at = place('head_sum', [P, P], at)
    permute, at = place('permute', [P, P], at)
    centre, at = place('centre', [P, P], at)
    gather, at = place('gather', [P, 4, 32], at)
    stats, at = place('stats', [P, C, 6], at)
    moments, at = place('moments', [P, C, 2], at)
    rstd, at = place('rstd', [P, C], at)
    varep, at = place('varep', [P, C], at)
    minus_half, at = place('minus_half', [P, 32], at)
    top_common = at
    rows, at = place('rows', [P, NROWS, H], at)
    srcT, at = place('srcT', [P, C, L], at)
    v1, at = place('v1', [P, C, H], at)
    v0, _ = place('v0', [P, C, 8, 32], at - 8192)
    oT, at = place('oT', [P, C, L], at)
    probs, at = place('probs', [P, PSLOTS, C, L], at)
    xn, _ = place('xn', [P, C, H], at - 4 * PSLOTS * C * L)
    pT, at = place('pT', [P, 4, C, L], at)
    hidden, _ = place('hidden', [P, C, L], at - 4 * (4 + PSLOTS - 1) * C * L)
    hidden_hi, _ = place('hidden_hi', [P, 2, C, L], at - 4 * 4 * C * L, F32R)
    hidden_lo, _ = place('hidden_lo', [P, 2, C, L], at - 4 * 2 * C * L, F32R)
    mlp_w, _ = place('mlp_w', [P, 2, 2, C * H], at, F32R)
    qstack, at = place('qstack', [96, 2, 4, L], at, F32R)
    kstack, at = place('kstack', [96, 2, 4, L], at, F32R)
    split, at = place('split', [P, 2, L], at)
    hi, at = place('hi', [P, 4, L], at, F32R)
    lo, at = place('lo', [P, 4, L], at, F32R)
    row_max, at = place('row_max', [P, PSLOTS, C], at)
    row_sum, at = place('row_sum', [P, PSLOTS, C], at)
    row_inv, at = place('row_inv', [P, PSLOTS, C], at)
    at = top_common
    xa, at = place('xa', [P, C, L + 1], at)
    sx, at = place('sx', [P, C, L], at)
    mix, at = place('mix', [P, 4, C, L], at)
    xn2, _ = place('xn2', [P, C, H], at - 16 * C * L)
    centred, _ = place('centred', [P, C, H], at - 16 * C * L)
    squared, _ = place('squared', [P, C, H], at - 12 * C * L)
    ffn_w, _ = place('ffn_w', [P, 2, 2, C * H], at, F32R)
    act_hi, _ = place('act_hi', [P, 3, C, L], at + 4 * 4 * C * H, F32R)
    act_lo, _ = place('act_lo', [P, 4, C, L], at - 16 * C * L, F32R)
    decay, at = place('decay', [P, C, L], at)
    z, at = place('z', [32, 2, L], at)
    tdh, at = place('tdh', [64, L], at)
    kT, at = place('kT', [P, 2, L], at)
    rT, at = place('rT', [P, 2, L], at)
    vT, at = place('vT', [P, 2, L], at)
    vstack, at = place('vstack', [P, 2, 2, L], at, F32R)
    ruk, at = place('ruk', [P, L], at)
    bonus, at = place('bonus', [P, L], at)
    mixers, over = place('mixers', [96, 5 * H], at)
    mix_w, over = place('mix_w', [96, 5 * H], over, F32R)
    zstack, over = place('zstack', [96, 5, L], over, F32R)
    kvp, at = place('kvp', [P, 3, L], at)
    state, at = place('state', [P, 3, L + 1], at)
    prod, at = place('prod', [P, PRODS, L], at)
    recT, at = place('recT', [P, C, L], at)
    assert over <= at
    gT, at = place('gT', [P, C, L], at)
    pick, at = place('pick', [P, HS // 2 * P], at, F32R)
    fold, at = place('fold', [P, P // 2], at)
    s0, at = place('s0', [P, C, HS], at)
    gsum, at = place('gsum', [P, C, 32], at)
    gsq, at = place('gsq', [P, C, 32], at)
    ginv, at = place('ginv', [P, C, 32], at)

    with ExitStack() as stack:
        ps = stack.enter_context(nc.psum_tensor('ps', [P, 8, 512], F32))
        sems = {n: stack.enter_context(nc.semaphore(n)) for n in SIGNALS + LOADS + [f'w{i}' for i in range(WSLOTS)]}
        setup_in = stack.enter_context(nc.semaphore('setup_in'))
        sig = {n: Signal(sems[n], (known or {}).get(n)) for n in SIGNALS}
        ring = Ring((known or {}).get('ring'))
        S = sig
        tile_ready, act_emptied, dve_emptied = S['tile_ready'], S['act_emptied'], S['dve_emptied']
        act_done, dve_done, pool_done = S['act_done'], S['dve_done'], S['pool_done']

        def col(name, c):
            return cols[:, COL[name] + c:COL[name] + c + 1]

        with nc.Block() as block:
            @block.sync
            def _(sp):
                sp.dma_start(cols[:, :], a['cols']).then_inc(setup_in, 16)
                sp.dma_start(ident[:, :], a['ident']).then_inc(setup_in, 16)
                sp.dma_start(head_sum[:, :], a['head_sum']).then_inc(setup_in, 16)
                sp.dma_start(permute[:, :], a['permute']).then_inc(setup_in, 16)
                sp.dma_start(centre[:, :], a['centre']).then_inc(setup_in, 16)
                sp.dma_start(gather[:, :, :], a['gather']).then_inc(setup_in, 16)
                sp.wait_ge(setup_in, 16 * 6)

        with nc.Block() as block:
            @block.gpsimd
            def _(pool):
                pool.memset(minus_half[:, :], -0.5).then_inc(sems['x_stored'], 16)

            @block.vector
            def _(dve):
                for k, (n, s) in enumerate((('bq0', 0.25), ('bq1', 32.0 ** -0.5), ('bq2', 32.0 ** -0.5))):
                    dve.tensor_scalar(scaled[:, k * C:(k + 1) * C], cols[:, COL[n]:COL[n] + C], s, None, ALU.mult)

        def evac_wait(pe, label):
            if label in (act_emptied.known or {}):
                pe.wait_ge(*act_emptied.when(*label))
            else:
                pe.wait_ge(*dve_emptied.when(*label))

        def take(pe, *label):
            bank, before = ring.take(*label)
            if before is not None:
                evac_wait(pe, before)
            return ps[:, bank, :]

        uses = {b: n for n, b in enumerate(BLOCKS)}

        def weights(name):
            return wring[:, uses[name] % WSLOTS, :]

        def w_wait(pe, name):
            n = uses[name]
            pe.wait_ge(sems[f'w{n % WSLOTS}'], 16 * (n // WSLOTS + 1))

        loaded = [WSLOTS]

        def load_weights(sp, upto, freed):
            while loaded[0] <= uses[upto]:
                n = loaded[0]
                sp.wait_ge(*freed(BLOCKS[n - WSLOTS]))
                sp.dma_start(wring[:, n % WSLOTS, :], a['blocks'][n]).then_inc(sems[f'w{n % WSLOTS}'], 16)
                loaded[0] += 1

        LAST = {'kv0': ('v', 0, 3), 'q0': ('q', 0, 3), 'o0': ('out', 0, 3),
                'v1': ('v', 1, 3), 'q1': ('q', 1, 3), 'k1': ('k', 1, 3), 'o1': ('out', 1, 3),
                'v2': ('v', 2, 3), 'q2': ('q', 2, 3), 'k2': ('k', 2, 3), 'o2': ('out', 2, 3)}
        for i in range(FFN):
            LAST[f'up_{i}'] = ('up', i, 3)
        for l in (2, 3):
            LAST |= {f'small_{l}': ('decay', l, 3), f'k_{l}': ('kp', l, 3),
                     f'r_{l}': ('rp', l, 3), f'v_{l}': ('vp', l, 3), f'g_{l}': ('gp', l, 3), f'o_{l}': ('wo', l, 3),
                     f'fk_{l}': ('fk', l, 3), f'fr_{l}': ('fr', l, 3), f'fv_{l}': ('fv', l, 3)}

        MLP_ORDER = [n for n in BLOCKS if n.startswith(('up', 'down'))]
        SPLIT = {n: (mlp_w, k) for k, n in enumerate(MLP_ORDER)}
        for l in (2, 3):
            SPLIT |= {f'{n}_{l}': (ffn_w, k) for k, n in enumerate(('o', 'fk', 'fr', 'fv'))}

        def used(name):
            if name.startswith('down'):
                return S['mlp_ready'].when(name)
            return tile_ready.when(*LAST[name])

        def freed(name):
            return pool_done.when('wlo', name) if name in SPLIT else used(name)

        def w_parts(name):
            buf, k = SPLIT[name]
            return buf[:, k % 2, 0, :], buf[:, k % 2, 1, :]

        def act_w(act, name, *first):
            buf, k = SPLIT[name]
            w_wait(act, name)
            if k >= 2:
                order = MLP_ORDER if buf is mlp_w else [f'{n}_{name[-1]}' for n in ('o', 'fk', 'fr', 'fv')]
                act.wait_ge(*used(order[k - 2]))
            for w in first:
                act.wait_ge(*w)
            nc.scalar.activation(w_parts(name)[0], weights(name), ACT.Copy).then_inc(*act_done.reach('whi', name))

        def pool_w(pool, name):
            pool.wait_ge(*act_done.when('whi', name))
            high, low = w_parts(name)
            nc.gpsimd.tensor_tensor(low, weights(name), high.bitcast(F32), ALU.subtract).then_inc(*pool_done.reach('wlo', name))

        def parts_wait(pe, name):
            pe.wait_ge(*act_done.when('whi', name))
            pe.wait_ge(*pool_done.when('wlo', name))

        def three(w, src):
            return ((w[0], src[0]), (w[1], src[0]), (w[0], src[1]))

        def to_T3(pe, tile, name, src, oc, fin, ready=None):
            for fc in range(C):
                if ready is not None:
                    ready(fc)
                for k, (w, x_) in enumerate(three(w_parts(name), src)):
                    m = nc.tensor.matmul(tile, w[:, fc * H + oc * P:fc * H + (oc + 1) * P], x_[:, fc, :],
                                         start=(fc == 0 and k == 0), stop=(fc == C - 1 and k == 2))
            m.then_inc(*fin)

        def to_N3(pe, tile, name, src, tc, fin=None, ready=None, begins=True, ends=True):
            for fc in range(C):
                if ready is not None:
                    ready(fc)
                for k, (w, x_) in enumerate(three(w_parts(name), src)):
                    m = nc.tensor.matmul(tile, x_[:, fc, tc * P:(tc + 1) * P], w[:, fc * H:(fc + 1) * H],
                                         start=(begins and fc == 0 and k == 0), stop=(ends and fc == C - 1 and k == 2))
            if fin is not None:
                m.then_inc(*fin)
            return m

        def to_T(pe, tile, w, src, oc, base_=0, fin=None, fcs=range(C), ready=None):
            for fc in fcs:
                if ready is not None:
                    ready(fc)
                m = nc.tensor.matmul(tile, w[:, base_ + fc * H + oc * P:base_ + fc * H + (oc + 1) * P],
                                     src[:, fc, :], start=(fc == 0), stop=(fc == C - 1))
            if C - 1 in fcs:
                m.then_inc(*fin)

        def to_N(pe, tile, w, src, tc, n=H, base_=0, fin=None, ready=None):
            for fc in range(C):
                if ready is not None:
                    ready(fc)
                m = nc.tensor.matmul(tile[:, 0:n], src[:, fc, tc * P:(tc + 1) * P],
                                     w[:, fc * H + base_:fc * H + base_ + n], start=(fc == 0), stop=(fc == C - 1))
            m.then_inc(*fin)

        def dve_stats(dve, tag, tc):
            nc.vector.bn_stats(stats[:, tc, :], x[:, tc, :]).then_inc(*dve_done.reach('stats', tag, tc))
            dve.wait_ge(*dve_done.when('stats', tag, tc))
            nc.vector.bn_aggr(moments[:, tc, :], stats[:, tc, :]).then_inc(*dve_done.reach('moments', tag, tc))

        def dve_normalise(dve, tag, tc, out):
            dve.wait_ge(*pool_done.when('rstd', tag, tc))
            nc.vector.tensor_scalar(out[:, tc, :], x[:, tc, :], moments[:, tc, 0:1], rstd[:, tc:tc + 1],
                                    ALU.subtract, ALU.mult).then_inc(*dve_done.reach('xn', tag, tc))

        def dve_norm(dve, tag, out, before, after=None):
            for tc in range(C + 1):
                if tc < C:
                    before(tc)
                    dve_stats(dve, tag, tc)
                if tc > 0:
                    dve_normalise(dve, tag, tc - 1, out)
                    if after is not None:
                        after(tc - 1)

        def pool_norm(pool, tag, eps, tiles=range(C)):
            for tc in tiles:
                pool.wait_ge(*dve_done.when('moments', tag, tc))
                nc.gpsimd.tensor_scalar(varep[:, tc:tc + 1], moments[:, tc, 1:2], 1.0, eps, ALU.mult, ALU.add)\
                    .then_inc(*pool_done.reach('varep', tag, tc))
                pool.wait_ge(*pool_done.when('varep', tag, tc))
                nc.gpsimd.tensor_tensor(rstd[:, tc:tc + 1], varep[:, tc:tc + 1], minus_half[:, 0:1], ALU.pow)\
                    .then_inc(*pool_done.reach('rstd', tag, tc))

        def pe_turn(pe, tag, src, what, wait, matrix=None):
            for c in range(C):
                tile = take(pe, what, tag, c)
                for t in range(C):
                    wait(pe, c, t)
                    m = nc.tensor.transpose(tile[:, t * P:(t + 1) * P], src[:, t, c * P:(c + 1) * P],
                                            (ident if matrix is None else matrix)[:, :])
                m.then_inc(*tile_ready.reach(what, tag, c))

        def pe_norm_turn(pe, tag, src):
            def wait(pe, c, t):
                if c == 0:
                    pe.wait_ge(*dve_done.when('xn', tag, t))
            pe_turn(pe, tag, src, 'lnT', wait)

        def act_norm(act, tag, out, wcol, bcol, shift=0, parts=False):
            for c in range(C):
                act.wait_ge(*tile_ready.when('lnT', tag, c))
                nc.scalar.activation(out[:, c, shift:shift + L], ps[:, ring.bank('lnT', tag, c), :], ACT.Identity,
                                     bias=col(bcol, c), scale=col(wcol, c)).then_inc(*act_emptied.reach('lnT', tag, c))
                if parts:
                    act.wait_ge(*act_emptied.when('lnT', tag, c))
                    nc.scalar.activation(hi[:, c, :], out[:, c, :], ACT.Copy).then_inc(*act_done.reach('srcT_hi', c))

        class Attention:
            def __init__(self, tag, hd, groups, vcols, vblk, voff, qblk, kblk, koff, src, oblk, bq, bk, scale, mask, rowbv, rowbo):
                self.tag, self.hd, self.groups, self.vcols = tag, hd, groups, vcols
                self.vblk, self.voff, self.qblk, self.kblk, self.koff = vblk, voff, qblk, kblk, koff
                self.src, self.oblk, self.bq, self.bk, self.scale, self.mask = src, oblk, bq, bk, scale, mask
                self.kt = 3 * hd
                self.rowbv, self.rowbo = rowbv, rowbo
                self.shared = groups == 8
                self.heads = 4 * groups
                self.owner = 'adad' if self.shared else 'aaaa'

            def qi(self, g):
                return g if self.shared else g % 2

            def ki(self, g):
                return 2 + g % 2

            def parts(self, kind, g):
                if kind == 'k' and self.shared:
                    return khi0[:, :], klo0[:, :]
                idx = self.qi(g) if kind == 'q' else self.ki(g)
                return hi[:, idx, :], lo[:, idx, :]

        cross_src = ctxT
        A0 = Attention(0, 16, 8, 128, 'kv0', 128, 'q0', 'kv0', 0, cross_src, 'o0', 0, 'bk0', 0.25, maskA, 0, 1)
        A1 = Attention(1, 32, 4, 512, 'v1', 0, 'q1', 'k1', 0, srcT, 'o1', 1, 'bk1', 32.0 ** -0.5, maskB, 0, 1)
        A2 = Attention(2, 32, 4, 512, 'v2', 0, 'q2', 'k2', 0, cross_src, 'o2', 2, 'bk2', 32.0 ** -0.5, maskA, 2, 3)

        def pe_q(pe, A, g, fcs=range(C), tile=None, ready=None):
            tile = take(pe, 'q', A.tag, g) if tile is None else tile
            to_T(pe, tile, weights(A.qblk), srcT, g, fcs=fcs, ready=ready, fin=tile_ready.reach('q', A.tag, g) if C - 1 in fcs else None)
            return tile

        def pe_k(pe, A, g, fcs=range(C), tile=None, ready=None):
            label = ('k', A.tag) if A.shared else ('k', A.tag, g)
            tile = take(pe, *label) if tile is None else tile
            to_T(pe, tile, weights(A.kblk), A.src, 0 if A.shared else g, base_=A.koff, fcs=fcs, ready=ready,
                 fin=tile_ready.reach(*label) if C - 1 in fcs else None)
            return tile

        def pe_values(pe, A, tiles=range(C)):
            w_wait(pe, A.vblk)
            for tc in tiles:
                to_N(pe, take(pe, 'v', A.tag, tc), weights(A.vblk), A.src, tc, n=A.vcols, base_=A.voff,
                     fin=tile_ready.reach('v', A.tag, tc))

        def pe_queries(pe, A, chunks=None):
            w_wait(pe, A.qblk)
            if A.tag == 0:
                pe.wait_ge(sems['xT_in'], 16)
            for g in (range(4 if A.shared else 2) if chunks is None else chunks):
                pe_q(pe, A, g, ready=(lambda fc: pe.wait_ge(*act_emptied.when('lnT', f'ln{A.tag}', fc))) if A.tag > 0 and g == 0 else None)

        def pe_attention(pe, A):
            t = A.tag
            if t == 0:
                w_wait(pe, A.kblk)
                pe.wait_ge(sems['ctx_in'], 16)
                pe_k(pe, A, 0)
                pe_queries(pe, A, (0,))
                pe_values(pe, A)
                pe_queries(pe, A, (1, 2, 3))
            if t == 1:
                pe_queries(pe, A, (0,))
                w_wait(pe, A.kblk)
                pe_k(pe, A, 0)
                pe_queries(pe, A, (1,))
                pe_k(pe, A, 1)
                pe_values(pe, A)
            if t == 2:
                pe_queries(pe, A)
                pe_values(pe, A, (2, 3))
            part = None
            for n in range(A.heads + LAG + 1):
                g, i = divmod(n, 4)
                m = n - LAG
                mg, mi = divmod(m, 4)
                vg = mg - 1
                first, final = (vg % 2 == 0, vg % 2 == 1) if A.shared else (True, True)
                if n < A.heads and i == 0:
                    pe.wait_ge(sems[f'stack{g % 2}'], stack_total(A, g))
                for kc in range(C):
                    if n < A.heads:
                        if n >= 1:
                            pe.wait_ge(*S['scores_taken'].when(t, n - 1, kc))
                        nc.tensor.matmul(ps[:, kc, :], qstack[0:A.kt, g % 2, i, kc * P:(kc + 1) * P],
                                         kstack[0:A.kt, g % 2, 0 if A.shared else i, :], start=True, stop=True)\
                            .then_inc(*S['scores_ready'].reach(t, n, kc))
                    if m >= 0 and mi == 0 and vg >= 0:
                        if kc == 0:
                            if first and vg > 0:
                                pe.wait_ge(*act_done.when('context', t, (vg // 2 if A.shared else vg) - 1))
                            if vg == 0:
                                for tc in range(C):
                                    pe.wait_ge(*dve_emptied.when('v', t, tc))
                        for h in range(4):
                            evac_wait(pe, ('pT', t, 4 * vg + h, kc))
                        for h in range(4):
                            lhs = v0[:, kc, vg, :] if A.shared else v1[:, kc, (4 * vg + h) * 32:(4 * vg + h + 1) * 32]
                            ins = nc.tensor.matmul(ps[32 * h:32 * h + 32, OBANK, :], lhs, pT[:, h, kc, :],
                                                   start=(kc == 0 and first), stop=(kc == C - 1 and final))
                        ins.then_inc(*S['context_ready'].reach(t, vg, kc))
                    if 0 <= m < A.heads:
                        tile = take(pe, 'pT', t, m, kc)
                        for qc in range(C):
                            if kc == 0:
                                pe.wait_ge(*S['normalised'].when(t, m, qc))
                            ins = nc.tensor.transpose(tile[:, qc * P:(qc + 1) * P],
                                                      probs[:, m % PSLOTS, qc, kc * P:(kc + 1) * P], ident[:, :])
                        ins.then_inc(*tile_ready.reach('pT', t, m, kc))
                    if not A.shared and g + 2 < A.groups and kc < 2 and i < 2:
                        part = (pe_q, pe_k)[i](pe, A, g + 2, fcs=(2 * kc, 2 * kc + 1), tile=None if kc == 0 else part)
            w_wait(pe, A.oblk)
            for tc in range(C):
                to_N(pe, take(pe, 'out', t, tc), weights(A.oblk), oT, tc, fin=tile_ready.reach('out', t, tc),
                     ready=(lambda fc: pe.wait_ge(*act_done.when('context', t, fc))) if tc == 0 else None)

        stack_counts = {}

        def stack_total(A, g):
            return stack_counts[(A.tag, g)]

        totals = [0, 0]
        for A in (A0, A1, A2):
            for g in range(A.groups):
                totals[g % 2] += 16 * (15 if A.shared else 24)
                stack_counts[(A.tag, g)] = totals[g % 2]

        def sp_stack(sp, A, g, kinds='qk'):
            t, s = A.tag, sems[f'stack{g % 2}']

            def copy(out, in_):
                return sp.dma_start(out.bitcast(F32), in_.bitcast(F32))

            if g >= 2:
                sp.wait_ge(*S['scores_ready'].when(t, 4 * (g - 2) + 3, C - 1))
            elif t > 0:
                sp.wait_ge(*S['scores_ready'].when(t - 1, (31 if t == 1 else 15), C - 1))
            for kind in kinds:
                buf = qstack if kind == 'q' else kstack
                if not A.shared:
                    sp.wait_ge(*pool_done.when(kind + 'lo', t, g))
                elif kind == 'q':
                    sp.wait_ge(*pool_done.when('qlo', t, g // 2))
                else:
                    sp.wait_ge(*pool_done.when('klo', t, 0))
                for part, order in enumerate((0, 1, 0) if kind == 'q' else (0, 0, 1)):
                    r = part * A.hd
                    if A.shared and kind == 'k':
                        copy(buf[r:r + 16, g % 2, 0, :], (khi0, klo0)[order][16 * g:16 * g + 16, :]).then_inc(s, 16)
                        continue
                    first, idx = (64 * (g % 2), g // 2) if A.shared else (0, A.qi(g) if kind == 'q' else A.ki(g))
                    for i in range(4):
                        p0 = first + A.hd * i
                        copy(buf[r:r + A.hd, g % 2, i, :], (hi, lo)[order][p0:p0 + A.hd, idx, :]).then_inc(s, 16)

        def act_split(act, A, kind, g):
            t = A.tag
            label = ('k', t) if kind == 'k' and A.shared else (kind, t, g)
            act.wait_ge(*tile_ready.when(*label))
            prev = last_split.get(kind)
            if prev is not None:
                act.wait_ge(*pool_done.when(*prev))
            last_split[kind] = (f'{kind}lo', t, g)
            s = 0 if kind == 'q' else 1
            bias = scaled[:, t * C + g:t * C + g + 1] if kind == 'q' else col(A.bk, g)
            nc.scalar.activation(split[:, s, :], ps[:, ring.bank(*label), :], ACT.Identity, bias=bias,
                                 scale=A.scale if kind == 'q' else 1.0).then_inc(*act_emptied.reach(*label))
            if not A.shared and g >= 2:
                act.wait_ge(sems[f'stack{g % 2}'], stack_total(A, g - 2))
            act.wait_ge(*act_emptied.when(*label))
            nc.scalar.activation(A.parts(kind, g)[0], split[:, s, :], ACT.Copy).then_inc(*act_done.reach(f'{kind}hi', t, g))

        last_split = {}

        def pool_split(pool, A, kind, g):
            t, s = A.tag, 0 if kind == 'q' else 1
            high, low = A.parts(kind, g)
            pool.wait_ge(*act_done.when(f'{kind}hi', t, g))
            nc.gpsimd.tensor_tensor(low, split[:, s, :], high.bitcast(F32), ALU.subtract)\
                .then_inc(*pool_done.reach(f'{kind}lo', t, g))

        def act_attention(act, A):
            t = A.tag
            if t == 1:
                act.wait_ge(sems['stack0'], stack_total(A0, 6))
                act.wait_ge(sems['stack1'], stack_total(A0, 7))
            if A.shared:
                act_split(act, A, 'k', 0)
            for g in range(4 if A.shared else 2):
                act_split(act, A, 'q', g)
                if t == 1:
                    act_split(act, A, 'k', g)

            def empty(m, kc):
                if A.owner[kc] != 'a':
                    return
                act.wait_ge(*tile_ready.when('pT', t, m, kc))
                if m >= 4:
                    act.wait_ge(*S['context_ready'].when(t, m // 4 - 1, kc))
                nc.scalar.activation(pT[:, m % 4, kc, :], ps[:, ring.bank('pT', t, m, kc), :], ACT.Copy)\
                    .then_inc(*act_emptied.reach('pT', t, m, kc))

            def exp(n, qc):
                act.wait_ge(*S['scores_taken'].when(t, n, qc) if A.shared else dve_done.when('sm', t, n, qc))
                p = probs[:, n % PSLOTS, qc, :]
                nc.scalar.activation(p, p, ACT.Exp, bias=row_max[:, n % PSLOTS, qc:qc + 1], scale=-1.0,
                                     accum_out=row_sum[:, n % PSLOTS, qc:qc + 1]).then_inc(*S['exp_done'].reach(t, n, qc))

            for n in range(A.heads + LAG + 1):
                g, i = divmod(n, 4)
                m = n - LAG
                if m >= 5 and (m - 1) % 4 == 0 and (not A.shared or (m // 4) % 2 == 0):
                    vg = m // 4 - 1
                    c = vg // 2 if A.shared else vg
                    act.wait_ge(*S['context_ready'].when(t, vg, C - 1))
                    nc.scalar.activation(oT[:, c, :], ps[:, OBANK, :], ACT.Copy).then_inc(*act_done.reach('context', t, c))
                for step in ('e0', 'e1', 'x0', 's', 'e2', 'x1', 'e3', 'x2', 'x3'):
                    if step == 's' and not A.shared and g + 2 < A.groups and i < 2:
                        act_split(act, A, 'qk'[i], g + 2)
                    if step[0] == 'e' and 0 <= m < A.heads:
                        empty(m, int(step[1]))
                    if step[0] == 'x' and n < A.heads:
                        exp(n, int(step[1]))
            c = C - 1
            act.wait_ge(*S['context_ready'].when(t, A.groups - 1, C - 1))
            nc.scalar.activation(oT[:, c, :], ps[:, OBANK, :], ACT.Copy).then_inc(*act_done.reach('context', t, c))

        def dve_values(dve, A, tiles):
            t = A.tag
            if t < 2:
                dve.wait_ge(sems['rows_in'], 16 * (t + 1))
            for tc in tiles:
                dve.wait_ge(*tile_ready.when('v', t, tc))
                tile = ps[:, ring.bank('v', t, tc), :]
                if A.shared:
                    if tc == 0:
                        dve.wait_ge(*pool_done.when('v0', 'clear'))
                    for par in range(2):
                        o = v0[:, tc, :, :].rearrange('p (g two) d -> p two g d', two=2)[:, par, :, 16 * par:16 * par + 16]
                        i0 = tile[:, 0:128].rearrange('p (g two d) -> p two g d', two=2, d=16)[:, par, :, :]
                        i1 = rows[:, A.rowbv, 0:128].rearrange('p (g two d) -> p two g d', two=2, d=16)[:, par, :, :]
                        ins = nc.vector.tensor_tensor(o, i0, i1, ALU.add)
                    ins.then_inc(*dve_emptied.reach('v', t, tc))
                else:
                    nc.vector.tensor_tensor(v1[:, tc, :], tile, rows[:, A.rowbv, :], ALU.add)\
                        .then_inc(*dve_emptied.reach('v', t, tc))

        def dve_attention(dve, A):
            t = A.tag
            if t < 2:
                dve_values(dve, A, range(C))
            dve.wait_ge(sems['mask%d_in' % t], 16)
            if t > 0:
                dve.wait_ge(*pool_done.when('neg', t))

            def inverse(n, half):
                for qc in (2 * half, 2 * half + 1):
                    dve.wait_ge(*S['exp_done'].when(t, n, qc))
                two = slice(2 * half, 2 * half + 2)
                nc.vector.reciprocal(row_inv[:, n % PSLOTS, two], row_sum[:, n % PSLOTS, two])\
                    .then_inc(*S['inverse_done'].reach(t, n, half))

            def slot_free(n):
                if n >= PSLOTS:
                    dve.wait_ge(*tile_ready.when('pT', t, n - PSLOTS, C - 1))

            def add_max(n, qc):
                s = n % PSLOTS
                if A.shared:
                    dve.wait_ge(*S['scores_ready'].when(t, n, qc))
                    src, other, fin = ps[:, qc, :], A.mask[:, qc, :], S['scores_taken'].reach(t, n, qc)
                else:
                    dve.wait_ge(*S['scores_taken'].when(t, n, qc))
                    src, other, fin = probs[:, s, qc, :], neg[:, qc, :], dve_done.reach('sm', t, n, qc)
                nc.vector.tensor_tensor_reduce(out=probs[:, s, qc, :], in0=src, in1=other, scale=-1.0, scalar=3.0e38,
                                               op0=ALU.add, op1=ALU.min,
                                               accum_out=row_max[:, s, qc:qc + 1]).then_inc(*fin)

            def times_mask(n, qc):
                dve.wait_ge(*S['scores_ready'].when(t, n, qc))
                nc.vector.tensor_tensor(probs[:, n % PSLOTS, qc, :], ps[:, qc, :], A.mask[:, qc, :], ALU.mult)\
                    .then_inc(*S['scores_taken'].reach(t, n, qc))

            for n in range(A.heads + LAG):
                m = n - LAG
                if n < A.heads:
                    slot_free(n)
                if A.shared:
                    for qc in range(C):
                        if qc == 0 and 0 < n <= A.heads:
                            inverse(n - 1, 0)
                        if n < A.heads:
                            add_max(n, qc)
                        if qc == 1 and 0 < n <= A.heads:
                            inverse(n - 1, 1)
                        if m >= 0 and A.owner[qc] == 'd':
                            dve.wait_ge(*tile_ready.when('pT', t, m, qc))
                            if m >= 4:
                                dve.wait_ge(*S['context_ready'].when(t, m // 4 - 1, qc))
                            nc.vector.tensor_copy(pT[:, m % 4, qc, :], ps[:, ring.bank('pT', t, m, qc), :])\
                                .then_inc(*dve_emptied.reach('pT', t, m, qc))
                else:
                    for step in ('m0', 'i0', 'm1', 'a0', 'i1', 'm2', 'a1', 'm3', 'a2', 'a3'):
                        if step[0] == 'i' and 0 < n <= A.heads:
                            inverse(n - 1, int(step[1]))
                        if step[0] == 'm' and n < A.heads:
                            times_mask(n, int(step[1]))
                        if step[0] == 'a' and n < A.heads:
                            add_max(n, int(step[1]))

        def residual(dve, t, tc):
            dve.wait_ge(*pool_done.when('biased', t, tc))
            dve.wait_ge(*tile_ready.when('out', t, tc))
            nc.vector.tensor_tensor(x[:, tc, :], ps[:, ring.bank('out', t, tc), :], x[:, tc, :], ALU.add)\
                .then_inc(*dve_emptied.reach('out', t, tc))
            dve.wait_ge(*dve_emptied.when('out', t, tc))

        def pool_bias(pool, t, row, before):
            for tc in range(C):
                before(pool, tc)
                nc.gpsimd.tensor_tensor(x[:, tc, :], x[:, tc, :], rows[:, row, :], ALU.add)\
                    .then_inc(*pool_done.reach('biased', t, tc))

        def pool_attention(pool, A):
            t = A.tag
            if A.shared:
                pool_split(pool, A, 'k', 0)
            for g in range(4 if A.shared else 2):
                pool_split(pool, A, 'q', g)
                if t == 1:
                    pool_split(pool, A, 'k', g)
            for n in range(1, A.heads + 1):
                g, i = divmod(n - 1, 4)
                if not A.shared and g + 2 < A.groups:
                    if i == 1:
                        pool_split(pool, A, 'q', g + 2)
                    if i == 2:
                        pool_split(pool, A, 'k', g + 2)
                for qc in range(C):
                    pool.wait_ge(*S['inverse_done'].when(t, n - 1, qc // 2))
                    p = probs[:, (n - 1) % PSLOTS, qc, :]
                    nc.gpsimd.tensor_scalar(p, p, row_inv[:, (n - 1) % PSLOTS, qc:qc + 1], 1.0, ALU.mult, ALU.mult)\
                        .then_inc(*S['normalised'].reach(t, n - 1, qc))

        def pool_neg(pool, A):
            pool.wait_ge(sems[f'mask{A.tag}_in'], 16)
            if A.tag == 2:
                pool.wait_ge(*dve_done.when('sm', 1, 15, C - 1))
            ins = None
            for qc in range(C):
                ins = nc.gpsimd.tensor_scalar(neg[:, qc, :], A.mask[:, qc, :], -1.0, 10000.0, ALU.add, ALU.mult)
            ins.then_inc(*pool_done.reach('neg', A.tag))

        MIX_ROW = {'k': 0, 'w': 1, 'v': 2, 'r': 3, 'g': 4}
        MIX_AT = {'w': 3, 'k': 0, 'v': 1, 'r': 2, 'g': 3}

        HI_AT = {'xk2': 0, 'xr2': 1, 'gated': 2, 'kk': 2}

        def mix_wait(eng, l, name, c):
            eng.wait_ge(*(dve_done if c == C - 1 and name != 'g' else pool_done).when('mix', l, name, c))

        def pe_rwkv(pe, l):
            pe_norm_turn(pe, f'a{l}', xn2)
            w_wait(pe, f'small_{l}')
            small = weights(f'small_{l}')
            for part, (n0, rows_) in enumerate(((0, 128), (128, 32))):
                tile = ps[:, part, :]
                for fc in range(C):
                    if part == 0:
                        pe.wait_ge(*dve_done.when('xin', l, fc))
                    m = nc.tensor.matmul(tile[0:rows_, :], small[:, SMALL_MAA + fc * 160 + n0:SMALL_MAA + fc * 160 + n0 + rows_],
                                         mix[:, 2, fc, :], start=(fc == 0), stop=(fc == C - 1))
                m.then_inc(*tile_ready.reach('z', l, part))
            pe.wait_ge(*pool_done.when('mix_w', l))

            def mixing(name, c):
                f = MIX_ROW[name]
                if c == 0:
                    pe.wait_ge(*dve_done.when('z_lo', l, name))
                    pe.wait_ge(*(act_emptied.when('z', l, int(f == 4)) if name in 'rg' else act_done.when('z_hi2', l, name)))
                tile = take(pe, 'mix', l, name, c)
                nc.tensor.matmul(tile, mix_w[0:96, f * H + c * P:f * H + (c + 1) * P], zstack[0:96, f, :],
                                 start=True, stop=True).then_inc(*tile_ready.reach('mix', l, name, c))

            def project(hg, name, fcs=range(C), tile=None):
                if hg == 0:
                    w_wait(pe, f'{name}_{l}')
                tile = take(pe, f'{name}p', l, hg) if tile is None else tile
                to_T(pe, tile, weights(f'{name}_{l}'), mix[:, MIX_AT[name]], hg, fcs=fcs,
                     fin=tile_ready.reach(f'{name}p', l, hg) if C - 1 in fcs else None,
                     ready=(lambda fc: mix_wait(pe, l, name, fc)) if hg == 0 else None)
                return tile

            for name in 'kw':
                for c in range(C):
                    mixing(name, c)
            project(0, 'k')
            for c in range(C):
                mixing('v', c)
            tile = take(pe, 'td', l)
            for fc in range(C):
                mix_wait(pe, l, 'w', fc)
                m = nc.tensor.matmul(tile[0:64, :], small[:, SMALL_TD1 + fc * 64:SMALL_TD1 + (fc + 1) * 64],
                                     mix[:, MIX_AT['w'], fc, :], start=(fc == 0), stop=(fc == C - 1))
            m.then_inc(*tile_ready.reach('td', l))
            for c in range(C):
                mixing('r', c)
            pe.wait_ge(*act_emptied.when('td', l))
            for c in range(C):
                tile = take(pe, 'decay', l, c)
                nc.tensor.matmul(tile, small[0:64, SMALL_TD2 + c * P:SMALL_TD2 + (c + 1) * P], tdh[:, :],
                                 start=True, stop=True).then_inc(*tile_ready.reach('decay', l, c))
            project(0, 'v')
            project(0, 'r')
            for c in range(C):
                mixing('g', c)

            def bonus_sum(hg):
                pe.wait_ge(*dve_done.when('ruk', l, hg))
                tile = take(pe, 'bonus', l, hg)
                nc.tensor.matmul(tile, head_sum[:, :], ruk[:, :], start=True, stop=True)\
                    .then_inc(*tile_ready.reach('bonus', l, hg))

            def gate(c, fc, tile):
                if (c, fc) == (0, 0):
                    w_wait(pe, f'g_{l}')
                tile = take(pe, 'gp', l, c) if fc == 0 else tile
                to_T(pe, tile, weights(f'g_{l}'), mix[:, MIX_AT['g']], c, fcs=(fc,),
                     fin=tile_ready.reach('gp', l, c) if fc == C - 1 else None,
                     ready=(lambda fc: mix_wait(pe, l, 'g', fc)) if c == 0 else None)
                return tile

            def reduce(group):
                hg, m = divmod(group, HS // 4)
                if m == 0 and hg > 0:
                    pe.wait_ge(*act_done.when('rec', l, hg - 1))
                pe.wait_ge(*pool_done.when('prod', l, 4 * group + 3))
                for jj in range(4):
                    ins = nc.tensor.matmul(ps[32 * jj:32 * jj + 32, OBANK, :], gather[:, m, :], prod[:, (4 * group + jj) % PRODS, :],
                                           start=(m == 0), stop=False, skip_group_check=True)
                ins.then_inc(*S['reduced'].reach(l, group))
                if m == HS // 4 - 1:
                    pe.wait_ge(*dve_emptied.when('bonus', l, hg))
                    nc.tensor.matmul(ps[:, OBANK, :], permute[:, :], bonus[:, :], start=False, stop=True,
                                     skip_group_check=True).then_inc(*S['context_ready'].reach('rec', l, hg))

            def centring(c):
                pe.wait_ge(*act_done.when('rec', l, c))
                for tc in range(C):
                    if c == 0:
                        pe.wait_ge(*S['scores_taken'].when('kv', l, C * HS - C + tc))
                    m = nc.tensor.matmul(ps[:, tc, c * P:(c + 1) * P], recT[:, c, tc * P:(tc + 1) * P], centre[:, :],
                                         start=True, stop=True)
                    if c == C - 1:
                        m.then_inc(*S['vb_ready'].reach('centred', l, tc))

            part = None
            lag = WKV_LAG
            for t in range(C * HS + lag):
                hg, j = divmod(t, HS)
                if t < C * HS:
                    if j in (0, HS // 2):
                        pe.wait_ge(*dve_done.when('vlo', l, hg, j // (HS // 2)))
                    if t >= 4:
                        pe.wait_ge(*S['scores_taken'].when('kv', l, t - 4))
                    half, jh = divmod(j, HS // 2)
                    nc.tensor.matmul(ps[:, t % 4, :], pick[:, jh * P:(jh + 1) * P], vstack[:, hg % 2, half, :],
                                     start=True, stop=True)\
                        .then_inc(*S['vb_ready'].reach(l, t))
                    if hg + 1 < C and 1 <= j <= 12:
                        fc = (j - 1) % 4
                        part = project(hg + 1, 'kvr'[(j - 1) // 4], (fc,), None if fc == 0 else part)
                    if j == 3:
                        bonus_sum(hg)
                    if hg == C - 1:
                        part = gate(j // 4, j % 4, part)
                if t == C * HS + lag - 1:
                    for c in range(C - 1):
                        centring(c)
                if t >= lag and (t - lag) % 4 == 3:
                    reduce((t - lag) // 4)
            centring(C - 1)

            def wait(pe, c, t):
                if c == 0:
                    pe.wait_ge(*dve_done.when('gn', l, t))
            pe_turn(pe, l, centred, 'gnT', wait)
            parts_wait(pe, f'o_{l}')
            for tc in range(C):
                to_N3(pe, take(pe, 'wo', l, tc), f'o_{l}', (act_hi[:, 2], act_lo[:, 2]), tc, tile_ready.reach('wo', l, tc),
                      ready=(lambda fc: pe.wait_ge(*dve_done.when('gated_lo', l, fc))) if tc == 0 else None)
            pe_norm_turn(pe, f'f{l}', xn2)
            parts_wait(pe, f'fk_{l}')
            for c in range(C):
                to_T3(pe, take(pe, 'fk', l, c), f'fk_{l}', (act_hi[:, 0], act_lo[:, 1]), c, tile_ready.reach('fk', l, c),
                      ready=(lambda fc: pe.wait_ge(*dve_done.when('xk2_lo', l, fc))) if c == 0 else None)
            parts_wait(pe, f'fr_{l}')
            for tc in range(C):
                to_N3(pe, take(pe, 'fr', l, tc), f'fr_{l}', (act_hi[:, 1], act_lo[:, 2]), tc, tile_ready.reach('fr', l, tc),
                      ready=(lambda fc: pe.wait_ge(*dve_done.when('xr2_lo', l, fc))) if tc == 0 else None)
            parts_wait(pe, f'fv_{l}')
            for tc in range(C):
                to_N3(pe, take(pe, 'fv', l, tc), f'fv_{l}', (act_hi[:, 2], act_lo[:, 3]), tc, tile_ready.reach('fv', l, tc),
                      ready=(lambda fc: pe.wait_ge(*dve_done.when('kk_lo', l, fc))) if tc == 0 else None)

        def dve_rwkv(dve, l):
            def shift_mix(tag, mixes, then=None):
                def shift(c):
                    dve.wait_ge(*act_emptied.when('lnT', tag, c))
                    if c % 2:
                        dve.wait_ge(*pool_done.when('sx', tag, c))
                        return
                    if c == 0:
                        dve.wait_ge(*pool_done.when('prev', tag))
                    nc.vector.tensor_tensor(sx[:, c, :], xa[:, c, 0:L], xa[:, c, 1:L + 1], ALU.subtract)\
                        .then_inc(*dve_done.reach('sx', tag, c))

                for k, (at_, name, out_label) in enumerate(mixes):
                    for c in range(C + 1):
                        if c < C:
                            if k == 0:
                                shift(c)
                                if c % 2 == 0:
                                    dve.wait_ge(*dve_done.when('sx', tag, c))
                            nc.vector.scalar_tensor_tensor(mix[:, at_, c, :], sx[:, c, :], col(f'{name}_{l}', c),
                                                           xa[:, c, 1:L + 1], ALU.mult, ALU.add)\
                                .then_inc(*dve_done.reach(out_label, l, c))
                        if c > 0 and then is not None:
                            then(out_label, c - 1, at_)

            shift_mix(f'a{l}', ((2, 'maa_x', 'xin'),))

            if l == 2:
                dve.wait_ge(sems['fold_in'], 16)
                nc.vector.tensor_copy(pick[:, :].rearrange('p (j h i) -> p j h i', j=HS // 2, h=HEADS),
                                      fold[:, :].rearrange('p (j h) -> p j h', h=HEADS).unsqueeze(3)
                                      .to_broadcast([P, HS // 2, HEADS, HS])).then_inc(*dve_done.reach('pick'))
                dve.wait_ge(*dve_done.when('pick'))

            def mixed(name, chunks=range(C)):
                for c in chunks:
                    dve.wait_ge(*tile_ready.when('mix', l, name, c))
                    if name == 'r':
                        dve.wait_ge(*tile_ready.when('z', l, 1))
                    if name == 'g':
                        dve.wait_ge(*tile_ready.when('td', l))
                    nc.vector.scalar_tensor_tensor(mix[:, MIX_AT[name], c, :], ps[:, ring.bank('mix', l, name, c), :],
                                                   col(f'maa_{name}_{l}', c), sx[:, c, :], ALU.add, ALU.mult)\
                        .then_inc(*dve_emptied.reach('mix', l, name, c))
                    if c == C - 1 and name != 'g':
                        dve.wait_ge(*dve_emptied.when('mix', l, name, c))
                        m = mix[:, MIX_AT[name], c, :]
                        nc.vector.tensor_tensor(m, m, xa[:, c, 1:L + 1], ALU.add).then_inc(*dve_done.reach('mix', l, name, c))

            def z_low(name):
                dve.wait_ge(*act_done.when('z_hi', l, name))
                nc.vector.tensor_tensor(zstack[32:64, MIX_ROW[name], :], z[:, 'kwvrg'.index(name) % 2, :],
                                        zstack[0:32, MIX_ROW[name], :].bitcast(F32), ALU.subtract)\
                    .then_inc(*dve_done.reach('z_lo', l, name))

            z_low('k')
            z_low('w')
            mixed('k')
            z_low('v')
            mixed('w')
            z_low('r')
            z_low('g')
            for name in 'vr':
                mixed(name)

            def values_in(hg):
                s = hg % 2
                dve.wait_ge(*act_done.when('vhi', l, hg, 1))
                if hg >= 2:
                    dve.wait_ge(*S['vb_ready'].when(l, HS * (hg - 1) - 1))
                nc.vector.tensor_tensor(vstack[64:128, s, 0, :], vT[0:64, s, :], vstack[0:64, s, 0, :].bitcast(F32), ALU.subtract)\
                    .then_inc(*dve_done.reach('vlo', l, hg, 0))
                nc.vector.tensor_tensor(vstack[0:64, s, 1, :], vT[64:128, s, :], vstack[64:128, s, 1, :].bitcast(F32), ALU.subtract)\
                    .then_inc(*dve_done.reach('vlo', l, hg, 1))

            def receptance_in(hg):
                s = hg % 2
                dve.wait_ge(*act_emptied.when('rp', l, hg))
                dve.wait_ge(*act_emptied.when('kp', l, hg))
                if hg >= 1:
                    dve.wait_ge(*tile_ready.when('bonus', l, hg - 1))
                nc.vector.scalar_tensor_tensor(ruk[:, :], rT[:, s, :], col(f'u_{l}', hg), kT[:, s, :], ALU.mult, ALU.mult)\
                    .then_inc(*dve_done.reach('ruk', l, hg))

            def bonus_out(hg):
                dve.wait_ge(*tile_ready.when('bonus', l, hg))
                if hg >= 1:
                    dve.wait_ge(*S['context_ready'].when('rec', l, hg - 1))
                nc.vector.tensor_tensor(bonus[:, :], ps[:, ring.bank('bonus', l, hg), :], vT[:, hg % 2, :], ALU.mult)\
                    .then_inc(*dve_emptied.reach('bonus', l, hg))

            values_in(0)
            mixed('g')
            receptance_in(0)
            dve.wait_ge(*act_done.when('w', l, C - 1))
            dve.wait_ge(sems['s0_in'], 16)
            n = C * HS
            for t in range(n + 1):
                hg, j = divmod(t, HS)
                if t < n:
                    dve.wait_ge(*S['vb_ready'].when(l, t))
                    if t >= 3:
                        dve.wait_ge(*dve_done.when('scan', l, t - 3))
                    nc.vector.tensor_tensor(kvp[:, t % 3, :], kT[:, hg % 2, :], ps[:, t % 4, :], ALU.mult)\
                        .then_inc(*S['scores_taken'].reach('kv', l, t))
                if t >= 1:
                    u = t - 1
                    ug, uj = divmod(u, HS)
                    dve.wait_ge(*S['scores_taken'].when('kv', l, u))
                    if u >= 3:
                        dve.wait_ge(*pool_done.when('prod', l, u - 3))
                    nc.vector.tensor_tensor_scan(state[:, u % 3, 1:L + 1], decay[:, ug, :], kvp[:, u % 3, :],
                                                 s0[:, ug, uj:uj + 1], ALU.mult, ALU.add)\
                        .then_inc(*dve_done.reach('scan', l, u))
                if t < n and j == 6:
                    bonus_out(hg)
                if t < n and j == 10 and hg + 1 < C:
                    values_in(hg + 1)
                if t < n and j == 13 and hg + 1 < C:
                    receptance_in(hg + 1)
            def heads(ap):
                return ap.rearrange('p (h j) -> p h j', j=HS)

            def wide(ap):
                return ap.unsqueeze(2).to_broadcast([P, 32, HS])

            for tc in range(C):
                dve.wait_ge(*act_done.when('gsq', l, tc))
                nc.vector.tensor_reduce(gsq[:, tc, :], heads(squared[:, tc, :]), AX.X, ALU.add)\
                    .then_inc(*dve_done.reach('gsq', l, tc))
            def small_step(what, *before):
                for w in before:
                    dve.wait_ge(*w)
                return dve_done.reach(what, l)

            fin = small_step('gvar', *(dve_done.when('gsq', l, tc) for tc in range(C)))
            nc.vector.tensor_scalar(gsq[:, :, :], gsq[:, :, :], 1.0 / HS, 1e-5, ALU.mult, ALU.add).then_inc(*fin)
            fin = small_step('root_inverse', act_done.when('root', l))
            nc.vector.reciprocal(ginv[:, :, :], gsum[:, :, :]).then_inc(*fin)
            fin = small_step('root_other', dve_done.when('root_inverse', l))
            nc.vector.tensor_tensor(ginv[:, :, :], gsq[:, :, :], ginv[:, :, :], ALU.mult).then_inc(*fin)
            fin = small_step('root_twice', dve_done.when('root_other', l))
            nc.vector.tensor_tensor(ginv[:, :, :], ginv[:, :, :], gsum[:, :, :], ALU.add).then_inc(*fin)
            fin = small_step('ginv', dve_done.when('root_twice', l))
            nc.vector.reciprocal(ginv[:, :, :], ginv[:, :, :]).then_inc(*fin)
            dve.wait_ge(*dve_done.when('ginv', l))
            for tc in range(C):
                nc.vector.scalar_tensor_tensor(heads(centred[:, tc, :]), heads(ps[:, tc, :]), 2.0, wide(ginv[:, tc, :]),
                                               ALU.mult, ALU.mult).then_inc(*dve_done.reach('gn', l, tc))
            def low_part(name, c, place_):
                dve.wait_ge(*act_done.when(name + '_hi', l, c))
                nc.vector.tensor_tensor(act_lo[:, place_, c, :], mix[:, place_, c, :],
                                        act_hi[:, HI_AT[name], c, :].bitcast(F32), ALU.subtract)\
                    .then_inc(*dve_done.reach(name + '_lo', l, c))

            for c in range(C + 1):
                if c < C:
                    dve.wait_ge(*act_emptied.when('gnT', l, c))
                    dve.wait_ge(*act_emptied.when('gp', l, c))
                    nc.vector.tensor_tensor(mix[:, 2, c, :], squared[:, c, :], gT[:, c, :], ALU.mult)\
                        .then_inc(*dve_done.reach('gated', l, c))
                if c > 0:
                    low_part('gated', c - 1, 2)

            def add_wo(tc):
                dve.wait_ge(*tile_ready.when('wo', l, tc))
                nc.vector.tensor_tensor(x[:, tc, :], ps[:, ring.bank('wo', l, tc), :], x[:, tc, :], ALU.add)\
                    .then_inc(*dve_emptied.reach('wo', l, tc))
                dve.wait_ge(*dve_emptied.when('wo', l, tc))

            dve_norm(dve, f'f{l}', xn2, add_wo)
            shift_mix(f'f{l}', ((1, 'ffn_k', 'xk2'), (2, 'ffn_r', 'xr2')), low_part)
            for c in range(C):
                low_part('kk', c, 3)
            def add_ffn(tc):
                dve.wait_ge(*act_emptied.when('fr', l, tc))
                dve.wait_ge(*tile_ready.when('fv', l, tc))
                nc.vector.tensor_tensor(recT[:, tc, :], ps[:, ring.bank('fv', l, tc), :], gT[:, tc, :], ALU.mult)\
                    .then_inc(*dve_emptied.reach('fv', l, tc))
                dve.wait_ge(*dve_emptied.when('fv', l, tc))
                nc.vector.tensor_tensor(x[:, tc, :], x[:, tc, :], recT[:, tc, :], ALU.add)\
                    .then_inc(*dve_done.reach('x', l, tc))
                dve.wait_ge(*dve_done.when('x', l, tc))

            if l == 2:
                dve_norm(dve, 'a3', xn2, add_ffn)
            else:
                for tc in range(C):
                    add_ffn(tc)

        def act_rwkv(act, l):
            act_norm(act, f'a{l}', xa, f'ln1_w_{l}', f'ln1_b_{l}', shift=1)
            act.wait_ge(sems['mixers_in'], 16 * (l - 1))
            nc.scalar.activation(mix_w[:, :], mixers[:, :], ACT.Copy).then_inc(*act_done.reach('mix_w', l))
            for k, name in enumerate('kwvrg'):
                f = MIX_ROW[name]
                part, row = (0, 32 * f) if f < 4 else (1, 0)
                act.wait_ge(*tile_ready.when('z', l, part))
                src = ps[row:row + 32, part, :]
                if k >= 2:
                    act.wait_ge(*dve_done.when('z_lo', l, 'kwvrg'[k - 2]))
                nc.scalar.activation(z[:, k % 2, :], src, ACT.Tanh).then_inc(*act_done.reach('z', l, name))
                nc.scalar.activation(zstack[0:32, f, :], src, ACT.Tanh).then_inc(*act_done.reach('z_hi', l, name))
                fin = act_emptied.reach('z', l, part) if name in 'rg' else act_done.reach('z_hi2', l, name)
                nc.scalar.activation(zstack[64:96, f, :], src, ACT.Tanh).then_inc(*fin)
            def heads_in(hg, names=('k', 'v', 'r')):
                s = hg % 2
                for name in names:
                    out = {'k': kT, 'v': vT, 'r': rT}[name]
                    act.wait_ge(*tile_ready.when(f'{name}p', l, hg))
                    if hg >= 2:
                        act.wait_ge(*pool_done.when('prod', l, HS * (hg - 1) - 1))
                        act.wait_ge(*dve_emptied.when('bonus', l, hg - 2))
                    nc.scalar.activation(out[:, s, :], ps[:, ring.bank(f'{name}p', l, hg), :], ACT.Copy)\
                        .then_inc(*act_emptied.reach(f'{name}p', l, hg))
                    if name == 'v':
                        act.wait_ge(*act_emptied.when('vp', l, hg))
                        if hg >= 2:
                            act.wait_ge(*S['vb_ready'].when(l, HS * (hg - 1) - 1))
                        for half in range(2):
                            rows_ = slice(64 * half, 64 * half + 64)
                            nc.scalar.activation(vstack[rows_, s, half, :], vT[rows_, s, :], ACT.Copy)\
                                .then_inc(*act_done.reach('vhi', l, hg, half))

            heads_in(0, 'k')
            act.wait_ge(*tile_ready.when('td', l))
            nc.scalar.activation(tdh[:, :], ps[0:64, ring.bank('td', l), :], ACT.Tanh).then_inc(*act_emptied.reach('td', l))
            for c in range(C):
                act.wait_ge(*tile_ready.when('decay', l, c))
                nc.scalar.activation(decay[:, c, :], ps[:, ring.bank('decay', l, c), :], ACT.Exp, bias=col(f'decay_{l}', c))\
                    .then_inc(*act_emptied.reach('decay', l, c))
            heads_in(0, 'v')
            for c in range(C):
                act.wait_ge(*act_emptied.when('decay', l, c))
                nc.scalar.activation(decay[:, c, :], decay[:, c, :], ACT.Exp, scale=-1.0).then_inc(*act_done.reach('w', l, c))

            heads_in(0, 'r')
            act.wait_ge(sems['s0_in'], 16)
            for t in range(C * HS):
                hg, j = divmod(t, HS)
                if t >= 3:
                    act.wait_ge(*pool_done.when('prod', l, t - 3))
                nc.scalar.activation(state[:, t % 3, 0:1], s0[:, hg, j:j + 1], ACT.Copy).then_inc(*act_done.reach('s0', l, t))
                if j in (5, 9, 13) and hg + 1 < C:
                    heads_in(hg + 1, 'kvr'[j // 4 - 1])
                if j == 6 and hg > 0:
                    act.wait_ge(*S['context_ready'].when('rec', l, hg - 1))
                    nc.scalar.activation(recT[:, hg - 1, :], ps[:, OBANK, :], ACT.Copy).then_inc(*act_done.reach('rec', l, hg - 1))
                if hg == C - 1 and j % 4 == 3:
                    c = j // 4
                    act.wait_ge(*tile_ready.when('gp', l, c))
                    nc.scalar.activation(gT[:, c, :], ps[:, ring.bank('gp', l, c), :], ACT.Silu)\
                        .then_inc(*act_emptied.reach('gp', l, c))
            act.wait_ge(*S['context_ready'].when('rec', l, C - 1))
            nc.scalar.activation(recT[:, C - 1, :], ps[:, OBANK, :], ACT.Copy).then_inc(*act_done.reach('rec', l, C - 1))

            def high_part(name, c, place_, ready):
                act.wait_ge(*ready)
                nc.scalar.activation(act_hi[:, HI_AT[name], c, :], mix[:, place_, c, :], ACT.Copy)\
                    .then_inc(*act_done.reach(name + '_hi', l, c))

            act_w(act, f'o_{l}')
            for tc in range(C):
                act.wait_ge(*S['vb_ready'].when('centred', l, tc))
                nc.scalar.activation(squared[:, tc, :], ps[:, tc, :], ACT.Square).then_inc(*act_done.reach('gsq', l, tc))
            act.wait_ge(*dve_done.when('gvar', l))
            nc.scalar.activation(gsum[:, :, :], gsq[:, :, :], ACT.Sqrt).then_inc(*act_done.reach('root', l))
            act_w(act, f'fk_{l}')
            for c in range(C + 1):
                if c < C:
                    act.wait_ge(*tile_ready.when('gnT', l, c))
                    nc.scalar.activation(squared[:, c, :], ps[:, ring.bank('gnT', l, c), :], ACT.Identity,
                                         bias=col(f'gn_b_{l}', c), scale=col(f'gn_w_{l}', c))\
                        .then_inc(*act_emptied.reach('gnT', l, c))
                if c > 0:
                    high_part('gated', c - 1, 2, dve_done.when('gated', l, c - 1))
            act_norm(act, f'f{l}', xa, f'ln2_w_{l}', f'ln2_b_{l}', shift=1)
            for c in range(C):
                high_part('xk2', c, 1, dve_done.when('xk2', l, c))
            act_w(act, f'fr_{l}')
            for c in range(C):
                high_part('xr2', c, 2, dve_done.when('xr2', l, c))
            for c in range(C):
                act.wait_ge(*tile_ready.when('fk', l, c))
                nc.scalar.activation(mix[:, 3, c, :], ps[:, ring.bank('fk', l, c), :], ACT.Relu)\
                    .then_inc(*act_emptied.reach('fk', l, c))
                act.wait_ge(*act_emptied.when('fk', l, c))
                nc.scalar.activation(mix[:, 3, c, :], mix[:, 3, c, :], ACT.Square).then_inc(*act_done.reach('kk', l, c))
                high_part('kk', c, 3, act_done.when('kk', l, c))
            act_w(act, f'fv_{l}')
            for tc in range(C):
                act.wait_ge(*tile_ready.when('fr', l, tc))
                nc.scalar.activation(gT[:, tc, :], ps[:, ring.bank('fr', l, tc), :], ACT.Sigmoid)\
                    .then_inc(*act_emptied.reach('fr', l, tc))

        def pool_rwkv(pool, l):
            def previous(tag, token):
                nc.gpsimd.tensor_copy(xa[:, :, 0:1], ctxT[:, :, token:token + 1]).then_inc(*pool_done.reach('prev', tag))
                pool.wait_ge(*pool_done.when('prev', tag))
                for c in (1, 3):
                    pool.wait_ge(*act_emptied.when('lnT', tag, c))
                    nc.gpsimd.tensor_tensor(sx[:, c, :], xa[:, c, 0:L], xa[:, c, 1:L + 1], ALU.subtract)\
                        .then_inc(*pool_done.reach('sx', tag, c))

            pool_norm(pool, f'a{l}', 1e-5)
            previous(f'a{l}', 1)
            pool.wait_ge(*pool_done.when('sx', f'a{l}', 3))
            pool.wait_ge(*act_done.when('mix_w', l))
            nc.gpsimd.tensor_tensor(mix_w[64:96, :], mixers[64:96, :], mix_w[64:96, :].bitcast(F32), ALU.subtract)\
                .then_inc(*pool_done.reach('mix_w', l))

            def add_xa(name, c):
                pool.wait_ge(*dve_emptied.when('mix', l, name, c))
                m = mix[:, MIX_AT[name], c, :]
                nc.gpsimd.tensor_tensor(m, m, xa[:, c, 1:L + 1], ALU.add).then_inc(*pool_done.reach('mix', l, name, c))

            for name in 'kwvr':
                for c in range(C - 1):
                    add_xa(name, c)
            for t in range(C * HS):
                hg, j = divmod(t, HS)
                pool.wait_ge(*dve_done.when('scan', l, t))
                pool.wait_ge(*act_done.when('s0', l, t))
                if t >= PRODS:
                    pool.wait_ge(*S['reduced'].when(l, (t - PRODS) // 4))
                nc.gpsimd.tensor_tensor(prod[:, t % PRODS, :], state[:, t % 3, 0:L], rT[:, hg % 2, :], ALU.mult)\
                    .then_inc(*pool_done.reach('prod', l, t))
                if hg == 0 and j >= 12:
                    add_xa('g', j - 12)
            pool_w(pool, f'o_{l}')
            pool_w(pool, f'fk_{l}')
            pool_norm(pool, f'f{l}', 1e-5)
            previous(f'f{l}', 0)
            pool_w(pool, f'fr_{l}')
            pool_w(pool, f'fv_{l}')

        AHEAD = ['ctx_in', 'mask0_in', 'xT_in'] + [f'w{n}' for n in range(WSLOTS)]

        def ahead(sp, name, index, clear=True):
            if clear:
                sp.sem_clear(sems[name])
            if name[0] == 'w':
                n = int(name[1])
                sp.dma_start(wring[:, n, :], a['blocks'][n]).then_inc(sems[name], 16)
                return
            src, dst = {'ctx_in': ('ctxT', ctxT), 'mask0_in': ('mask0', maskA), 'xT_in': ('xT', srcT)}[name]
            sp.dma_start(dst[:, :, :], a[src][index].rearrange('(c p) t -> p c t', p=P)).then_inc(sems[name], 16)

        with nc.Block() as block:
            @block.sync
            def _(sp):
                for name in ('w0', 'ctx_in', 'xT_in', 'w1', 'mask0_in', 'w2'):
                    ahead(sp, name, 0, clear=False)
                sp.dma_start(maskB[:, :, :], a['mask1'].rearrange('(c p) t -> p c t', p=P)).then_inc(sems['mask1_in'], 16)

        with nc.Fori(0, samples) as b:
            with nc.Block() as block:
                @block.gpsimd
                def _(pool):
                    for n, s in sems.items():
                        if n not in AHEAD + ['mask1_in', 'x_stored']:
                            nc.gpsimd.sem_clear(s)

            with nc.Block() as block:
                @block.tensor
                def _(pe):
                    pe_attention(pe, A0)
                    pe_norm_turn(pe, 'ln1', xn)
                    pe_attention(pe, A1)
                    w_wait(pe, A2.kblk)
                    pe_k(pe, A2, 0)
                    pe_k(pe, A2, 1)
                    pe_values(pe, A2, (0, 1))
                    pe_norm_turn(pe, 'ln2', xn)
                    pe_attention(pe, A2)
                    pe_norm_turn(pe, 'ln3', xn)
                    def up(i):
                        parts_wait(pe, f'up_{i}')
                        for c in range(C):
                            to_T3(pe, take(pe, 'up', i, c), f'up_{i}', (hi, lo), c, tile_ready.reach('up', i, c),
                                  ready=(lambda fc: pe.wait_ge(*dve_done.when('srcT_lo', fc))) if (i, c) == (0, 0) else None)

                    def down(i):
                        parts_wait(pe, f'down_{i}')
                        src = hidden_hi[:, i % 2], hidden_lo[:, i % 2]
                        for tc in range(C):
                            m = to_N3(pe, ps[:, tc, :], f'down_{i}', src, tc, begins=(i == 0), ends=(i == FFN - 1),
                                      ready=(lambda fc: pe.wait_ge(*dve_done.when('hidden_lo', i, fc))) if tc == 0 else None)
                            if i == FFN - 1 and tc < C - 1:
                                m.then_inc(*S['mlp_ready'].reach('tile', tc))
                        m.then_inc(*S['mlp_ready'].reach(f'down_{i}'))

                    up(0)
                    for i in range(1, FFN):
                        up(i)
                        down(i - 1)
                    down(FFN - 1)
                    for l in (2, 3):
                        pe_rwkv(pe, l)

                @block.scalar
                def _(act):
                    act_attention(act, A0)
                    act_norm(act, 'ln1', srcT, 'ln1_s', 'ln1_b')
                    act_attention(act, A1)
                    act.wait_ge(sems['stack0'], stack_total(A1, 2))
                    act.wait_ge(sems['stack1'], stack_total(A1, 3))
                    act_split(act, A2, 'k', 0)
                    act_split(act, A2, 'k', 1)
                    act_norm(act, 'ln2', srcT, 'ln2_s', 'ln2_b')
                    act_attention(act, A2)
                    act_w(act, 'up_0', S['scores_ready'].when(2, 15, C - 1))
                    act_norm(act, 'ln3', srcT, 'ln3_s', 'ln3_b', parts=True)
                    act_w(act, 'up_1')
                    for k, name in enumerate(MLP_ORDER):
                        if name.startswith('up'):
                            i = int(name[-1])
                            for c in range(C):
                                act.wait_ge(*tile_ready.when('up', i, c))
                                if i >= 1:
                                    act.wait_ge(*dve_done.when('hidden_lo', i - 1, c))
                                nc.scalar.activation(hidden[:, c, :], ps[:, ring.bank('up', i, c), :],
                                                     ACT.Gelu_apprx_tanh, bias=col(f'b1_{i}', c))\
                                    .then_inc(*act_emptied.reach('up', i, c))
                                act.wait_ge(*act_emptied.when('up', i, c))
                                if i >= 2:
                                    act.wait_ge(*S['mlp_ready'].when(f'down_{i - 2}'))
                                nc.scalar.activation(hidden_hi[:, i % 2, c, :], hidden[:, c, :], ACT.Copy)\
                                    .then_inc(*act_done.reach('hidden_hi', i, c))
                        if k + 2 < len(MLP_ORDER):
                            act_w(act, MLP_ORDER[k + 2])
                    for l in (2, 3):
                        act_rwkv(act, l)

                @block.vector
                def _(dve):
                    dve_attention(dve, A0)
                    def affine(tc):
                        dve.wait_ge(*dve_done.when('xn', 'ln0', tc))
                        nc.vector.tensor_tensor(xn[:, tc, :], xn[:, tc, :], rows[:, 2, :], ALU.mult)\
                            .then_inc(*dve_done.reach('gamma', tc))

                    dve_norm(dve, 'ln0', xn, lambda tc: residual(dve, 0, tc), affine)
                    dve_norm(dve, 'ln1', xn, lambda tc: dve.wait_ge(*pool_done.when('x0', tc)))
                    dve_attention(dve, A1)

                    dve_norm(dve, 'ln2', xn, lambda tc: residual(dve, 1, tc))
                    dve_values(dve, A2, range(C))
                    dve_attention(dve, A2)
                    dve_norm(dve, 'ln3', xn, lambda tc: residual(dve, 2, tc))
                    for c in range(C):
                        dve.wait_ge(*act_done.when('srcT_hi', c))
                        nc.vector.tensor_tensor(lo[:, c, :], srcT[:, c, :], hi[:, c, :].bitcast(F32), ALU.subtract)\
                            .then_inc(*dve_done.reach('srcT_lo', c))
                    for i in range(FFN):
                        for c in range(C):
                            dve.wait_ge(*act_done.when('hidden_hi', i, c))
                            nc.vector.tensor_tensor(hidden_lo[:, i % 2, c, :], hidden[:, c, :],
                                                    hidden_hi[:, i % 2, c, :].bitcast(F32), ALU.subtract)\
                                .then_inc(*dve_done.reach('hidden_lo', i, c))

                    def add_mlp(tc):
                        dve.wait_ge(*(S['mlp_ready'].when('tile', tc) if tc < C - 1 else S['mlp_ready'].when(f'down_{FFN - 1}')))
                        dve.wait_ge(*pool_done.when('biased', 'mlp', tc))
                        nc.vector.tensor_tensor(x[:, tc, :], ps[:, tc, :], x[:, tc, :], ALU.add)\
                            .then_inc(*dve_done.reach('x', 1, tc))
                        dve.wait_ge(*dve_done.when('x', 1, tc))

                    dve_norm(dve, 'a2', xn2, add_mlp)
                    dve_rwkv(dve, 2)
                    dve_rwkv(dve, 3)

                @block.gpsimd
                def _(pool):
                    nc.gpsimd.memset(v0[:, :, :, :], 0.0).then_inc(*pool_done.reach('v0', 'clear'))
                    pool_attention(pool, A0)
                    pool.wait_ge(sems['x_in'], 16)
                    pool.wait_ge(sems['rows_in'], 16)
                    pool_bias(pool, 0, A0.rowbo, lambda e, tc: None)
                    pool_norm(pool, 'ln0', 1e-6, (0, 1))
                    for tc in range(C):
                        pool.wait_ge(*dve_done.when('gamma', tc))
                        nc.gpsimd.tensor_tensor(x[:, tc, :], xn[:, tc, :], rows[:, 3, :], ALU.add)\
                            .then_inc(*pool_done.reach('x0', tc))
                        if tc + 2 < C:
                            pool_norm(pool, 'ln0', 1e-6, (tc + 2,))
                    pool_norm(pool, 'ln1', 1e-5)
                    pool_neg(pool, A1)
                    pool.wait_ge(sems['rows_in'], 32)
                    pool_bias(pool, 1, A1.rowbo, lambda e, tc: e.wait_ge(*dve_done.when('xn', 'ln1', tc)))
                    pool_attention(pool, A1)
                    pool_norm(pool, 'ln2', 1e-5)
                    pool_split(pool, A2, 'k', 0)
                    pool_split(pool, A2, 'k', 1)
                    pool_neg(pool, A2)
                    pool_bias(pool, 2, A2.rowbo, lambda e, tc: e.wait_ge(*dve_done.when('xn', 'ln2', tc)))
                    pool_attention(pool, A2)
                    pool_w(pool, 'up_0')
                    pool_norm(pool, 'ln3', 1e-5)
                    pool.wait_ge(sems['rows_in'], 48)
                    pool_w(pool, 'up_1')
                    pool_bias(pool, 'mlp', 0, lambda e, tc: e.wait_ge(*dve_done.when('xn', 'ln3', tc)))
                    for name in MLP_ORDER[2:]:
                        pool_w(pool, name)
                    for l in (2, 3):
                        pool_rwkv(pool, l)

                @block.sync
                def _(sp):
                    def load(dst, src, name):
                        sp.dma_start(dst, src).then_inc(sems[name], 16)

                    load(rows[:, 0:4, :], a['rows0'].unsqueeze(0).to_broadcast([P, 4, H]), 'rows_in')
                    sp.wait_ge(sems['x_stored'], 16)
                    sp.sem_clear(sems['x_stored'])
                    load(x[:, :, :], a['x'][b].rearrange('(c p) t -> p c t', p=P), 'x_in')
                    for g in range(A0.groups):
                        sp_stack(sp, A0, g, 'kq')
                        if g == 1:
                            load_weights(sp, 'k1', freed)
                    sp.wait_ge(*pool_done.when('x0', C - 1))
                    load(rows[:, :, :], a['rows1'][0:NROWS].unsqueeze(0).to_broadcast([P, NROWS, H]), 'rows_in')
                    load(maskA[:, :, :], a['mask2'][b].rearrange('(c p) t -> p c t', p=P), 'mask2_in')
                    load_weights(sp, 'v1', freed)
                    sp_stack(sp, A1, 0)
                    sp_stack(sp, A1, 1)
                    sp_stack(sp, A1, 2)
                    load_weights(sp, 'o1', freed)
                    sp_stack(sp, A1, 3)
                    load_weights(sp, 'k2', freed)
                    load_weights(sp, 'v2', freed)
                    load(rows[:, 0, :], a['rows1'][NROWS:].to_broadcast([P, H]), 'rows_in')
                    load_weights(sp, 'q2', freed)
                    sp_stack(sp, A2, 0, 'k')
                    sp_stack(sp, A2, 1, 'k')
                    sp_stack(sp, A2, 0, 'q')
                    sp_stack(sp, A2, 1, 'q')
                    sp_stack(sp, A2, 2)
                    load_weights(sp, 'o2', freed)
                    sp_stack(sp, A2, 3)
                    load_weights(sp, 'down_3', freed)
                    sp.wait_ge(*dve_done.when('x', 1, C - 1))
                    load(s0[:, :, :], a['ctx'][b, 2:2 + HS, :].rearrange('(c r) (q j) -> (r q) c j', c=C, j=HS), 's0_in')
                    load(mixers[:, :], a['mixers'][0], 'mixers_in')
                    load(fold[:, :], a['fold'], 'fold_in')
                    load_weights(sp, 'small_3', freed)
                    sp.wait_ge(*dve_done.when('x', 2, C - 1))
                    load(mixers[:, :], a['mixers'][1], 'mixers_in')
                    load_weights(sp, 'fv_3', freed)
                    sp.wait_ge(*pool_done.when('prev', 'f3'))
                    ahead(sp, 'ctx_in', b + 1)
                    ahead(sp, 'mask0_in', b + 1)
                    sp.wait_ge(*dve_done.when('xr2', 3, C - 1))
                    ahead(sp, 'xT_in', b + 1)
                    for n in (1, 2, 0):
                        sp.wait_ge(*freed(BLOCKS[len(BLOCKS) - WSLOTS + (n - len(BLOCKS)) % WSLOTS]))
                        ahead(sp, f'w{n}', b + 1)
                    fin = dve_done.when('x', 3, C - 1)
                    sp.wait_ge(*fin)
                    sp.dma_start(a['out'][b].rearrange('(c p) t -> p c t', p=P), x[:, :, :]).then_inc(sems['x_stored'], 16)

        with nc.Block() as block:
            @block.sync
            def _(sp):
                for name in AHEAD + ['x_stored']:
                    sp.wait_ge(sems[name], 16)

    out = {n: s.marks for n, s in sig.items()}
    out['ring'] = {label: n for n, label in enumerate(ring.labels)}
    return out


def _block(w):
    import numpy as np
    n = w.shape[1]
    out = np.zeros((P, C * H), np.float32)
    out[:, :C * n] = w.reshape(C, P, n).transpose(1, 0, 2).reshape(P, C * n)
    return out


def _arrays(v):
    import numpy as np
    x, ctx = v['x'], v['ctx_2048']
    more = lambda w: np.concatenate([w, w[-1:]])
    d = {'x': x, 'xT': more(x.transpose(0, 2, 1)), 'ctx': ctx, 'ctxT': more(ctx.transpose(0, 2, 1)),
         'mask0': more(v['mask_Bx1xSxS2_ff0'].reshape(B, L, L)), 'mask1': v['mask_1x1xSxS2_fc1'].reshape(L, L),
         'mask2': v['mask_Bx1xSxS2_ff1'].reshape(B, L, L)}
    g = lambda n: v['L0_xattn_' + n]
    blk = {'kv0': _block(np.concatenate([g('Wk'), g('Wv'), np.zeros((H, 256), np.float32)], 1)),
           'q0': _block(g('Wq')),
           'o0': _block(g('Wo').reshape(4, 2, 4, 16, H).transpose(0, 2, 1, 3, 4).reshape(H, H))}
    vec = {'bq0': g('bq'), 'bk0': np.pad(g('bk'), (0, 384))}
    r0 = [np.pad(g('bv'), (0, 384)), g('bo'), g('gamma'), g('beta')]
    g = lambda n: v['L1_xattn_' + n]
    q, k, w = np.split(g('w_qkv'), 3, 1)
    k2, w2 = np.split(g('w_kv'), 2, 1)
    blk |= {'q1': _block(q), 'k1': _block(k), 'v1': _block(w), 'o1': _block(g('w_ao')), 'q2': _block(g('w_q')),
            'k2': _block(k2), 'v2': _block(w2), 'o2': _block(g('w_co'))}
    b, b2 = g('b_qkv'), g('b_kv')
    vec |= {'ln1_s': g('ln1_s'), 'ln1_b': g('ln1_b'), 'bq1': b[:H], 'bk1': b[H:2 * H], 'ln2_s': g('ln2_s'),
            'ln2_b': g('ln2_b'), 'bq2': g('b_q'), 'bk2': b2[:H], 'ln3_s': g('ln3_s'), 'ln3_b': g('ln3_b')}
    r1 = [b[2 * H:], g('b_ao'), b2[H:], g('b_co'), g('b2')]
    for i in range(FFN):
        s = slice(i * H, (i + 1) * H)
        blk |= {f'up_{i}': _block(g('w1')[:, s]), f'down_{i}': _block(g('w2')[s])}
        vec[f'b1_{i}'] = g('b1')[s]
    mixers = []
    for l in (2, 3):
        g = lambda n: v[f'L{l}_xattn_' + n]
        td, u = ('td', 'u') if l == 2 else ('decay', 'faaaa')
        wf = {c: g(f'Wf{c}') if l == 2 else g(f'ffn_W{c}') for c in 'krv'}
        small = _block(g('maa_w1'))
        small[:, SMALL_TD1:SMALL_TD2] = _block(g(f'{td}_w1'))[:, :SMALL_TD2 - SMALL_TD1]
        small[:64, SMALL_TD2:SMALL_TD2 + H] = g(f'{td}_w2')
        blk[f'small_{l}'] = small
        mixers.append(np.tile(g('maa_w2').transpose(1, 0, 2).reshape(32, 5 * H), (3, 1)))
        for n, w in (('k', g('Wk')), ('r', g('Wr')), ('v', g('Wv').reshape(C, HEADS, HS, H).transpose(0, 2, 1, 3).reshape(H, H)), ('g', g('Wg')), ('o', g('Wo')),
                     ('fk', wf['k']), ('fr', wf['r']), ('fv', wf['v'])):
            blk[f'{n}_{l}'] = _block(w.T)
        ms = g('maa_stack').reshape(5, H)
        vec |= {f'{n}_{l}': g(n) for n in ('ln1_w', 'ln1_b', 'ln2_w', 'ln2_b', 'maa_x', 'gn_w', 'gn_b')}
        vec |= {f'maa_{n}_{l}': ms[i] for i, n in enumerate('kwvrg')}
        vec |= {f'decay_{l}': g('time_decay'), f'u_{l}': g(u).reshape(H), f'ffn_k_{l}': g('ffn_maa_k'),
                f'ffn_r_{l}': g('ffn_maa_r')}
    d['mixers'] = np.stack(mixers)
    d['blocks'] = np.stack([blk[n] for n in BLOCKS])
    d['cols'] = np.stack([vec[n] for n in VECTORS]).reshape(len(VECTORS), C, P).transpose(2, 0, 1).reshape(P, -1)
    d['rows0'], d['rows1'] = np.stack(r0), np.stack(r1)
    d['ident'] = np.eye(P, dtype=np.float32)
    by_feature = np.arange(P).reshape(HS, HEADS).T.reshape(P)
    natural = np.argsort(by_feature)
    one_head = np.kron(np.eye(HEADS), np.ones((HS, HS)))
    d['head_sum'] = np.zeros((P, P))
    d['head_sum'][:, by_feature] = one_head
    d['fold'] = np.concatenate([np.eye(P // 2)] * 2)
    perm, gather = np.zeros((P, P), np.float32), np.zeros((P, 4, 32), np.float32)
    for h in range(HEADS):
        for j in range(HS):
            m, jj = divmod(j, 4)
            perm[h * HS + j, 32 * jj + 4 * h + m] = 1
        for m in range(4):
            gather[h * HS:(h + 1) * HS, m, 4 * h + m] = 1
    d['permute'], d['gather'] = perm[natural], gather
    d['centre'] = perm.T @ (np.eye(P) - one_head / HS)
    return {n: np.ascontiguousarray(w, dtype=np.float32) for n, w in d.items()}


def kernel(**inputs):
    import numpy as np
    import concourse.bacc as bacc
    from concourse.bass_utils import run_bass_kernel_spmd
    arrays = _arrays({n: np.asarray(w) for n, w in inputs.items()})
    known = None
    for _ in range(2):
        nc = bacc.Bacc("TRN2", target_bir_lowering=False, num_devices=1)
        a = {n: nc.dram_tensor(f"in_{n}_dram", w.shape, F32, kind="ExternalInput").ap() for n, w in arrays.items()}
        a['out'] = nc.dram_tensor("out_dram", (B, L, H), F32, kind="ExternalOutput").ap()
        known = build(nc, a, known)
    r = run_bass_kernel_spmd(nc, [{f"in_{n}_dram": w for n, w in arrays.items()}], core_ids=[0])
    return r.results[0]["out_dram"]
```
